# Optimizing a Trainium2 kernel written in Bass

```python
import numpy as np
import jax
import jax.numpy as jnp

def _softmax(x, axis=-1):
    return jax.nn.softmax(x, axis=axis)

def _gelu(x):
    return jax.nn.gelu(x, approximate=True)

def _silu(x):
    return jax.nn.silu(x)

def _sigmoid(x):
    return jax.nn.sigmoid(x)

def _layernorm(x, axis=-1, eps=1e-05):
    m = jnp.mean(x, axis=axis, keepdims=True)
    v = jnp.var(x, axis=axis, keepdims=True)
    return (x - m) / jnp.sqrt(v + eps)

def _scatter_add(tgt, idx, src, axis=0):
    return tgt.at[idx].add(src)

def _segment_sum(src, seg, n):
    return jax.ops.segment_sum(src, seg, n)
kernel_name = 'mk_xattn_ffn_d2_seqx_r8_412dff'

def setup_inputs(seed: int=0):
    np.random.seed(seed)
    _w = jnp.asarray

    def _rec_inputs():
        import jax
        import jax.numpy as jnp
        _rk = jax.random.key(seed)
        x = 7.22e-05 + 1 * jax.random.normal(jax.random.fold_in(_rk, 1), (16, 128, 128), jnp.float32)
        _lenS = 128 - jax.random.randint(jax.random.fold_in(_rk, 7), (16,), 0, max(1, 128 // 4) + 1, jnp.int32)
        _lenS2 = 77 - jax.random.randint(jax.random.fold_in(_rk, 8), (16,), 0, max(1, 77 // 4) + 1, jnp.int32)
        _ctx_1024P = jax.random.normal(jax.random.fold_in(_rk, 11), (16, 16, 128), jnp.float32)
        _ctx_1024c = jax.random.dirichlet(jax.random.fold_in(_rk, 511), 0.3 * jnp.ones((16,), jnp.float32), (16, 77))
        _ctx_1024t = jnp.einsum('bsk,bkd->bsd', _ctx_1024c, _ctx_1024P)
        _ctx_1024t = _ctx_1024t * jax.lax.rsqrt(jnp.mean(jnp.square(_ctx_1024t)) + 1e-12) * 0.953939
        ctx_1024 = 4.13588e-05 + 0.999923 * (_ctx_1024t + 0.3 * jax.random.normal(jax.random.fold_in(_rk, 611), (16, 77, 128), jnp.float32))
        _validS = jnp.arange(128)[None, :] < _lenS[:, None]
        _validS2 = jnp.arange(77)[None, :] < _lenS2[:, None]
        _causal = jnp.tril(jnp.ones((128, 128), dtype=bool))
        mask_Bx1x1xS2_ik0 = jnp.where(jnp.broadcast_to(_validS2[:, None, None, :], (16, 1, 1, 77)), 0, 1).astype(jnp.int32)
        return (x, ctx_1024, mask_Bx1x1xS2_ik0)
    x, ctx_1024, mask_Bx1x1xS2_ik0 = _rec_inputs()

    def _L0_xattn_setup():
        import jax, jax.numpy as jnp
        import numpy as np
        EMBED_DIM = 128
        NUM_HEADS = 16
        HEAD_DIM = EMBED_DIM // NUM_HEADS
        NEG = -1000000000.0

        def _split_heads(x):
            B, S, D = x.shape
            return x.reshape(B, S, NUM_HEADS, HEAD_DIM).transpose(0, 2, 1, 3)
        key = jax.random.key(seed)
        ks = jax.random.split(key, 13)
        B, S, D = (4, 256, EMBED_DIM)
        scale = 1.0 / np.sqrt(D)
        inp = {'query': jax.random.normal(ks[0], (B, S, D), jnp.float32), 'key': jax.random.normal(ks[1], (B, S, D), jnp.float32), 'value': jax.random.normal(ks[2], (B, S, D), jnp.float32), 'mask': jax.random.randint(ks[3], (B, 1, 1, S), 0, 2, jnp.int32), 'Wq': jax.random.normal(ks[4], (D, D), jnp.float32) * scale, 'bq': jnp.zeros((D,), jnp.float32), 'Wk': jax.random.normal(ks[5], (D, D), jnp.float32) * scale, 'bk': jnp.zeros((D,), jnp.float32), 'Wv': jax.random.normal(ks[6], (D, D), jnp.float32) * scale, 'bv': jnp.zeros((D,), jnp.float32), 'Wo': jax.random.normal(ks[7], (D, D), jnp.float32) * scale, 'bo': jnp.zeros((D,), jnp.float32)}
        return inp
    _L0_xattn_all = _L0_xattn_setup()
    _L0_xattn_in = {k: v for k, v in _L0_xattn_all.items() if k in ('Wq', 'bq', 'Wk', 'bk', 'Wv', 'bv', 'Wo', 'bo')}
    del _L0_xattn_all

    def _L0_ffn_setup():
        import jax, jax.numpy as jnp
        import numpy as np
        E, D, F = (8, 128, 512)
        B, S = (4, 256)

        def _layernorm(x, g, b, eps=1e-05):
            mu = jnp.mean(x, axis=-1, keepdims=True)
            var = jnp.var(x, axis=-1, keepdims=True)
            return (x - mu) * jax.lax.rsqrt(var + eps) * g + b
        key = jax.random.key(seed)
        ks = jax.random.split(key, 5)
        return {'input_features': jax.random.normal(ks[0], (B, S, D), jnp.float32), 'centroids': jax.random.normal(ks[1], (E, D), jnp.float32) * 0.1, 'ln_g': jnp.ones((E, D), jnp.float32), 'ln_b': jnp.zeros((E, D), jnp.float32), 'w1': jax.random.normal(ks[2], (E, F, D), jnp.float32) * (1.0 / np.sqrt(D).astype(np.float32)), 'b1': jnp.zeros((E, F), jnp.float32), 'w2': jax.random.normal(ks[3], (E, D, F), jnp.float32) * (1.0 / np.sqrt(F).astype(np.float32)), 'b2': jnp.zeros((E, D), jnp.float32)}
    _L0_ffn_all = _L0_ffn_setup()
    _L0_ffn_in = {k: v for k, v in _L0_ffn_all.items() if k in ('centroids', 'ln_g', 'ln_b', 'w1', 'b1', 'w2', 'b2')}
    del _L0_ffn_all

    def _L1_xattn_setup():
        import jax, jax.numpy as jnp
        import numpy as np
        D = 128
        NUM_ITERS = 3
        EPS = 1e-06
        SCALE = D ** (-0.5)

        def rmsnorm(x, w, eps=EPS):
            return x * jax.lax.rsqrt(jnp.mean(x * x, axis=-1, keepdims=True) + eps) * w

        def gru_cell(x, h, wih, whh, bih, bhh):
            gx = x @ wih.T + bih
            gh = h @ whh.T + bhh
            xr, xz, xn = jnp.split(gx, 3, axis=-1)
            hr, hz, hn = jnp.split(gh, 3, axis=-1)
            r = jax.nn.sigmoid(xr + hr)
            z = jax.nn.sigmoid(xz + hz)
            n = jnp.tanh(xn + r * hn)
            return (1.0 - z) * n + z * h
        key = jax.random.key(seed)
        ks = jax.random.split(key, 8)
        B, K, M, d = (8, 64, 512, D)
        w_std = d ** (-0.5)
        return {'slots': jax.random.normal(ks[0], (B, K, d), jnp.float32), 'P': jax.random.normal(ks[1], (B, M, d), jnp.float32), 'Wq': jax.random.normal(ks[2], (d, d), jnp.float32) * w_std, 'Wk': jax.random.normal(ks[3], (d, d), jnp.float32) * w_std, 'Wv': jax.random.normal(ks[4], (d, d), jnp.float32) * w_std, 'gru_wih': jax.random.normal(ks[5], (3 * d, d), jnp.float32) * w_std, 'gru_whh': jax.random.normal(ks[6], (3 * d, d), jnp.float32) * w_std, 'gru_bih': jnp.zeros((3 * d,), jnp.float32), 'gru_bhh': jnp.zeros((3 * d,), jnp.float32), 'slot_norm_w': jnp.ones((d,), jnp.float32), 'input_norm_w': jnp.ones((d,), jnp.float32)}
    _L1_xattn_all = _L1_xattn_setup()
    _L1_xattn_in = {k: v for k, v in _L1_xattn_all.items() if k in ('Wq', 'Wk', 'Wv', 'gru_wih', 'gru_whh', 'gru_bih', 'gru_bhh', 'slot_norm_w', 'input_norm_w')}
    del _L1_xattn_all

    def _L1_ffn_setup():
        import jax, jax.numpy as jnp
        import numpy as np
        D_MODEL = 128
        D_HIDDEN = 512
        NUM_EXPERTS = 8
        B, T = (2, 256)
        key = jax.random.key(seed)
        ks = jax.random.split(key, 8)
        s = 0.02
        x = jax.random.normal(ks[0], (B, T, D_MODEL), dtype=jnp.float32)
        Wg = jax.random.normal(ks[1], (D_MODEL, NUM_EXPERTS), dtype=jnp.float32) * s
        bg = jnp.zeros((NUM_EXPERTS,), dtype=jnp.float32)
        W1 = jax.random.normal(ks[2], (NUM_EXPERTS, D_MODEL, D_HIDDEN), dtype=jnp.float32) * s
        b1 = jnp.zeros((NUM_EXPERTS, D_HIDDEN), dtype=jnp.float32)
        W2 = jax.random.normal(ks[3], (NUM_EXPERTS, D_HIDDEN, D_MODEL), dtype=jnp.float32) * s
        b2 = jnp.zeros((NUM_EXPERTS, D_MODEL), dtype=jnp.float32)
        return {'x': x, 'Wg': Wg, 'bg': bg, 'W1': W1, 'b1': b1, 'W2': W2, 'b2': b2}
    _L1_ffn_all = _L1_ffn_setup()
    _L1_ffn_in = {k: v for k, v in _L1_ffn_all.items() if k in ('Wg', 'bg', 'W1', 'b1', 'W2', 'b2')}
    del _L1_ffn_all
    return {'x': x, 'ctx_1024': ctx_1024, 'mask_Bx1x1xS2_ik0': mask_Bx1x1xS2_ik0, 'L0_xattn_Wq': _L0_xattn_in['Wq'], 'L0_xattn_bq': _L0_xattn_in['bq'], 'L0_xattn_Wk': _L0_xattn_in['Wk'], 'L0_xattn_bk': _L0_xattn_in['bk'], 'L0_xattn_Wv': _L0_xattn_in['Wv'], 'L0_xattn_bv': _L0_xattn_in['bv'], 'L0_xattn_Wo': _L0_xattn_in['Wo'], 'L0_xattn_bo': _L0_xattn_in['bo'], 'L0_ffn_centroids': _L0_ffn_in['centroids'], 'L0_ffn_ln_g': _L0_ffn_in['ln_g'], 'L0_ffn_ln_b': _L0_ffn_in['ln_b'], 'L0_ffn_w1': _L0_ffn_in['w1'], 'L0_ffn_b1': _L0_ffn_in['b1'], 'L0_ffn_w2': _L0_ffn_in['w2'], 'L0_ffn_b2': _L0_ffn_in['b2'], 'L1_xattn_Wq': _L1_xattn_in['Wq'], 'L1_xattn_Wk': _L1_xattn_in['Wk'], 'L1_xattn_Wv': _L1_xattn_in['Wv'], 'L1_xattn_gru_wih': _L1_xattn_in['gru_wih'], 'L1_xattn_gru_whh': _L1_xattn_in['gru_whh'], 'L1_xattn_gru_bih': _L1_xattn_in['gru_bih'], 'L1_xattn_gru_bhh': _L1_xattn_in['gru_bhh'], 'L1_xattn_slot_norm_w': _L1_xattn_in['slot_norm_w'], 'L1_xattn_input_norm_w': _L1_xattn_in['input_norm_w'], 'L1_ffn_Wg': _L1_ffn_in['Wg'], 'L1_ffn_bg': _L1_ffn_in['bg'], 'L1_ffn_W1': _L1_ffn_in['W1'], 'L1_ffn_b1': _L1_ffn_in['b1'], 'L1_ffn_W2': _L1_ffn_in['W2'], 'L1_ffn_b2': _L1_ffn_in['b2']}

def reference(x, ctx_1024, mask_Bx1x1xS2_ik0, L0_xattn_Wq, L0_xattn_bq, L0_xattn_Wk, L0_xattn_bk, L0_xattn_Wv, L0_xattn_bv, L0_xattn_Wo, L0_xattn_bo, L0_ffn_centroids, L0_ffn_ln_g, L0_ffn_ln_b, L0_ffn_w1, L0_ffn_b1, L0_ffn_w2, L0_ffn_b2, L1_xattn_Wq, L1_xattn_Wk, L1_xattn_Wv, L1_xattn_gru_wih, L1_xattn_gru_whh, L1_xattn_gru_bih, L1_xattn_gru_bhh, L1_xattn_slot_norm_w, L1_xattn_input_norm_w, L1_ffn_Wg, L1_ffn_bg, L1_ffn_W1, L1_ffn_b1, L1_ffn_W2, L1_ffn_b2):
    import jax
    import jax.numpy as jnp

    def _L0_xattn_ref(query, key, value, mask, Wq, bq, Wk, bk, Wv, bv, Wo, bo):
        import jax, jax.numpy as jnp
        import numpy as np
        EMBED_DIM = 128
        NUM_HEADS = 16
        HEAD_DIM = EMBED_DIM // NUM_HEADS
        NEG = -1000000000.0

        def _split_heads(x):
            B, S, D = x.shape
            return x.reshape(B, S, NUM_HEADS, HEAD_DIM).transpose(0, 2, 1, 3)
        B, S, D = query.shape
        Q = _split_heads(query @ Wq + bq)
        K = _split_heads(key @ Wk + bk)
        V = _split_heads(value @ Wv + bv)
        scores = jnp.einsum('bhqd,bhkd->bhqk', Q, K) / jnp.sqrt(jnp.float32(HEAD_DIM))
        scores = jnp.where(mask == 0, jnp.float32(NEG), scores)
        attn = jax.nn.softmax(scores, axis=-1)
        out = jnp.einsum('bhqk,bhkd->bhqd', attn, V)
        out = out.transpose(0, 2, 1, 3).reshape(B, S, D)
        return out @ Wo + bo

    def _L0_ffn_ref(input_features, centroids, ln_g, ln_b, w1, b1, w2, b2):
        import jax, jax.numpy as jnp
        import numpy as np
        E, D, F = (8, 128, 512)
        B, S = (4, 256)

        def _layernorm(x, g, b, eps=1e-05):
            mu = jnp.mean(x, axis=-1, keepdims=True)
            var = jnp.var(x, axis=-1, keepdims=True)
            return (x - mu) * jax.lax.rsqrt(var + eps) * g + b
        Bf, Sf, Df = input_features.shape
        x = input_features.reshape(-1, Df)
        aff = x @ centroids.T
        assign = jnp.argmax(aff, axis=1)
        order = jnp.argsort(assign)
        xs = x[order]
        es = assign[order]
        alpha = jax.nn.sigmoid(jnp.take_along_axis(aff[order], es[:, None], axis=1))
        nE = centroids.shape[0]
        y = jnp.zeros_like(xs)
        for e in range(nE):
            h = _layernorm(xs, ln_g[e], ln_b[e])
            h = jax.nn.relu(h @ w1[e].T + b1[e])
            ye = xs + h @ w2[e].T + b2[e]
            y = y + jnp.where((es == e)[:, None], ye, 0.0)
        out_sorted = alpha * y + (1.0 - alpha) * xs
        inv = jnp.argsort(order)
        return out_sorted[inv].reshape(Bf, Sf, Df)

    def _L1_xattn_ref(slots, P, Wq, Wk, Wv, gru_wih, gru_whh, gru_bih, gru_bhh, slot_norm_w, input_norm_w):
        import jax, jax.numpy as jnp
        import numpy as np
        D = 128
        NUM_ITERS = 3
        EPS = 1e-06
        SCALE = D ** (-0.5)

        def rmsnorm(x, w, eps=EPS):
            return x * jax.lax.rsqrt(jnp.mean(x * x, axis=-1, keepdims=True) + eps) * w

        def gru_cell(x, h, wih, whh, bih, bhh):
            gx = x @ wih.T + bih
            gh = h @ whh.T + bhh
            xr, xz, xn = jnp.split(gx, 3, axis=-1)
            hr, hz, hn = jnp.split(gh, 3, axis=-1)
            r = jax.nn.sigmoid(xr + hr)
            z = jax.nn.sigmoid(xz + hz)
            n = jnp.tanh(xn + r * hn)
            return (1.0 - z) * n + z * h
        Pn = rmsnorm(P, input_norm_w)
        k_proj = Pn @ Wk.T
        v_proj = Pn @ Wv.T
        for _ in range(NUM_ITERS):
            sn = rmsnorm(slots, slot_norm_w)
            q_proj = sn @ Wq.T
            scores = jnp.einsum('bkd,bmd->bkm', q_proj, k_proj) * SCALE
            attn = jax.nn.softmax(scores, axis=-2)
            attn = attn / (jnp.sum(attn, axis=-1, keepdims=True) + EPS)
            updates = jnp.einsum('bkm,bmd->bkd', attn, v_proj)
            slots = gru_cell(updates, slots, gru_wih, gru_whh, gru_bih, gru_bhh)
        return slots

    def _L1_ffn_ref(x, Wg, bg, W1, b1, W2, b2):
        import jax, jax.numpy as jnp
        import numpy as np
        D_MODEL = 128
        D_HIDDEN = 512
        NUM_EXPERTS = 8
        B, T = (2, 256)
        gate_logits = jnp.einsum('btd,de->bte', x, Wg) + bg
        gate_scores = jax.nn.softmax(gate_logits, axis=-1)
        top1_idx = jnp.argmax(gate_scores, axis=-1)
        top1_mask = jax.nn.one_hot(top1_idx, NUM_EXPERTS, dtype=x.dtype)
        top1_weight = jnp.sum(gate_scores * top1_mask, axis=-1, keepdims=True)
        h = jax.nn.silu(jnp.einsum('btd,edh->bteh', x, W1) + b1)
        o = jnp.einsum('bteh,ehd->bted', h, W2) + b2
        y = jnp.sum(o * top1_mask[..., None], axis=2) * top1_weight
        return y
    x = x + _L0_xattn_ref(_layernorm(x, axis=-1), ctx_1024, ctx_1024, mask_Bx1x1xS2_ik0, L0_xattn_Wq, L0_xattn_bq, L0_xattn_Wk, L0_xattn_bk, L0_xattn_Wv, L0_xattn_bv, L0_xattn_Wo, L0_xattn_bo)
    x = x + _L0_ffn_ref(_layernorm(x, axis=-1), L0_ffn_centroids, L0_ffn_ln_g, L0_ffn_ln_b, L0_ffn_w1, L0_ffn_b1, L0_ffn_w2, L0_ffn_b2)
    x = x + _L1_xattn_ref(_layernorm(x, axis=-1), ctx_1024, L1_xattn_Wq, L1_xattn_Wk, L1_xattn_Wv, L1_xattn_gru_wih, L1_xattn_gru_whh, L1_xattn_gru_bih, L1_xattn_gru_bhh, L1_xattn_slot_norm_w, L1_xattn_input_norm_w)
    x = x + _L1_ffn_ref(_layernorm(x, axis=-1), L1_ffn_Wg, L1_ffn_bg, L1_ffn_W1, L1_ffn_b1, L1_ffn_W2, L1_ffn_b2)
    return x

_drawn_inputs = setup_inputs


def setup_inputs(seed=0):
    import zlib

    import numpy as np

    out = dict(_drawn_inputs(seed))
    spreads = {'L0_xattn_bq': (0.0, 0.1),
     'L0_xattn_bk': (0.0, 0.8),
     'L0_xattn_bv': (0.0, 0.1),
     'L0_xattn_bo': (0.0, 0.1),
     'L0_ffn_ln_g': (1.0, 0.2),
     'L0_ffn_ln_b': (0.0, 0.3),
     'L0_ffn_b1': (0.0, 0.309),
     'L0_ffn_b2': (0.0, 0.1),
     'L1_xattn_gru_bih': (0.0, 0.284),
     'L1_xattn_gru_bhh': (0.0, 0.466),
     'L1_xattn_slot_norm_w': (1.0, 0.6),
     'L1_xattn_input_norm_w': (1.0, 0.2),
     'L1_ffn_bg': (0.0, 0.8),
     'L1_ffn_b1': (0.0, 0.8),
     'L1_ffn_b2': (0.0, 0.8)}
    factors = {'L1_ffn_Wg': 7.345, 'L1_ffn_W1': 8.0, 'L1_ffn_W2': 8.0}
    for name, (base, spread) in spreads.items():
        noise = np.random.default_rng([zlib.crc32(name.encode()), seed]).standard_normal(out[name].shape)
        drawn = base * np.exp(spread * noise) if base else spread * noise
        out[name] = jnp.asarray(drawn.astype(out[name].dtype))
    for name, factor in factors.items():
        out[name] = (out[name] * factor).astype(out[name].dtype)
    return out
```

```python
from contextlib import ExitStack

import numpy as np

import concourse.bass as bass
from concourse import mybir

F32 = mybir.dt.float32
BF16 = mybir.dt.bfloat16
I32 = mybir.dt.int32
ALU = mybir.AluOpType
ACT = mybir.ActivationFunctionType
X = mybir.AxisListType.X

P = 128
B, S, D = 16, 128, 128
M = 77
H, HD = 16, 8
HV = HD + 1
E, F = 8, 512
FC = F // P
TILES = B * S // P + E - 1
HEAD_GROUPS = ((0, 6), (6, 5), (11, 5))
LN_EPS, RMS_EPS, ATT_EPS = 1e-5, 1e-6, 1e-6
NEG = -1e9
GATES = 3 * D

C_IDENT, C_HEAD, C_TIE, C_JOTA = 0, 128, 144, 272
C_RESET = C_JOTA + TILES * E
C_UPPER = C_RESET + E * B
C_ALL = C_UPPER + P
V_BQ, V_BK, V_WIN, V_WSLOT, V_BIH, V_BHH = 0, 1, 2, 3, 4, 7
V_ALL = 10
W_2 = F
W_B1 = 2 * F
W_G = W_B1 + FC
W_B = W_G + 1
W_ALL = W_B + 1
GROUP = 4
G = GROUP * S
NG = B // GROUP
ITERS = 3
ROUTE_LINKS = 20
SLOT_STEPS = ITERS * NG
R_BV, R_BO, R_BG = 0, 128, 256
R_ALL = 264


def need(eng, sem, count):
    if not (isinstance(count, int) and count <= 0):
        eng.wait_ge(sem, count)


def skewed(eng, first, main, last, step):
    lo, hi = main
    for t in range(first, lo):
        step(t, t % 2)
    with eng.Fori(0, (hi - lo) // 2) as i:
        for k in range(2):
            step(i * 2 + (lo + k), (lo + k) % 2)
    for t in range(hi, last + 1):
        step(t, t % 2)


def skewed_groups(eng, first, main, last, step):
    lo, hi = main
    for s in range(first, lo):
        step(s, s % NG)
    with eng.Fori(0, (hi - lo) // NG) as i:
        for k in range(NG):
            step(i * NG + (lo + k), (lo + k) % NG)
    for s in range(hi, last + 1):
        step(s, s % NG)


def build(nc, a, out):
    with ExitStack() as ctx:
        def sb(name, shape, dt=F32):
            return ctx.enter_context(nc.sbuf_tensor(name, shape, dt))

        first = ExitStack()

        def sb1(name, shape, dt=F32):
            return first.enter_context(nc.sbuf_tensor(name, shape, dt))

        def sem(name):
            return ctx.enter_context(nc.semaphore(name))

        bank = [ctx.enter_context(nc.psum_tensor(f"bank{i}", [P, 512], F32)) for i in range(8)]

        consts = sb("consts", [P, C_ALL])
        vecs = sb("vecs", [P, V_ALL])
        rows = sb("rows", [P, R_ALL])
        w0 = sb("w0", [P, 4, D])
        w1 = sb("w1", [P, 3, D])
        gru = sb("gru", [P, 2, GATES])
        gates = sb("gates", [P, 2, E])
        x_all = sb("x_all", [P, B, D])
        negp = sb("negp", [3, 1])
        ones3 = sb("ones3", [3, P], BF16)
        v_all = sb("v_all", [M, B, H * HV])
        ab = sb("ab", [P, D + GATES])
        vw_all = sb("vw_all", [M, B, GATES])
        kq_all = sb("kq_all", [P, B, M])
        ctx_ms = sb("ctx_ms", [M, B])
        ctx_ln = sb("ctx_ln", [M, B])
        ctx_r = sb("ctx_r", [M, B])
        wslot = sb("wslot", [P, 1])
        bq = sb("bq", [P, 1])
        eps_ln = sb("eps_ln", [P, 1])
        hold = sb("hold", [1, 1])
        eps_rms = sb("eps_rms", [P, 1])
        ident = consts[:, C_IDENT:C_IDENT + P]
        headmask = consts[:, C_HEAD:C_HEAD + H]

        def pair(name, shape, dt=F32):
            return [sb(f"{name}{i}", shape, dt) for i in range(2)]

        xh_all = sb("xh_all", [P, B, D])
        res_all = sb("res_all", [P, B, D])
        aff_all = sb("aff_all", [P, B, E])

        upper = sb("upper", [P, P], BF16)
        ones_b = sb("ones_b", [P, P], BF16)
        ones_e = sb("ones_e", [P, E])
        amax = sb("amax", [P, B])
        apick = sb("apick", [P, B, E])
        onehot = sb("onehot", [P, B, E], BF16)
        tot = sb("tot", [P, E, B])
        cum = sb("cum", [P, E * B])
        n_pad = sb("n_pad", [P, E], I32)
        n_tile_i = sb("n_tile_i", [P, E], I32)
        n_tile = sb("n_tile", [P, E])
        tile_end = sb("tile_end", [P, E])
        base = sb("base", [P, E])
        pos_be = sb("pos_be", [P, B, E])
        pos_f = sb("pos_f", [P, B])
        pos = sb("pos", [P, B], I32)
        tile_cmp = sb("tile_cmp", [P, TILES, E])
        tile_e = sb("tile_e", [P, TILES])
        tile_tab = sb("tile_tab", [P, TILES], I32)
        share = sb("share", [P, B])
        eg = sb("eg", [P, B, E])
        zero = sb("zero", [P, D])
        one_row = sb("one_row", [1, P])
        att = pair("att", [M + 1, G])
        ones_f = sb("ones_f", [P, P])
        brz = sb("brz", [P, 2])
        bhn = sb("bhn", [P, 1])

        def pair1(name, shape, dt=F32):
            return [sb1(f"{name}{i}", shape, dt) for i in range(2)]
        ctx_all = sb1("ctx_all", [M, B, D])
        ctxT_all = sb1("ctxT_all", [P, B * M])
        mask_i = sb1("mask_i", [P, B * M], I32)
        mask_f = sb1("mask_f", [P, B * M])
        neg3 = sb1("neg3", [3, B * M], BF16)
        kT_all = sb1("kT_all", [P, B * M])
        ctx_sq = sb1("ctx_sq", [M, B, D])
        ctxT = pair1("ctxT", [P, M])
        kq = pair1("kq", [M, D])
        st = pair1("st", [P, 6])
        mv = pair1("mv", [P, 2])
        lnv = pair1("lnv", [P, 1])
        rstd = pair1("rstd", [P, 1])
        xn = pair1("xn", [P, D])
        xnT = pair1("xnT", [P, S])
        qT = pair1("qT", [P, S])
        xbo = pair1("xbo", [P, D])
        kblk = pair1("kblk", [P, H, M])
        smax = pair1("smax", [P, H])
        probs = pair1("probs", [P, H, M])
        pT = pair1("pT", [M, 4, S])
        rden = pair1("rden", [P, H])
        o_sb = pair1("o_sb", [P, D])
        oT = pair1("oT", [P, S])
        x1 = pair1("x1", [P, D])
        st1 = pair1("st1", [P, 6])
        mv1 = pair1("mv1", [P, 2])
        lnv1 = pair1("lnv1", [P, 1])
        rstd1 = pair1("rstd1", [P, 1])
        xin = pair1("xin", [P, D])
        st2 = pair1("st2", [P, 6])
        mv2 = pair1("mv2", [P, 2])
        lnv2 = pair1("lnv2", [P, 1])
        rstd2 = pair1("rstd2", [P, 1])
        xinT = pair1("xinT", [P, S])
        first.close()

        wp = pair("wp", [P, W_ALL])
        b2r = pair("b2r", [1, D])
        xt = pair("xt", [P, D])
        xtT = pair("xtT", [P, P])
        hid = pair("hid", [P, FC, P])
        yt = pair("yt", [P, D])
        f_all = sb("f_all", [P, B, D])
        xs_dram = [nc.dram_tensor(f"xs{l}", (TILES * P, D), F32, kind="Internal").ap() for l in range(2)]
        ys_dram = [nc.dram_tensor(f"ys{l}", (TILES * P, D), F32, kind="Internal").ap() for l in range(2)]

        x2_all = sb("x2_all", [P, B, D])
        gst = sb("gst", [P, GROUP, 6])
        gmv = sb("gmv", [P, GROUP, 2])
        gln = sb("gln", [P, GROUP])
        gr = sb("gr", [P, GROUP])
        gx = pair("gx", [P, GROUP, D])
        hT = sb("hT", [P, B * S])
        sq = pair("sq", [P, G])
        ms = pair("ms", [P, GROUP])
        half = pair("half", [P, GROUP], I32)
        guess = pair("guess", [P, GROUP], I32)
        y2 = pair("y2", [P, GROUP])
        yv = pair("yv", [P, GROUP])
        diag = pair("diag", [P, GROUP, P])
        hs = pair("hs", [P, G])
        cmax = pair("cmax", [M, GROUP])
        ex = pair("ex", [M, GROUP, S])
        csum = pair("csum", [M, GROUP])
        crec = pair("crec", [M, GROUP])
        arec = pair("arec", [M, G])
        attn = pair("attn", [M, G])
        tr = pair("tr", [P, G])
        tz = pair("tz", [P, G])
        hnb = pair("hnb", [P, G])
        u = pair("u", [P, G])
        nn = pair("nn", [P, G])
        dd = pair("dd", [P, G])
        x3T = pair("x3T", [P, G])

        ld_const, ld_rows, ld_x, ld_ctx, ld_w1 = sem("ld_const"), sem("ld_rows"), sem("ld_x"), sem("ld_ctx"), sem("ld_w1")
        ld_ctxT = [sem("ld_ctxT0"), sem("ld_ctxT1")]
        memset_ready = sem("memset_ready")
        mask_ready, neg_ready, kproj, kT_ready, kT_mask = (sem(n) for n in ("mask_ready", "neg_ready", "kproj", "kT_ready", "kT_mask"))
        small_ready, abproj, ab_ready = sem("small_ready"), sem("abproj"), sem("ab_ready")
        ctxsq_ready, ctxms_ready, ctxln_ready, ctxr_ready = (sem(n) for n in ("ctxsq_ready", "ctxms_ready", "ctxln_ready", "ctxr_ready"))
        cproj, v_ready, vw_ready, kq_ready, kqT_done, kqT_ready = (sem(n) for n in ("cproj", "v_ready", "vw_ready", "kq_ready", "kqT_done", "kqT_ready"))
        lnx_st, lnx_mv, lnx_ln, lnx_r, xn_ready = (sem(n) for n in ("lnx_st", "lnx_mv", "lnx_ln", "lnx_r", "xn_ready"))
        xbo_ready, kblk_ready = sem("xbo_ready"), sem("kblk_ready")
        xnT_done, xnT_ready, q_done, q_ready = (sem(n) for n in ("xnT_done", "xnT_ready", "q_done", "q_ready"))
        s_done, max_ready, sub_ready, exp_ready = (sem(n) for n in ("s_done", "max_ready", "sub_ready", "exp_ready"))
        pT_done, pT_ready, pv_done = sem("pT_done"), sem("pT_ready"), sem("pv_done")
        rden_ready, o_ready, oT_done, oT_ready, wo_done = (sem(n) for n in ("rden_ready", "o_ready", "oT_done", "oT_ready", "wo_done"))
        x1_ready, st1_ready, mv1_ready, ln1_ready, r1_ready, xin_ready = (sem(n) for n in ("x1_ready", "st1_ready", "mv1_ready", "ln1_ready", "r1_ready", "xin_ready"))
        st2_ready, mv2_ready, ln2_ready, r2_ready, xh_ready = (sem(n) for n in ("st2_ready", "mv2_ready", "ln2_ready", "r2_ready", "xh_ready"))
        res_ready, xinT_done, xinT_ready, aff_done, aff_ready = (sem(n) for n in ("res_ready", "xinT_done", "xinT_ready", "aff_done", "aff_ready"))
        stored = sem("stored")
        consts2_ready, zeroed = sem("consts2_ready"), sem("zeroed")

        class Layer:
            def __init__(self, l):
                once = ROUTE_LINKS * l, l, TILES * l, 4 * TILES * l
                self.chain0, self.one0, self.tile0, self.chunk0 = once
                self.scatter0, self.gather0 = 16 * B * l, 16 * GROUP * l
                self.load0 = (48 * ((TILES + 1) // 2) * l, 48 * (TILES // 2) * l)
                self.store0 = (16 * ((TILES + 1) // 2) * l, 16 * (TILES // 2) * l)
        layers = [Layer(0), Layer(1)]
        (chain, onehot_ready, rank_done, total_done, pos_ready, tab_ready, share_in, share_exp, share_ready,
         scattered, xtT_done, xtT_ready, up_done, hid_ready, down_done, y_ready) = (sem(n) for n in (
             "chain", "onehot_ready", "rank_done", "total_done", "pos_ready", "tab_ready", "share_in", "share_exp", "share_ready",
             "scattered", "xtT_done", "xtT_ready", "up_done", "hid_ready", "down_done", "y_ready"))
        loaded = [sem(f"loaded{p}") for p in range(2)]
        y_stored = [sem(f"y_stored{p}") for p in range(2)]
        gathered = [sem(f"gathered{g}") for g in range(NG)]
        x2_chain, gmv_ready, gln_ready, gr_ready, gx_ready, gT_done = (sem(n) for n in ("x2_chain", "gmv_ready", "gln_ready", "gr_ready", "gx_ready", "gT_done"))
        h_ready, sq_ready, ss_done, rs_chain, diag_ready, rb_done, hs_ready = (
            sem(n) for n in ("h_ready", "sq_ready", "ss_done", "rs_chain", "diag_ready", "rb_done", "hs_ready"))
        c_done, cmax_ready, csub_ready, cexp_ready, rsq_ready, crec_ready, att_ready = (
            sem(n) for n in ("c_done", "cmax_ready", "csub_ready", "cexp_ready", "rsq_ready", "crec_ready", "att_ready"))
        asum_done, arec_ready, attn_ready, gh_done, gx_done = (sem(n) for n in ("asum_done", "arec_ready", "attn_ready", "gh_done", "gx_done"))
        hnb_ready, tr_ready, tz_ready, u_ready, un_ready, nn_ready, dd_ready, e_ready = (
            sem(n) for n in ("hnb_ready", "tr_ready", "tz_ready", "u_ready", "un_ready", "nn_ready", "dd_ready", "e_ready"))
        hb_done, x3_chain, gmv3_ready, gln3_ready, gr3_ready, x3_ready, x3T_done, x3T_ready, logit_done, logit_ready = (
            sem(n) for n in ("hb_done", "x3_chain", "gmv3_ready", "gln3_ready", "gr3_ready", "x3_ready", "x3T_done", "x3T_ready", "logit_done", "logit_ready"))
        fin_chain, fin_ready = sem("fin_chain"), sem("fin_ready")

        def route_vector(dve, l):
            L = layers[l]
            count = [0]

            def link(ins):
                count[0] += 1
                ins.then_inc(chain, 1)
                dve.wait_ge(chain, L.chain0 + count[0])
            link(nc.vector.tensor_reduce(amax[:], aff_all[:], X, ALU.max))
            peak = amax[:].unsqueeze(2).broadcast_to([P, B, E])
            if l == 0:
                nc.vector.tensor_scalar(share[:], amax[:], -1.0, None, ALU.mult).then_inc(share_in, 1)
            else:
                nc.vector.tensor_tensor(eg[:], aff_all[:], peak, ALU.subtract).then_inc(share_in, 1)
            link(nc.vector.tensor_tensor(apick[:], aff_all[:], peak, ALU.is_ge))
            link(nc.vector.tensor_tensor(apick[:], apick[:], consts[:, C_TIE:C_TIE + B * E].rearrange("p (b e) -> p b e", e=E), ALU.mult))
            link(nc.vector.tensor_reduce(amax[:], apick[:], X, ALU.max))
            nc.vector.tensor_tensor(onehot[:], apick[:], peak, ALU.is_equal).then_inc(onehot_ready, 1)
            dve.wait_ge(total_done, L.one0 + 1)
            link(nc.vector.tensor_copy(tot[:], bank[1][:, 0:B * E].rearrange("p (b e) -> p e b", e=E)))
            link(nc.vector.tensor_tensor_scan(cum[:], consts[:, C_RESET:C_RESET + E * B], tot[:].rearrange("p e b -> p (e b)"), 0.0, ALU.mult, ALU.add))
            cum_v = cum[:].rearrange("p (e b) -> p e b", b=B)
            link(nc.vector.tensor_scalar(n_pad[:], cum_v[:, :, B - 1:B].rearrange("p e b -> p (e b)"), P - 1.0, None, ALU.add))
            link(nc.vector.tensor_scalar(n_tile_i[:], n_pad[:], 7, None, ALU.arith_shift_right))
            link(nc.vector.tensor_copy(n_tile[:], n_tile_i[:]))
            link(nc.vector.tensor_tensor_scan(tile_end[:], ones_e[:], n_tile[:], 0.0, ALU.mult, ALU.add))
            link(nc.vector.tensor_tensor(tile_cmp[:], tile_end[:].unsqueeze(1).broadcast_to([P, TILES, E]),
                                         consts[:, C_JOTA:C_JOTA + TILES * E].rearrange("p (j e) -> p j e", e=E), ALU.is_le))
            link(nc.vector.tensor_reduce(tile_e[:], tile_cmp[:], X, ALU.add))
            nc.vector.tensor_scalar(tile_tab[:], tile_e[:], E - 1.0, None, ALU.min).then_inc(tab_ready, 1)
            link(nc.vector.scalar_tensor_tensor(base[:], n_tile[:], -1.0, tile_end[:], ALU.mult, ALU.add))
            link(nc.vector.tensor_scalar(base[:], base[:], float(P), None, ALU.mult))
            link(nc.vector.tensor_tensor(cum[:], cum[:], tot[:].rearrange("p e b -> p (e b)"), ALU.subtract))
            link(nc.vector.tensor_tensor(cum_v, cum_v, base[:].unsqueeze(2).broadcast_to([P, E, B]), ALU.add))
            dve.wait_ge(rank_done, L.one0 + 1)
            link(nc.vector.tensor_tensor(pos_be[:], bank[0][:, 0:B * E].rearrange("p (b e) -> p b e", e=E), cum[:].rearrange("p (e b) -> p b e", b=B), ALU.add))
            link(nc.vector.tensor_tensor(pos_be[:], pos_be[:], onehot[:], ALU.mult))
            link(nc.vector.tensor_reduce(pos_f[:], pos_be[:], X, ALU.add))
            nc.vector.tensor_copy(pos[:], pos_f[:]).then_inc(pos_ready, 1)
            dve.wait_ge(share_exp, L.one0 + 1)
            if l == 0:
                link(nc.vector.tensor_scalar(share[:], share[:], 1.0, None, ALU.add))
            else:
                link(nc.vector.tensor_reduce(share[:], eg[:], X, ALU.add))
            nc.vector.reciprocal(share[:], share[:]).then_inc(share_ready, 1)
            assert count[0] == ROUTE_LINKS

        def route_tensor(pe, l):
            L = layers[l]
            pe.wait_ge(onehot_ready, L.one0 + 1)
            flat = onehot[:].rearrange("p b e -> p (b e)")
            nc.tensor.matmul(bank[1][:, 0:B * E], ones_b[:], flat, start=True, stop=True).then_inc(total_done, 1)
            nc.tensor.matmul(bank[0][:, 0:B * E], upper[:], flat, start=True, stop=True).then_inc(rank_done, 1)

        def route_scalar(act, l):
            L = layers[l]
            act.wait_ge(share_in, L.one0 + 1)
            t = share if l == 0 else eg
            nc.scalar.activation(t[:], t[:], ACT.Exp).then_inc(share_exp, 1)

        def scatter(pool, l):
            L = layers[l]
            pool.wait_ge(pos_ready, L.one0 + 1)
            pool.wait_ge(zeroed, 32)
            for b in range(B):
                nc.gpsimd.indirect_dma_start(xs_dram[l], bass.IndirectOffsetOnAxis(pos[:, b:b + 1], 0), xh_all[:, b, :], None).then_inc(scattered, 16)

        def gather(pool, l):
            L = layers[l]
            pool.wait_ge(y_stored[0], L.store0[0] + 16 * ((TILES + 1) // 2))
            pool.wait_ge(y_stored[1], L.store0[1] + 16 * (TILES // 2))
            for b in range(B):
                nc.gpsimd.indirect_dma_start(f_all[:, b, :], None, ys_dram[l], bass.IndirectOffsetOnAxis(pos[:, b:b + 1], 0)).then_inc(gathered[b // GROUP], 16)

        def up(p, c):
            return bank[(2, 6)[p] + c // 2][:, c % 2 * P:(c % 2 + 1) * P]

        def tile_rows(dram, j):
            return dram[bass.ds(j * P, P), :]

        def experts_sync(sp, l):
            L = layers[l]
            sp.wait_ge(tab_ready, L.one0 + 1)
            sp.wait_ge(scattered, L.scatter0 + 16 * B)

            def load(j, p):
                e = sp.value_load(tile_tab[0:1, bass.ds(j, 1)], min_val=0, max_val=E - 1)
                need(sp, down_done, L.tile0 + (j - 1))
                sp.dma_start(wp[p][:], a[f"wf{l}"][bass.ds(e, 1)].rearrange("o p n -> (o p) n")).then_inc(loaded[p], 16)
                sp.dma_start(b2r[p][:], a[f"b2{l}"][bass.ds(e, 1)]).then_inc(loaded[p], 16)
                sp.dma_start(xt[p][:], tile_rows(xs_dram[l], j)).then_inc(loaded[p], 16)

            def store(j, p):
                sp.wait_ge(y_ready, L.tile0 + (j + 1))
                sp.dma_start(tile_rows(ys_dram[l], j), yt[p][:]).then_inc(y_stored[p], 16)

            def step(j, p):
                fixed = isinstance(j, int)
                if not fixed or j < TILES:
                    load(j, p)
                if not fixed or j >= 2:
                    store(j - 2, p)
            skewed(sp, 0, (2, 22), TILES + 1, step)

        def experts_tensor(pe, l):
            L = layers[l]

            def turn(j, p):
                pe.wait_ge(loaded[p], (j - p) * 24 + (48 + L.load0[p]))
                need(pe, xtT_ready, L.tile0 + (j - 1))
                nc.tensor.transpose(bank[p][:, 0:P], xt[p][:], ident).then_inc(xtT_done, 1)

            def step(j, p):
                pe.wait_ge(xtT_ready, L.tile0 + (j + 1))
                need(pe, hid_ready, (j - 1) * 4 + L.chunk0)
                for c in range(FC):
                    last = nc.tensor.matmul(up(p, c), wp[p][:, c * P:(c + 1) * P], xtT[p][:], start=True, stop=True)
                    if c % 2:
                        last.then_inc(up_done, 1)
                if not isinstance(j, int) or j + 1 < TILES:
                    turn(j + 1, 1 - p)
                need(pe, y_ready, L.tile0 + (j - 1))
                nc.tensor.matmul(bank[4 + p][:, 0:D], one_row[:], b2r[p][:], start=True, stop=False)
                for c in range(FC):
                    pe.wait_ge(hid_ready, j * 4 + (L.chunk0 + c + 1))
                    last = nc.tensor.matmul(bank[4 + p][:, 0:D], hid[p][:, c, :], wp[p][:, W_2 + c * D:W_2 + (c + 1) * D], start=False, stop=c == FC - 1)
                last.then_inc(down_done, 1)
            turn(0, 0)
            skewed(pe, 0, (2, 22), TILES - 1, step)

        def experts_scalar(act, l):
            L = layers[l]

            def step(j, p):
                act.wait_ge(xtT_done, L.tile0 + (j + 1))
                if l == 0:
                    nc.scalar.activation(xtT[p][:], bank[p][:, 0:P], ACT.Identity, scale=wp[p][:, W_G:W_G + 1], bias=wp[p][:, W_B:W_B + 1]).then_inc(xtT_ready, 1)
                else:
                    nc.scalar.copy(xtT[p][:], bank[p][:, 0:P]).then_inc(xtT_ready, 1)
                for c in range(FC):
                    act.wait_ge(up_done, j * 2 + (2 * L.tile0 + c // 2 + 1))
                    nc.scalar.activation(hid[p][:, c, :], up(p, c), ACT.Silu if l else ACT.Relu,
                                         bias=wp[p][:, W_B1 + c:W_B1 + c + 1]).then_inc(hid_ready, 1)
            skewed(act, 0, (2, 22), TILES - 1, step)

        def experts_vector(dve, l):
            L = layers[l]

            def step(j, p):
                dve.wait_ge(down_done, L.tile0 + (j + 1))
                need(dve, y_stored[p], (j - p) * 8 + L.store0[p])
                nc.vector.tensor_copy(yt[p][:], bank[4 + p][:, 0:D]).then_inc(y_ready, 1)
            skewed(dve, 0, (2, 22), TILES - 1, step)

        SLOT_MAIN = (2, 10)

        MAIN = (4, 14)
        block = ctx.enter_context(nc.Block())

        @block.sync
        def _(sp):
            sp.dma_start(consts[:], a["consts"]).then_inc(ld_const, 16)
            sp.dma_start(vecs[:], a["vecs"]).then_inc(ld_const, 16)
            sp.dma_start(w0[:], a["w0"]).then_inc(ld_const, 16)
            sp.dma_start(ctxT_all[:], a["ctxT_all"]).then_inc(ld_const, 16)
            sp.dma_start(x_all[:, 0:4, :], a["x"][0:4].rearrange("b s d -> s b d")).then_inc(ld_x, 16)
            sp.dma_start(w1[:], a["w1"]).then_inc(ld_w1, 16)
            sp.dma_start(gru[:], a["gru"]).then_inc(ld_w1, 16)
            sp.dma_start(gates[:], a["gates"]).then_inc(ld_w1, 16)
            sp.dma_start(x_all[:, 4:B, :], a["x"][4:B].rearrange("b s d -> s b d")).then_inc(ld_x, 16)

            def load(b, p):
                need(sp, cproj, 2 * (b - 1))
                sp.dma_start(ctxT[p][:], a["ctxT"][b:b + 1] if isinstance(b, int) else a["ctxT"][bass.ds(b, 1)]).then_inc(ld_ctxT[p], 16)
            skewed(sp, 0, (2, B), B - 1, load)
            sp.wait_ge(memset_ready, 10)
            for l in range(2):
                sp.dma_start(xs_dram[l].rearrange("(j p) d -> p j d", p=P), zero[:].unsqueeze(1).broadcast_to([P, TILES, D])).then_inc(zeroed, 16)
            experts_sync(sp, 0)
            experts_sync(sp, 1)
            for g in range(NG):
                sp.wait_ge(fin_ready, g + 1)
                sp.dma_start(out[g * GROUP:(g + 1) * GROUP].rearrange("b s d -> s b d"), f_all[:, g * GROUP:(g + 1) * GROUP, :]).then_inc(stored, 16)
            sp.wait_ge(stored, 16 * NG)

        @block.gpsimd
        def _(pool):
            nc.gpsimd.memset(v_all[:], 1.0).then_inc(memset_ready, 1)
            nc.gpsimd.memset(ones3[:], 1.0).then_inc(memset_ready, 1)
            nc.gpsimd.memset(eps_ln[:], LN_EPS).then_inc(memset_ready, 1)
            nc.gpsimd.memset(eps_rms[:], RMS_EPS).then_inc(memset_ready, 1)
            nc.gpsimd.memset(ones_b[:], 1.0).then_inc(memset_ready, 1)
            nc.gpsimd.memset(ones_f[:], 1.0).then_inc(memset_ready, 1)
            nc.gpsimd.memset(ones_e[:], 1.0).then_inc(memset_ready, 1)
            nc.gpsimd.memset(one_row[:], 1.0).then_inc(memset_ready, 1)
            nc.gpsimd.memset(zero[:], 0.0).then_inc(memset_ready, 1)
            nc.gpsimd.memset(att[0][:], ATT_EPS)
            nc.gpsimd.memset(att[1][:], ATT_EPS).then_inc(memset_ready, 1)
            pool.wait_ge(ld_ctx, 32)
            nc.gpsimd.tensor_tensor(ctx_sq[:], ctx_all[:], ctx_all[:], ALU.mult).then_inc(ctxsq_ready, 1)
            pool.wait_ge(kT_ready, 3)
            pool.wait_ge(ld_const, 64)
            pool.wait_ge(ld_rows, 32)
            pool.wait_ge(ld_x, 32)

            def step(b, p):
                need(pool, s_done, 3 * (b - 1))
                nc.gpsimd.tensor_tensor(
                    kblk[p][:], kT_all[:, bass.ds(b * M, M)].unsqueeze(1).broadcast_to([P, H, M]),
                    headmask.unsqueeze(2).broadcast_to([P, H, M]), ALU.mult).then_inc(kblk_ready, 1)
                need(pool, x1_ready, b - 1)
                nc.gpsimd.tensor_tensor(xbo[p][:], x_all[:, bass.ds(b, 1), :].rearrange("p o d -> p (o d)"), rows[:, R_BO:R_BO + D], ALU.add).then_inc(xbo_ready, 1)

            def residual(b, p):
                pool.wait_ge(xin_ready, b + 1)
                nc.gpsimd.tensor_tensor(res_all[:, bass.ds(b, 1), :].rearrange("p o d -> p (o d)"), x1[p][:], xin[p][:], ALU.add).then_inc(res_ready, 1)

            def both(t, p):
                if not isinstance(t, int) or t + 1 < B:
                    step(t + 1, 1 - p)
                if not isinstance(t, int) or 0 <= t - 2:
                    residual(t - 2, p)
            skewed(pool, -1, MAIN, B + 1, both)
            scatter(pool, 0)
            gather(pool, 0)

            def slot_step(s, g):
                p = g % 2
                pool.wait_ge(nn_ready, s + 1)
                nc.gpsimd.tensor_tensor(dd[p][:], hT[:, g * G:(g + 1) * G], nn[p][:], ALU.subtract).then_inc(dd_ready, 1)
            skewed_groups(pool, 0, (4, 12), SLOT_STEPS - 1, slot_step)
            pool.wait_ge(x3_ready, NG)
            scatter(pool, 1)
            gather(pool, 1)

        @block.scalar
        def _(act):
            act.dma_start(mask_i[:], a["mask"].partition_broadcast(P)).then_inc(ld_ctx, 16)
            act.dma_start(ctx_all[:], a["ctx"].rearrange("b m d -> m b d")).then_inc(ld_ctx, 16)
            act.dma_start(rows[:], a["rows"].partition_broadcast(P)).then_inc(ld_rows, 16)
            act.dma_start(negp[:], a["negp"]).then_inc(ld_rows, 16)
            act.preload_act_table_set("natural_log_exp_and_others")
            act.wait_ge(memset_ready, 10)
            act.wait_ge(ctxms_ready, 1)
            nc.scalar.activation(ctx_ln[:], ctx_ms[:], ACT.Ln, scale=1.0 / D, bias=eps_rms[0:M, :]).then_inc(ctxln_ready, 1)
            act.wait_ge(ctxln_ready, 1)
            nc.scalar.activation(ctx_r[:], ctx_ln[:], ACT.Exp, scale=-0.5).then_inc(ctxr_ready, 1)
            act.wait_ge(ctxr_ready, 1)

            def rstd_of(b, mv_ready, mvt, ln_t, ln_sem, r_t, r_sem):
                act.wait_ge(mv_ready, b + 1)
                nc.scalar.activation(ln_t[:], mvt[:, 1:2], ACT.Ln, bias=eps_ln[:]).then_inc(ln_sem, 1)
                act.wait_ge(ln_sem, b + 1)
                nc.scalar.activation(r_t[:], ln_t[:], ACT.Exp, scale=-0.5).then_inc(r_sem, 1)

            def context(b, p):
                act.wait_ge(cproj, 2 * b + 2)
                need(act, kqT_done, b - 1)
                nc.scalar.activation(kq[p][:], bank[2 + p][0:M, 0:D], ACT.Copy, scale=ctx_r[:, bass.ds(b, 1)]).then_inc(kq_ready, 1)
                nc.scalar.activation(vw_all[:, bass.ds(b, 1), :].rearrange("p o d -> p (o d)"), bank[2 + p][0:M, D:], ACT.Copy,
                                     scale=ctx_r[:, bass.ds(b, 1)]).then_inc(vw_ready, 1)
            skewed(act, 0, (2, B), B - 1, context)

            def step(t, p):
                fixed = isinstance(t, int)
                if not fixed or t - 2 >= 0:
                    act.wait_ge(oT_done, t - 1)
                    nc.scalar.copy(oT[p][:], bank[7][:, 0:P]).then_inc(oT_ready, 1)
                if not fixed or 0 <= t + 1 < B:
                    act.wait_ge(xnT_done, t + 2)
                    nc.scalar.copy(xnT[1 - p][:], bank[6][:, 0:P]).then_inc(xnT_ready, 1)
                for q in range(4):
                    if not fixed or 0 <= t - 1 < B:
                        n = (t - 1) * 4 + q
                        act.wait_ge(pT_done, n + 1)
                        need(act, pv_done, n - 1)
                        nc.scalar.copy(pT[q % 2][:], bank[3 + q % 2][0:M, :].rearrange("m (i s) -> m i s", i=4)).then_inc(pT_ready, 1)
                    if q == 1 and (not fixed or 0 <= t + 1 < B):
                        act.wait_ge(q_done, t + 2)
                        need(act, s_done, 3 * t)
                        nc.scalar.activation(qT[1 - p][:], bank[6][:, P:2 * P], ACT.Identity, scale=HD ** -0.5, bias=bq[:]).then_inc(q_ready, 1)
                if not fixed or 0 <= t < B:
                    act.wait_ge(sub_ready, 3 * t + 3)
                    nc.scalar.activation(probs[p][:], probs[p][:], ACT.Exp).then_inc(exp_ready, 1)
                if not fixed or t + 2 < B:
                    rstd_of(t + 2, lnx_mv, mv[p], lnv[p], lnx_ln, rstd[p], lnx_r)
                if not fixed or t - 2 >= 0:
                    rstd_of(t - 2, mv1_ready, mv1[p], lnv1[p], ln1_ready, rstd1[p], r1_ready)
                    rstd_of(t - 2, mv2_ready, mv2[p], lnv2[p], ln2_ready, rstd2[p], r2_ready)
                    act.wait_ge(xinT_done, t - 1)
                    nc.scalar.copy(xinT[p][:], bank[7][:, 2 * P:3 * P]).then_inc(xinT_ready, 1)
            skewed(act, -2, MAIN, B + 1, step)
            route_scalar(act, 0)
            experts_scalar(act, 0)

            def group_rstd(g, mv_sem, ln_sem, r_sem):
                act.wait_ge(mv_sem, g + 1)
                nc.scalar.activation(gln[:], gmv[:, :, 1:2].rearrange("p b o -> p (b o)"), ACT.Ln, bias=eps_ln[:]).then_inc(ln_sem, 1)
                act.wait_ge(ln_sem, g + 1)
                nc.scalar.activation(gr[:], gln[:], ACT.Exp, scale=-0.5).then_inc(r_sem, 1)
            act.preload_act_table_set("natural_log_exp_and_others")
            for g in range(NG):
                group_rstd(g, gmv_ready, gln_ready, gr_ready)
            act.preload_act_table_set("exp_and_others")

            def slot_step(s, g):
                fixed = isinstance(s, int)
                p = g % 2
                if not fixed or 0 <= s - 1:
                    act.wait_ge(gh_done, s)
                    nc.scalar.activation(hnb[1 - p][:], bank[6][:], ACT.Identity, scale=0.5, bias=bhn[:]).then_inc(hnb_ready, 1)
                if not fixed or s + 1 < SLOT_STEPS:
                    g1 = (g + 1) % NG
                    act.wait_ge(h_ready, s + 2)
                    nc.scalar.activation(sq[1 - p][:], hT[:, g1 * G:(g1 + 1) * G], ACT.Square).then_inc(sq_ready, 1)
                if not fixed or 0 <= s < SLOT_STEPS:
                    act.wait_ge(csub_ready, s + 1)
                    nc.scalar.activation(ex[p][:], ex[p][:], ACT.Exp).then_inc(cexp_ready, 1)
                if not fixed or 0 <= s - 1:
                    act.wait_ge(gx_done, s)
                    nc.scalar.activation(tr[1 - p][:], bank[4][:], ACT.Tanh, scale=0.5, bias=brz[:, 0:1]).then_inc(tr_ready, 1)
                    nc.scalar.activation(tz[1 - p][:], bank[5][:], ACT.Tanh, scale=0.5, bias=brz[:, 1:2]).then_inc(tz_ready, 1)
                    act.wait_ge(un_ready, s)
                    nc.scalar.activation(nn[1 - p][:], u[1 - p][:], ACT.Tanh, bias=vecs[:, V_BIH + 2:V_BIH + 3]).then_inc(nn_ready, 1)
            skewed_groups(act, -1, SLOT_MAIN, SLOT_STEPS, slot_step)
            act.preload_act_table_set("natural_log_exp_and_others")
            for g in range(NG):
                group_rstd(g, gmv3_ready, gln3_ready, gr3_ready)
                act.wait_ge(x3T_done, g + 1)
                nc.scalar.copy(x3T[g % 2][:], bank[4 + g][:]).then_inc(x3T_ready, 1)
            route_scalar(act, 1)
            experts_scalar(act, 1)

        @block.vector
        def _(dve):
            dve.wait_ge(ld_ctx, 32)
            nc.vector.tensor_scalar(mask_f[:], mask_i[:], 0.0, None, ALU.not_equal).then_inc(mask_ready, 1)
            dve.wait_ge(ld_const, 64)
            dve.wait_ge(ld_rows, 32)
            dve.wait_ge(mask_ready, 1)
            nc.vector.tensor_scalar(neg3[:], mask_f[0:3, :], 0.0, negp[:], ALU.is_equal, ALU.mult).then_inc(neg_ready, 1)
            nc.vector.tensor_scalar(bq[:], vecs[:, V_BQ:V_BQ + 1], HD ** -0.5, None, ALU.mult).then_inc(small_ready, 1)
            nc.vector.tensor_copy(upper[:], consts[:, C_UPPER:C_UPPER + P]).then_inc(consts2_ready, 1)
            nc.vector.tensor_tensor(brz[:], vecs[:, V_BIH:V_BIH + 2], vecs[:, V_BHH:V_BHH + 2], ALU.add).then_inc(consts2_ready, 1)
            nc.vector.tensor_scalar(bhn[:], vecs[:, V_BHH + 2:V_BHH + 3], 0.5, None, ALU.mult).then_inc(consts2_ready, 1)
            dve.wait_ge(consts2_ready, 3)
            nc.vector.tensor_scalar(brz[:], brz[:], 0.5, None, ALU.mult).then_inc(consts2_ready, 1)
            nc.vector.tensor_scalar(wslot[:], vecs[:, V_WSLOT:V_WSLOT + 1], D ** -0.5, None, ALU.mult).then_inc(small_ready, 1)
            for c in range(3):
                lo, hi = c * 512, min((c + 1) * 512, B * M)
                dve.wait_ge(kproj, c + 1)
                nc.vector.scalar_tensor_tensor(kT_all[:, lo:hi], bank[5 + c][:, 0:hi - lo], vecs[:, V_BK:V_BK + 1], mask_f[:, lo:hi],
                                               ALU.add, ALU.mult).then_inc(kT_ready, 1)
            dve.wait_ge(ctxsq_ready, 1)
            nc.vector.tensor_reduce(ctx_ms[:], ctx_sq[:], X, ALU.add).then_inc(ctxms_ready, 1)
            dve.wait_ge(abproj, 2)
            nc.vector.tensor_scalar(ab[:, 0:D], bank[0][:, 0:D], vecs[:, V_WIN:V_WIN + 1], None, ALU.mult).then_inc(ab_ready, 1)
            nc.vector.tensor_scalar(ab[:, D:], bank[1][:, 0:GATES], vecs[:, V_WIN:V_WIN + 1], None, ALU.mult).then_inc(ab_ready, 1)

            def context(b, p):
                dve.wait_ge(cproj, 2 * b + 1)
                if isinstance(b, int) and b == 0:
                    dve.wait_ge(memset_ready, 10)
                nc.vector.tensor_tensor(
                    v_all[:, bass.ds(b, 1), :].rearrange("m o (h c) -> m (o h) c", c=HV)[:, :, 0:HD],
                    bank[p][0:M, 0:D].rearrange("m (h c) -> m h c", c=HD),
                    rows[0:M, R_BV:R_BV + D].rearrange("m (h c) -> m h c", c=HD), ALU.add).then_inc(v_ready, 1)
                dve.wait_ge(kqT_done, b + 1)
                nc.vector.tensor_scalar(kq_all[:, bass.ds(b, 1), :].rearrange("p o m -> p (o m)"), bank[4 + p][:, 0:M], wslot[:], None,
                                        ALU.mult).then_inc(kqT_ready, 1)
            dve.wait_ge(small_ready, 2)
            dve.wait_ge(ld_x, 32)
            skewed(dve, 0, (2, B), B - 1, context)

            def stats(b, src, st_t, st_sem, mv_t, mv_sem):
                nc.vector.bn_stats(st_t[:], src).then_inc(st_sem, 1)
                dve.wait_ge(st_sem, b + 1)
                nc.vector.memset(hold[:], 0.0)
                nc.vector.bn_aggr(mv_t[:], st_t[:]).then_inc(mv_sem, 1)

            def step(t, p):
                fixed = isinstance(t, int)
                if not fixed or 0 <= t < B:
                    for g, (h0, n) in enumerate(HEAD_GROUPS):
                        src = bank[g][:, 0:n * M].rearrange("p (h m) -> p h m", m=M)
                        dve.wait_ge(s_done, 3 * t + g + 1)
                        nc.vector.tensor_reduce(smax[p][:, h0:h0 + n], src, X, ALU.max).then_inc(max_ready, 1)
                        dve.wait_ge(max_ready, 3 * t + g + 1)
                        need(dve, pT_done, 4 * (t - 1))
                        nc.vector.tensor_tensor(probs[p][:, h0:h0 + n, :], src, smax[p][:, h0:h0 + n].unsqueeze(2).broadcast_to([P, n, M]),
                                                ALU.subtract).then_inc(sub_ready, 1)
                if not fixed or t + 2 < B:
                    b = t + 2
                    stats(b, x_all[:, bass.ds(b, 1), :].rearrange("p o d -> p (o d)"), st[p], lnx_st, mv[p], lnx_mv)
                if not fixed or t - 2 >= 0:
                    b = t - 2
                    dve.wait_ge(wo_done, b + 1)
                    dve.wait_ge(xbo_ready, b + 1)
                    need(dve, res_ready, b - 1)
                    nc.vector.tensor_tensor(x1[p][:], bank[7][:, P:2 * P], xbo[p][:], ALU.add).then_inc(x1_ready, 1)
                    dve.wait_ge(x1_ready, b + 1)
                    stats(b, x1[p][:], st1[p], st1_ready, mv1[p], mv1_ready)
                if not fixed or t + 2 < B:
                    b = t + 2
                    dve.wait_ge(lnx_r, b + 1)
                    need(dve, xnT_done, b - 1)
                    nc.vector.tensor_scalar(xn[p][:], x_all[:, bass.ds(b, 1), :].rearrange("p o d -> p (o d)"), mv[p][:, 0:1], rstd[p][:],
                                            ALU.subtract, ALU.mult).then_inc(xn_ready, 1)
                if not fixed or t - 2 >= 0:
                    b = t - 2
                    dve.wait_ge(r1_ready, b + 1)
                    nc.vector.tensor_scalar(xin[p][:], x1[p][:], mv1[p][:, 0:1], rstd1[p][:], ALU.subtract, ALU.mult).then_inc(xin_ready, 1)
                    dve.wait_ge(xin_ready, b + 1)
                    stats(b, xin[p][:], st2[p], st2_ready, mv2[p], mv2_ready)
                    dve.wait_ge(r2_ready, b + 1)
                    nc.vector.tensor_scalar(xh_all[:, bass.ds(b, 1), :].rearrange("p o d -> p (o d)"), xin[p][:], mv2[p][:, 0:1], rstd2[p][:],
                                            ALU.subtract, ALU.mult).then_inc(xh_ready, 1)
                if not fixed or 0 <= t - 1 < B:
                    b = t - 1
                    acc = bank[5][:, 0:H * HV].rearrange("p (h c) -> p h c", c=HV)
                    dve.wait_ge(pv_done, 4 * b + 4)
                    nc.vector.reciprocal(rden[1 - p][:], acc[:, :, HD:HV].rearrange("p h c -> p (h c)")).then_inc(rden_ready, 1)
                    dve.wait_ge(rden_ready, b + 1)
                    need(dve, oT_done, b - 1)
                    nc.vector.tensor_tensor(o_sb[1 - p][:].rearrange("p (h c) -> p h c", c=HD), acc[:, :, 0:HD],
                                            rden[1 - p][:].unsqueeze(2).broadcast_to([P, H, HD]), ALU.mult).then_inc(o_ready, 1)
                if not fixed or t - 2 >= 0:
                    b = t - 2
                    dve.wait_ge(aff_done, b + 1)
                    nc.vector.tensor_copy(aff_all[:, bass.ds(b, 1), :].rearrange("p o e -> p (o e)"), bank[7][:, 3 * P:3 * P + E]).then_inc(aff_ready, 1)
            skewed(dve, -2, MAIN, B + 1, step)
            dve.wait_ge(aff_ready, B)
            route_vector(dve, 0)
            experts_vector(dve, 0)

            def group_norm(g, src, chain, base_count, mv_sem, r_sem, dst, dst_sem):
                for i in range(GROUP):
                    nc.vector.bn_stats(gst[:, i, :], src[:, i, :]).then_inc(chain, 1)
                dve.wait_ge(chain, base_count + GROUP)
                for i in range(GROUP):
                    last = nc.vector.bn_aggr(gmv[:, i, :], gst[:, i, :])
                last.then_inc(mv_sem, 1)
                dve.wait_ge(mv_sem, g + 1)
                nc.vector.tensor_tensor(dst, src, gmv[:, :, 0:1].broadcast_to([P, GROUP, D]), ALU.subtract).then_inc(chain, 1)
                dve.wait_ge(chain, base_count + GROUP + 1)
                dve.wait_ge(r_sem, g + 1)
                nc.vector.tensor_tensor(dst, dst, gr[:].unsqueeze(2).broadcast_to([P, GROUP, D]), ALU.mult).then_inc(dst_sem, 1)

            for g in range(NG):
                gb = slice(g * GROUP, (g + 1) * GROUP)
                K = 2 + GROUP + 1
                dve.wait_ge(gathered[g], 16 * GROUP)
                dve.wait_ge(share_ready, 1)
                nc.vector.tensor_tensor(f_all[:, gb, :], f_all[:, gb, :], share[:, gb].unsqueeze(2).broadcast_to([P, GROUP, D]), ALU.mult).then_inc(x2_chain, 1)
                dve.wait_ge(x2_chain, K * g + 1)
                dve.wait_ge(res_ready, B)
                nc.vector.tensor_tensor(x2_all[:, gb, :], f_all[:, gb, :], res_all[:, gb, :], ALU.add).then_inc(x2_chain, 1)
                dve.wait_ge(x2_chain, K * g + 2)
                need(dve, gT_done, g - 1)
                group_norm(g, x2_all[:, gb, :], x2_chain, K * g + 2, gmv_ready, gr_ready, gx[g % 2][:], gx_ready)
                if g:
                    dve.wait_ge(gT_done, g)
                    nc.vector.tensor_copy(hT[:, (g - 1) * G:g * G], bank[4 + g - 1][:]).then_inc(h_ready, 1)
            dve.wait_ge(gT_done, NG)
            nc.vector.tensor_copy(hT[:, (NG - 1) * G:], bank[4 + NG - 1][:]).then_inc(h_ready, 1)

            def slot_step(s, g):
                fixed = isinstance(s, int)
                p = g % 2
                now = not fixed or 0 <= s < SLOT_STEPS
                before = not fixed or 0 <= s - 1 < SLOT_STEPS
                after = not fixed or s + 1 < SLOT_STEPS
                g0 = (g - 1) % NG
                h0 = hT[:, g0 * G:(g0 + 1) * G]
                if before:
                    dve.wait_ge(asum_done, s)
                    nc.vector.reciprocal(arec[1 - p][:], bank[3][0:M, :]).then_inc(arec_ready, 1)
                    dve.wait_ge(arec_ready, s)
                    nc.vector.tensor_tensor(attn[1 - p][:], att[1 - p][0:M, :], arec[1 - p][:], ALU.mult).then_inc(attn_ready, 1)
                if now:
                    dve.wait_ge(rb_done, s + 1)
                    nc.vector.tensor_tensor(hs[p][:], hT[:, g * G:(g + 1) * G], bank[1][:], ALU.mult).then_inc(hs_ready, 1)
                    dve.wait_ge(c_done, s + 1)
                    sc = bank[2][0:M, :].rearrange("m (b s) -> m b s", s=S)
                    nc.vector.tensor_reduce(cmax[p][:], sc, X, ALU.max).then_inc(cmax_ready, 1)
                    dve.wait_ge(cmax_ready, s + 1)
                    nc.vector.tensor_tensor(ex[p][:], sc, cmax[p][:].unsqueeze(2).broadcast_to([M, GROUP, S]), ALU.subtract).then_inc(csub_ready, 1)
                if after:
                    q = 1 - p
                    K = 11
                    at = (s + 1) * K
                    dve.wait_ge(ss_done, s + 2)
                    nc.vector.tensor_scalar(ms[q][:], bank[0][:, 0:GROUP], 1.0 / D, RMS_EPS, ALU.mult, ALU.add).then_inc(rs_chain, 1)
                    dve.wait_ge(rs_chain, at + 1)
                    nc.vector.tensor_scalar(half[q][:], ms[q][:].bitcast(I32), 1, None, ALU.arith_shift_right).then_inc(rs_chain, 1)
                    dve.wait_ge(rs_chain, at + 2)
                    nc.vector.tensor_scalar(guess[q][:], half[q][:], -1.0, 1597463007.0, ALU.mult, ALU.add).then_inc(rs_chain, 1)
                    dve.wait_ge(rs_chain, at + 3)
                    y = guess[q][:].bitcast(F32)
                    for r in range(3):
                        nc.vector.tensor_tensor(y2[q][:], y, y, ALU.mult).then_inc(rs_chain, 1)
                        dve.wait_ge(rs_chain, at + 3 + 3 * r + 1)
                        nc.vector.scalar_tensor_tensor(y2[q][:], y2[q][:], -0.5, ms[q][:], ALU.mult, ALU.mult).then_inc(rs_chain, 1)
                        dve.wait_ge(rs_chain, at + 3 + 3 * r + 2)
                        ins = nc.vector.scalar_tensor_tensor(yv[q][:], y2[q][:], 1.5, y, ALU.add, ALU.mult)
                        y = yv[q][:]
                        if r < 2:
                            ins.then_inc(rs_chain, 1)
                            dve.wait_ge(rs_chain, at + 3 + 3 * r + 3)
                    ins.then_inc(rsq_ready, 1)
                    dve.wait_ge(rsq_ready, s + 2)
                    nc.vector.tensor_tensor(diag[q][:], ident.unsqueeze(1).broadcast_to([P, GROUP, P]), yv[q][:].unsqueeze(2).broadcast_to([P, GROUP, P]),
                                            ALU.mult).then_inc(diag_ready, 1)
                if now:
                    dve.wait_ge(cexp_ready, s + 1)
                    ins = nc.vector.tensor_reduce(csum[p][:], ex[p][:], X, ALU.add)
                    ins.then_inc(crec_ready, 1)
                    dve.wait_ge(crec_ready, 2 * s + 1)
                    nc.vector.reciprocal(crec[p][:], csum[p][:]).then_inc(crec_ready, 1)
                    dve.wait_ge(crec_ready, 2 * s + 2)
                    nc.vector.tensor_tensor(att[p][0:M, :].rearrange("m (b s) -> m b s", s=S), ex[p][:], crec[p][:].unsqueeze(2).broadcast_to([M, GROUP, S]),
                                            ALU.mult).then_inc(att_ready, 1)
                if before:
                    dve.wait_ge(tr_ready, s)
                    dve.wait_ge(hnb_ready, s)
                    nc.vector.scalar_tensor_tensor(u[1 - p][:], tr[1 - p][:], 1.0, hnb[1 - p][:], ALU.add, ALU.mult).then_inc(u_ready, 1)
                    dve.wait_ge(u_ready, s)
                    nc.vector.tensor_tensor(u[1 - p][:], u[1 - p][:], bank[7][:], ALU.add).then_inc(un_ready, 1)
                    dve.wait_ge(dd_ready, s)
                    dve.wait_ge(tz_ready, s)
                    nc.vector.scalar_tensor_tensor(dd[1 - p][:], tz[1 - p][:], 1.0, dd[1 - p][:], ALU.add, ALU.mult).then_inc(e_ready, 1)
                    dve.wait_ge(e_ready, s)
                    nc.vector.scalar_tensor_tensor(h0, dd[1 - p][:], 0.5, nn[1 - p][:], ALU.mult, ALU.add).then_inc(h_ready, 1)
            skewed_groups(dve, -1, SLOT_MAIN, SLOT_STEPS, slot_step)

            for g in range(NG):
                gb = slice(g * GROUP, (g + 1) * GROUP)
                K = 1 + GROUP + 1
                dve.wait_ge(hb_done, g + 1)
                nc.vector.tensor_tensor(x2_all[:, gb, :], x2_all[:, gb, :], bank[g][:].rearrange("p (b d) -> p b d", d=D), ALU.add).then_inc(x3_chain, 1)
                dve.wait_ge(x3_chain, K * g + 1)
                group_norm(g, x2_all[:, gb, :], x3_chain, K * g + 1, gmv3_ready, gr3_ready, xh_all[:, gb, :], x3_ready)
                dve.wait_ge(logit_done, g + 1)
                nc.vector.tensor_tensor(aff_all[:, gb, :], bank[g][:, 0:GROUP * E].rearrange("p (b e) -> p b e", e=E),
                                        rows[:, R_BG:R_BG + E].unsqueeze(1).broadcast_to([P, GROUP, E]), ALU.add).then_inc(logit_ready, 1)
            dve.wait_ge(logit_ready, NG)
            route_vector(dve, 1)
            experts_vector(dve, 1)
            for g in range(NG):
                gb = slice(g * GROUP, (g + 1) * GROUP)
                dve.wait_ge(gathered[g], 2 * 16 * GROUP)
                dve.wait_ge(share_ready, 2)
                nc.vector.tensor_tensor(f_all[:, gb, :], f_all[:, gb, :], share[:, gb].unsqueeze(2).broadcast_to([P, GROUP, D]), ALU.mult).then_inc(fin_chain, 1)
                dve.wait_ge(fin_chain, g + 1)
                nc.vector.tensor_tensor(f_all[:, gb, :], f_all[:, gb, :], x2_all[:, gb, :], ALU.add).then_inc(fin_ready, 1)

        @block.tensor
        def _(pe):
            pe.wait_ge(ld_const, 64)
            for c in range(3):
                lo, hi = c * 512, min((c + 1) * 512, B * M)
                nc.tensor.matmul(bank[5 + c][:, 0:hi - lo], w0[:, 1, :], ctxT_all[:, lo:hi], start=True, stop=True).then_inc(kproj, 1)
            pe.wait_ge(ld_w1, 48)
            nc.tensor.matmul(bank[0][:, 0:D], w1[:, 1, :], w1[:, 0, :], start=True, stop=True).then_inc(abproj, 1)
            nc.tensor.matmul(bank[1][:, 0:GATES], w1[:, 2, :], gru[:, 0, :], start=True, stop=True).then_inc(abproj, 1)
            pe.wait_ge(ab_ready, 2)

            def project(b, p):
                pe.wait_ge(ld_ctxT[p], (b - p) * 8 + 16)
                need(pe, v_ready, b - 1)
                nc.tensor.matmul(bank[p][0:M, 0:D], ctxT[p][:], w0[:, 2, :], start=True, stop=True).then_inc(cproj, 1)
                need(pe, vw_ready, b - 1)
                nc.tensor.matmul(bank[2 + p][0:M, :], ctxT[p][:], ab[:], start=True, stop=True).then_inc(cproj, 1)

            def turn(b, p):
                pe.wait_ge(kq_ready, b + 1)
                need(pe, kqT_ready, b - 1)
                nc.tensor.transpose(bank[4 + p][:, 0:M], kq[p][:], ident[0:M, 0:M]).then_inc(kqT_done, 1)

            pe.wait_ge(kT_ready, 3)
            def project_and_turn(b, p):
                project(b, p)
                turn(b - 1, 1 - p)
            project(0, 0)
            skewed(pe, 1, (2, B), B - 1, project_and_turn)
            turn(B - 1, 1)
            pe.wait_ge(neg_ready, 1)
            pe.wait_ge(kqT_ready, B)
            pe.wait_ge(vw_ready, B)
            pe.wait_ge(v_ready, B)

            def p_turn(b, par, q):
                n = b * 4 + q
                need(pe, pT_ready, n - 1)
                for i in range(4):
                    last = nc.tensor.transpose(bank[3 + q % 2][0:M, i * S:(i + 1) * S], probs[par][:, 4 * q + i, :], ident)
                last.then_inc(pT_done, 1)

            def p_value(b, q):
                n = b * 4 + q
                pe.wait_ge(pT_ready, n + 1)
                if q == 0:
                    need(pe, o_ready, b)
                for i in range(4):
                    h = 4 * q + i
                    last = nc.tensor.matmul(bank[5][:, h * HV:(h + 1) * HV], pT[q % 2][:, i, :],
                                            v_all[:, bass.ds(b, 1), h * HV:(h + 1) * HV].rearrange("m o c -> m (o c)"), start=True, stop=True)
                last.then_inc(pv_done, 1)

            def step(t, p):
                fixed = isinstance(t, int)
                now = not fixed or 0 <= t < B
                before = not fixed or 0 <= t - 1 < B
                after = not fixed or 0 <= t + 1 < B
                old = not fixed or t - 2 >= 0
                if now:
                    pe.wait_ge(q_ready, t + 1)
                    pe.wait_ge(kblk_ready, t + 1)
                    for g, (h0, n) in enumerate(HEAD_GROUPS):
                        need(pe, sub_ready, 3 * (t - 1) + g + 1)
                        dst = bank[g][:, 0:n * M]
                        nc.tensor.matmul(dst, qT[p][:], kblk[p][:, h0:h0 + n, :].rearrange("p h m -> p (h m)"), start=True, stop=False)
                        nc.tensor.matmul(dst.rearrange("p (h m) -> p h m", m=M), ones3[:], neg3[:, bass.ds(t * M, M)].unsqueeze(1).broadcast_to([3, n, M]),
                                         start=False, stop=True).then_inc(s_done, 1)
                if old:
                    pe.wait_ge(o_ready, t - 1)
                    need(pe, aff_ready, t - 2)
                    nc.tensor.transpose(bank[7][:, 0:P], o_sb[p][:], ident).then_inc(oT_done, 1)
                if after:
                    pe.wait_ge(xn_ready, t + 2)
                    need(pe, q_ready, t + 1)
                    nc.tensor.transpose(bank[6][:, 0:P], xn[1 - p][:], ident).then_inc(xnT_done, 1)
                if before:
                    pe.wait_ge(exp_ready, t)
                    p_turn(t - 1, 1 - p, 0)
                    p_turn(t - 1, 1 - p, 1)
                if old:
                    pe.wait_ge(oT_ready, t - 1)
                    nc.tensor.matmul(bank[7][:, P:2 * P], oT[p][:], w0[:, 3, :], start=True, stop=True).then_inc(wo_done, 1)
                if before:
                    p_value(t - 1, 0)
                if after:
                    pe.wait_ge(xnT_ready, t + 2)
                    nc.tensor.matmul(bank[6][:, P:2 * P], w0[:, 0, :], xnT[1 - p][:], start=True, stop=True).then_inc(q_done, 1)
                if before:
                    p_turn(t - 1, 1 - p, 2)
                    p_value(t - 1, 1)
                    p_turn(t - 1, 1 - p, 3)
                    p_value(t - 1, 2)
                    p_value(t - 1, 3)
                if old:
                    pe.wait_ge(xin_ready, t - 1)
                    nc.tensor.transpose(bank[7][:, 2 * P:3 * P], xin[p][:], ident).then_inc(xinT_done, 1)
                    pe.wait_ge(xinT_ready, t - 1)
                    nc.tensor.matmul(bank[7][:, 3 * P:3 * P + E], xinT[p][:], gates[:, 0, :], start=True, stop=True).then_inc(aff_done, 1)
            skewed(pe, -1, MAIN, B + 1, step)
            pe.wait_ge(memset_ready, 10)
            pe.wait_ge(consts2_ready, 4)
            route_tensor(pe, 0)
            pe.wait_ge(pos_ready, 1)
            experts_tensor(pe, 0)
            pe.wait_ge(y_ready, TILES)
            for g in range(NG):
                pe.wait_ge(gx_ready, g + 1)
                for i in range(GROUP):
                    last = nc.tensor.transpose(bank[4 + g][:, i * P:(i + 1) * P], gx[g % 2][:, i, :], ident)
                last.then_inc(gT_done, 1)

            def slot_step(s, g):
                fixed = isinstance(s, int)
                p = g % 2
                now = not fixed or 0 <= s < SLOT_STEPS
                before = not fixed or 0 <= s - 1 < SLOT_STEPS
                after = not fixed or s + 1 < SLOT_STEPS
                g0 = (g - 1) % NG
                cols = lambda i: slice(i * S, (i + 1) * S)
                if before:
                    pe.wait_ge(att_ready, s)
                    nc.tensor.matmul(bank[3][0:M, :], ones_f[0:M + 1, 0:M], att[1 - p][:], start=True, stop=True).then_inc(asum_done, 1)
                if now:
                    pe.wait_ge(diag_ready, s + 1)
                    nc.tensor.matmul(bank[1][:], ones_f[:], diag[p][:].rearrange("p b s -> p (b s)"), start=True, stop=True).then_inc(rb_done, 1)
                if before:
                    h0 = hT[:, g0 * G:(g0 + 1) * G]
                    pe.wait_ge(h_ready, s)
                    if fixed and s == 1:
                        pe.wait_ge(h_ready, NG)
                    need(pe, hnb_ready, s - 1)
                    nc.tensor.matmul(bank[6][:], gru[:, 1, 2 * D:], h0, start=True, stop=True).then_inc(gh_done, 1)
                    need(pe, tz_ready, s - 1)
                    nc.tensor.matmul(bank[4][:], gru[:, 1, 0:D], h0, start=True, stop=False)
                    nc.tensor.matmul(bank[5][:], gru[:, 1, D:2 * D], h0, start=True, stop=False)
                if now:
                    pe.wait_ge(hs_ready, s + 1)
                    for i in range(GROUP):
                        last = nc.tensor.matmul(bank[2][0:M, cols(i)], kq_all[:, g * GROUP + i, :], hs[p][:, cols(i)], start=True, stop=True)
                    last.then_inc(c_done, 1)
                if after:
                    pe.wait_ge(sq_ready, s + 2)
                    for i in range(GROUP):
                        last = nc.tensor.matmul(bank[0][:, i:i + 1], sq[1 - p][:, cols(i)], ones_f[:, 0:1], start=True, stop=True)
                    last.then_inc(ss_done, 1)
                if before:
                    pe.wait_ge(attn_ready, s)
                    need(pe, un_ready, s - 1)
                    for k, bk in enumerate((4, 5, 7)):
                        for i in range(GROUP):
                            last = nc.tensor.matmul(bank[bk][:, cols(i)], vw_all[:, g0 * GROUP + i, k * D:(k + 1) * D], attn[1 - p][:, cols(i)],
                                                    start=bk == 7, stop=bk == 7 or i == GROUP - 1)
                    last.then_inc(gx_done, 1)
            skewed_groups(pe, -1, SLOT_MAIN, SLOT_STEPS, slot_step)

            pe.wait_ge(csub_ready, SLOT_STEPS)
            for g in range(NG):
                pe.wait_ge(h_ready, SLOT_STEPS + g + 1)
                for i in range(GROUP):
                    last = nc.tensor.transpose(bank[g][:, i * P:(i + 1) * P], hT[:, (g * GROUP + i) * S:(g * GROUP + i + 1) * S], ident)
                last.then_inc(hb_done, 1)
            for g in range(NG):
                pe.wait_ge(x3_ready, g + 1)
                for i in range(GROUP):
                    last = nc.tensor.transpose(bank[4 + g][:, i * P:(i + 1) * P], xh_all[:, g * GROUP + i, :], ident)
                last.then_inc(x3T_done, 1)
                pe.wait_ge(x3T_ready, g + 1)
                for i in range(GROUP):
                    last = nc.tensor.matmul(bank[g][:, i * E:(i + 1) * E], x3T[g % 2][:, i * P:(i + 1) * P], gates[:, 1, :], start=True, stop=True)
                last.then_inc(logit_done, 1)
            pe.wait_ge(logit_ready, NG)
            route_tensor(pe, 1)
            pe.wait_ge(pos_ready, 2)
            experts_tensor(pe, 1)


def _shape_constants():
    c = np.zeros((P, C_ALL), np.float32)
    c[:, C_IDENT:C_IDENT + P] = np.eye(P)
    c[:, C_HEAD:C_HEAD + H] = np.arange(P)[:, None] // HD == np.arange(H)[None]
    c[:, C_TIE:C_TIE + B * E] = np.tile(E - np.arange(E), B)[None]
    c[:, C_JOTA:C_JOTA + TILES * E] = np.repeat(np.arange(TILES), E)[None]
    c[:, C_RESET:C_UPPER] = np.tile(np.arange(B) > 0, E)[None]
    c[:, C_UPPER:] = np.arange(P)[:, None] < np.arange(P)[None]
    return c


def kernel(**inputs):
    import concourse.bacc as bacc
    from concourse.bass_utils import run_bass_kernel_spmd

    i = {k: np.asarray(v) for k, v in inputs.items()}
    col = lambda v: v.reshape(-1, P).T
    packed = {
        "consts": _shape_constants(),
        "negp": np.array([[-998244352.0], [-1753088.0], [-2560.0]], np.float32),
        "x": i["x"],
        "ctx": i["ctx_1024"],
        "ctxT": i["ctx_1024"].transpose(0, 2, 1),
        "ctxT_all": i["ctx_1024"].transpose(2, 0, 1).reshape(D, B * M),
        "mask": i["mask_Bx1x1xS2_ik0"].reshape(1, B * M),
        "vecs": np.concatenate([col(i[n]) for n in (
            "L0_xattn_bq", "L0_xattn_bk", "L1_xattn_input_norm_w", "L1_xattn_slot_norm_w", "L1_xattn_gru_bih", "L1_xattn_gru_bhh")], axis=1),
        "rows": np.concatenate([i["L0_xattn_bv"], i["L0_xattn_bo"], i["L1_ffn_bg"]])[None],
        "w0": np.stack([i[f"L0_xattn_W{n}"] for n in "qkvo"], axis=1),
        "w1": np.stack([i[f"L1_xattn_W{n}"] for n in "qkv"], axis=1),
        "gru": np.stack([i["L1_xattn_gru_wih"].T, i["L1_xattn_gru_whh"].T], axis=1),
        "gates": np.stack([i["L0_ffn_centroids"].T, i["L1_ffn_Wg"]], axis=1),
    }
    def experts(w1, w2, b1, extra):
        down = w2.reshape(E, FC, P, D).transpose(0, 2, 1, 3).reshape(E, P, FC * D)
        return np.concatenate([w1, down, b1.reshape(E, FC, P).transpose(0, 2, 1), *[v[:, :, None] for v in extra]], axis=2)
    packed |= {
        "wf0": experts(i["L0_ffn_w1"].transpose(0, 2, 1), i["L0_ffn_w2"].transpose(0, 2, 1), i["L0_ffn_b1"], [i["L0_ffn_ln_g"], i["L0_ffn_ln_b"]]),
        "wf1": experts(i["L1_ffn_W1"], i["L1_ffn_W2"], i["L1_ffn_b1"], [np.zeros((E, D), np.float32)] * 2),
        "b20": i["L0_ffn_b2"],
        "b21": i["L1_ffn_b2"],
    }
    nc = bacc.Bacc("TRN2", target_bir_lowering=False, num_devices=1)
    arrays, handles = {}, {}
    for name, v in packed.items():
        v = np.ascontiguousarray(v)
        arrays[f"in_{name}"] = v
        handles[name] = nc.dram_tensor(f"in_{name}", v.shape, mybir.dt.from_np(v.dtype), kind="ExternalInput").ap()
    out = nc.dram_tensor("out", (B, S, D), F32, kind="ExternalOutput").ap()
    build(nc, handles, out)
    got = run_bass_kernel_spmd(nc, [arrays], core_ids=[0])
    return got.results[0]["out"]
```

```python
from contextlib import ExitStack

import numpy as np

import concourse.bass as bass
from concourse import mybir

F32 = mybir.dt.float32
BF16 = mybir.dt.bfloat16
I32 = mybir.dt.int32
ALU = mybir.AluOpType
ACT = mybir.ActivationFunctionType
X = mybir.AxisListType.X

P = 128
B, S, D = 16, 128, 128
M = 77
H, HD = 16, 8
HV = HD + 1
E, F = 8, 512
FC = F // P
TILES = B * S // P + E - 1
HEAD_GROUPS = ((0, 6), (6, 5), (11, 5))
CHUNKS = -(-H * M // P)
PIECES = [(c, h, max(c * P - h * M, 0), max(h * M - c * P, 0), min((h + 1) * M, (c + 1) * P) - max(h * M, c * P))
          for c in range(CHUNKS) for h in range(c * P // M, min(((c + 1) * P - 1) // M + 1, H))]
CHUNK_ROWS = [min(P, H * M - c * P) for c in range(CHUNKS)]
CHUNK_PIECES = [[i for i, piece in enumerate(PIECES) if piece[0] == c] for c in range(CHUNKS)]
TURNS = ((0, 4), (4, 8), (8, CHUNKS))
NT = len(TURNS)
LN_EPS, RMS_EPS, ATT_EPS = 1e-5, 1e-6, 1e-6
NEG = -1e9
GATES = 3 * D

C_IDENT, C_HEAD, C_TIE, C_JOTA = 0, 128, 144, 272
C_RESET = C_JOTA + TILES * E
C_UPPER = C_RESET + E * B
C_ALL = C_UPPER + P
V_BQ, V_BK, V_WIN, V_WSLOT, V_BIH, V_BHH = 0, 1, 2, 3, 4, 7
V_ALL = 10
W_ALL = 2 * F
EB = F + D
BIAS_ROWS = E * EB // P
GROUP = 4
G = GROUP * S
NG = B // GROUP
ITERS = 3
ROUTE_LINKS = 20
SLOT_STEPS = ITERS * NG
R_BV, R_BO, R_BG = 0, 128, 256
R_ALL = 264


def need(eng, sem, count):
    if not (isinstance(count, int) and count <= 0):
        eng.wait_ge(sem, count)


def skewed(eng, first, main, last, step):
    lo, hi = main
    for t in range(first, lo):
        step(t, t % 2)
    with eng.Fori(0, (hi - lo) // 2) as i:
        for k in range(2):
            step(i * 2 + (lo + k), (lo + k) % 2)
    for t in range(hi, last + 1):
        step(t, t % 2)


def skewed_groups(eng, first, main, last, step):
    lo, hi = main
    for s in range(first, lo):
        step(s, s % NG)
    with eng.Fori(0, (hi - lo) // NG) as i:
        for k in range(NG):
            step(i * NG + (lo + k), (lo + k) % NG)
    for s in range(hi, last + 1):
        step(s, s % NG)


def build(nc, a, out):
    with ExitStack() as ctx:
        def sb(name, shape, dt=F32):
            return ctx.enter_context(nc.sbuf_tensor(name, shape, dt))

        first = ExitStack()
        second = ExitStack()

        def sb1(name, shape, dt=F32):
            return first.enter_context(nc.sbuf_tensor(name, shape, dt))

        def sb2(name, shape, dt=F32):
            return second.enter_context(nc.sbuf_tensor(name, shape, dt))

        def sem(name):
            return ctx.enter_context(nc.semaphore(name))

        bank = [ctx.enter_context(nc.psum_tensor(f"bank{i}", [P, 512], F32)) for i in range(8)]

        consts = sb("consts", [P, C_ALL])
        vecs = sb("vecs", [P, V_ALL])
        rows = sb("rows", [P, R_ALL])
        w1 = sb("w1", [P, 3, D])
        gru = sb("gru", [P, 2, GATES])
        gates = sb("gates", [P, 2, E])
        negp = sb("negp", [3, 1])
        ones3 = sb("ones3", [3, P], BF16)
        ab = sb("ab", [P, D + GATES])
        vw_all = sb("vw_all", [M, B, GATES])
        kq_all = sb("kq_all", [P, B, M])
        ctxT_all = sb("ctxT_all", [P, B * M])
        ctx_n = sb("ctx_n", [P, B * M])
        wslot = sb("wslot", [P, 1])
        bq = sb("bq", [P, 1])
        eps_ln = sb("eps_ln", [P, 1])
        hold = sb("hold", [1, 3])
        eps_rms = sb("eps_rms", [P, 1])
        ident = consts[:, C_IDENT:C_IDENT + P]
        headmask = consts[:, C_HEAD:C_HEAD + H]

        def pair(name, shape, dt=F32):
            return [sb(f"{name}{i}", shape, dt) for i in range(2)]

        xh_all = sb("xh_all", [P, B, D])
        res_all = sb("res_all", [P, B, D])
        aff_all = sb("aff_all", [P, B, E])

        upper = sb("upper", [P, P], BF16)
        ones_b = sb("ones_b", [P, P], BF16)
        ones_e = sb("ones_e", [P, E])
        amax = sb("amax", [P, B])
        apick = sb("apick", [P, B, E])
        onehot = sb("onehot", [P, B, E], BF16)
        tot = sb("tot", [P, E, B])
        cum = sb("cum", [P, E * B])
        n_pad = sb("n_pad", [P, E], I32)
        n_tile_i = sb("n_tile_i", [P, E], I32)
        n_tile = sb("n_tile", [P, E])
        tile_end = sb("tile_end", [P, E])
        base = sb("base", [P, E])
        pos_be = sb("pos_be", [P, B, E])
        pos_f = sb("pos_f", [P, B])
        pos = sb("pos", [P, B], I32)
        tile_cmp = sb("tile_cmp", [P, TILES, E])
        tile_e = sb("tile_e", [P, TILES])
        tile_tab = sb("tile_tab", [P, TILES], I32)
        share = sb("share", [P, B])
        eg = sb("eg", [P, B, E])
        zero = sb("zero", [P, D])
        weights = sb("weights", [P, E, W_ALL])
        ln_gb = sb("ln_gb", [P, 2, E, D])
        ctxn = pair("ctxn", [P, M])
        bias_in = sb("bias_in", [BIAS_ROWS, 2, P])
        bias_left = sb("bias_left", [BIAS_ROWS, 2, P])
        bias_part = sb("bias_part", [BIAS_ROWS, 2, 3, P], BF16)
        bias3 = sb("bias3", [3, E * EB], BF16)
        att = pair("att", [M + 1, G])
        ones_f = sb("ones_f", [P, P])
        brz = sb("brz", [P, 2])
        bhn = sb("bhn", [P, 1])

        def pair1(name, shape, dt=F32):
            return [sb1(f"{name}{i}", shape, dt) for i in range(2)]
        x_all = sb1("x_all", [P, B, D])
        v_all = sb1("v_all", [M, H, B, HV])
        v_rows = sb1("v_rows", [P, len(PIECES), B, HV])
        zero3 = sb1("zero3", [3, H * HV], BF16)
        w0 = sb1("w0", [P, 4, D])
        mask_i = xh_all[:].rearrange("p b d -> p (b d)")[:, 0:B * M].bitcast(I32)
        mask_f = res_all[:].rearrange("p b d -> p (b d)")[:, 0:B * M]
        neg3 = sb1("neg3", [3, B * M], BF16)
        kT_all = sb1("kT_all", [P, B * M])
        ctxT = pair1("ctxT", [P, M])
        st = pair1("st", [P, 6])
        mv = pair1("mv", [P, 2])
        lnv = pair1("lnv", [P, 1])
        rstd = pair1("rstd", [P, 1])
        xn = pair1("xn", [P, D])
        xnT = pair1("xnT", [P, S])
        qT = pair1("qT", [P, S])
        xbo = pair1("xbo", [P, D])
        kblk = pair1("kblk", [P, H, M])
        smax = pair1("smax", [P, H])
        probs = pair1("probs", [P, H, M])
        pT = pair1("pT", [P, 4, S])
        rden = pair1("rden", [P, H])
        o_sb = pair1("o_sb", [P, D])
        oT = pair1("oT", [P, S])
        x1 = pair1("x1", [P, D])
        st1 = pair1("st1", [P, 6])
        mv1 = pair1("mv1", [P, 2])
        lnv1 = pair1("lnv1", [P, 1])
        rstd1 = pair1("rstd1", [P, 1])
        xin = pair1("xin", [P, D])
        st2 = pair1("st2", [P, 6])
        mv2 = pair1("mv2", [P, 2])
        lnv2 = pair1("lnv2", [P, 1])
        rstd2 = pair1("rstd2", [P, 1])
        xinT = pair1("xinT", [P, S])
        first.close()

        f_all = sb("f_all", [P, B, D])
        x2_all = sb("x2_all", [P, B, D])
        tile_rows = sb2("tile_rows", [P, TILES, D])
        xt, xtT, hid, hidT = ([sb2(f"{n}{i}", shape) for i in range(2)] for n, shape in (("xt", [P, D]), ("xtT", [P, P]), ("hid", [P, F]), ("hidT", [P, FC, P])))
        second.close()
        xs_dram = [nc.dram_tensor(f"xs{l}", (TILES * P, D), F32, kind="Internal").ap() for l in range(2)]
        ys_dram = [nc.dram_tensor(f"ys{l}", (TILES * P, D), F32, kind="Internal").ap() for l in range(2)]

        gst = sb("gst", [P, GROUP, 6])
        gmv = sb("gmv", [P, GROUP, 2])
        gln = sb("gln", [P, GROUP])
        gr = sb("gr", [P, GROUP])
        gx = pair("gx", [P, GROUP, D])
        hT = sb("hT", [P, B * S])
        sq = pair("sq", [P, G])
        rln = pair("rln", [P, G])
        hs = pair("hs", [P, G])
        cmax = pair("cmax", [M, GROUP])
        ex = pair("ex", [M, GROUP, S])
        csum = pair("csum", [M, GROUP])
        crec = pair("crec", [M, GROUP])
        aln = pair("aln", [M, G])
        attn = pair("attn", [M, G])
        tr = pair("tr", [P, G])
        tz = pair("tz", [P, G])
        hnb = pair("hnb", [P, G])
        u = pair("u", [P, G])
        nn = pair("nn", [P, G])
        dd = pair("dd", [P, G])
        x3T = tr

        ld_const, ld_rows, ld_x, ld_ctx, ld_w1 = sem("ld_const"), sem("ld_rows"), sem("ld_x"), sem("ld_ctx"), sem("ld_w1")
        memset_ready = sem("memset_ready")
        mask_ready, neg_ready, kproj, kT_ready, kT_mask = (sem(n) for n in ("mask_ready", "neg_ready", "kproj", "kT_ready", "kT_mask"))
        small_ready, abproj, ab_ready = sem("small_ready"), sem("abproj"), sem("ab_ready")
        ctxsq_ready, ctxss_done, ctxln_ready, ctxr_ready, ctxn_ready, kq_done = (sem(n) for n in ("ctxsq_ready", "ctxss_done", "ctxln_ready", "ctxr_ready", "ctxn_ready", "kq_done"))
        ctx_copied, v_done, v_ready, rows_cleared, v_placed, ctxn_copied, vw_done, vw_ready, kq_ready = (
            sem(n) for n in ("ctx_copied", "v_done", "v_ready", "rows_cleared", "v_placed", "ctxn_copied", "vw_done", "vw_ready", "kq_ready"))
        lnx_st, lnx_mv, lnx_ln, lnx_r, xn_ready = (sem(n) for n in ("lnx_st", "lnx_mv", "lnx_ln", "lnx_r", "xn_ready"))
        xbo_ready, kblk_ready = sem("xbo_ready"), sem("kblk_ready")
        xnT_done, xnT_ready, q_done, q_ready = (sem(n) for n in ("xnT_done", "xnT_ready", "q_done", "q_ready"))
        s_done, max_ready, sub_ready, exp_ready = (sem(n) for n in ("s_done", "max_ready", "sub_ready", "exp_ready"))
        pT_done, pT_ready, pv_done = sem("pT_done"), sem("pT_ready"), sem("pv_done")
        rden_ready, o_ready, oT_done, oT_ready, wo_done = (sem(n) for n in ("rden_ready", "o_ready", "oT_done", "oT_ready", "wo_done"))
        x1_ready, st1_ready, mv1_ready, ln1_ready, r1_ready, xin_ready = (sem(n) for n in ("x1_ready", "st1_ready", "mv1_ready", "ln1_ready", "r1_ready", "xin_ready"))
        st2_ready, mv2_ready, ln2_ready, r2_ready, xh_ready = (sem(n) for n in ("st2_ready", "mv2_ready", "ln2_ready", "r2_ready", "xh_ready"))
        res_ready, xinT_done, xinT_ready, aff_done, aff_ready = (sem(n) for n in ("res_ready", "xinT_done", "xinT_ready", "aff_done", "aff_ready"))
        stored = sem("stored")
        consts2_ready, zeroed = sem("consts2_ready"), sem("zeroed")

        class Layer:
            def __init__(self, l):
                self.chain0, self.one0, self.tile0 = ROUTE_LINKS * l, l, TILES * l
                self.scatter0, self.gather0 = 16 * B * l, 16 * GROUP * l
        layers = [Layer(0), Layer(1)]
        (chain, onehot_ready, rank_done, total_done, pos_ready, tab_ready, share_in, share_exp, share_ready,
         scattered, xtT_done, xtT_ready, up_done, hid_ready, hidT_done, hidT_ready, down_done, y_ready) = (sem(n) for n in (
             "chain", "onehot_ready", "rank_done", "total_done", "pos_ready", "tab_ready", "share_in", "share_exp", "share_ready",
             "scattered", "xtT_done", "xtT_ready", "up_done", "hid_ready", "hidT_done", "hidT_ready", "down_done", "y_ready"))
        tiles_early, tiles_late, xg_ready, xt_ready, y_stored, weights_loaded = sem("tiles_early"), sem("tiles_late"), sem("xg_ready"), sem("xt_ready"), sem("y_stored"), sem("weights_loaded")
        ld_bias, bias_split, bias_chain, bias_loaded = (sem(n) for n in ("ld_bias", "bias_split", "bias_chain", "bias_loaded"))
        gathered = [sem(f"gathered{g}") for g in range(NG)]
        x2_chain, gmv_ready, gln_ready, gr_ready, gx_ready, gT_done = (sem(n) for n in ("x2_chain", "gmv_ready", "gln_ready", "gr_ready", "gx_ready", "gT_done"))
        h_ready, sq_ready, ss_done, rln_ready, rs_ready, hs_ready = (
            sem(n) for n in ("h_ready", "sq_ready", "ss_done", "rln_ready", "rs_ready", "hs_ready"))
        c_done, cmax_ready, csub_ready, cexp_ready, crec_ready, att_ready = (
            sem(n) for n in ("c_done", "cmax_ready", "csub_ready", "cexp_ready", "crec_ready", "att_ready"))
        asum_done, aln_ready, ar_ready, attn_ready, gh_done, gx_done = (sem(n) for n in ("asum_done", "aln_ready", "ar_ready", "attn_ready", "gh_done", "gx_done"))
        hnb_ready, tr_ready, tz_ready, u_ready, un_ready, nn_ready, dd_ready, e_ready = (
            sem(n) for n in ("hnb_ready", "tr_ready", "tz_ready", "u_ready", "un_ready", "nn_ready", "dd_ready", "e_ready"))
        hb_done, x3_chain, gmv3_ready, gln3_ready, gr3_ready, x3_ready, x3T_done, x3T_ready, logit_done, logit_ready = (
            sem(n) for n in ("hb_done", "x3_chain", "gmv3_ready", "gln3_ready", "gr3_ready", "x3_ready", "x3T_done", "x3T_ready", "logit_done", "logit_ready"))
        fin_chain, fin_ready = sem("fin_chain"), sem("fin_ready")

        def route_vector(dve, l):
            L = layers[l]
            count = [0]

            def link(ins):
                count[0] += 1
                ins.then_inc(chain, 1)
                dve.wait_ge(chain, L.chain0 + count[0])
            link(nc.vector.tensor_reduce(amax[:], aff_all[:], X, ALU.max))
            peak = amax[:].unsqueeze(2).broadcast_to([P, B, E])
            if l == 0:
                nc.vector.tensor_scalar(share[:], amax[:], -1.0, None, ALU.mult).then_inc(share_in, 1)
            else:
                nc.vector.tensor_tensor(eg[:], aff_all[:], peak, ALU.subtract).then_inc(share_in, 1)
            link(nc.vector.tensor_tensor(apick[:], aff_all[:], peak, ALU.is_ge))
            link(nc.vector.tensor_tensor(apick[:], apick[:], consts[:, C_TIE:C_TIE + B * E].rearrange("p (b e) -> p b e", e=E), ALU.mult))
            link(nc.vector.tensor_reduce(amax[:], apick[:], X, ALU.max))
            nc.vector.tensor_tensor(onehot[:], apick[:], peak, ALU.is_equal).then_inc(onehot_ready, 1)
            dve.wait_ge(total_done, L.one0 + 1)
            link(nc.vector.tensor_copy(tot[:], bank[1][:, 0:B * E].rearrange("p (b e) -> p e b", e=E)))
            link(nc.vector.tensor_tensor_scan(cum[:], consts[:, C_RESET:C_RESET + E * B], tot[:].rearrange("p e b -> p (e b)"), 0.0, ALU.mult, ALU.add))
            cum_v = cum[:].rearrange("p (e b) -> p e b", b=B)
            link(nc.vector.tensor_scalar(n_pad[:], cum_v[:, :, B - 1:B].rearrange("p e b -> p (e b)"), P - 1.0, None, ALU.add))
            link(nc.vector.tensor_scalar(n_tile_i[:], n_pad[:], 7, None, ALU.arith_shift_right))
            link(nc.vector.tensor_copy(n_tile[:], n_tile_i[:]))
            link(nc.vector.tensor_tensor_scan(tile_end[:], ones_e[:], n_tile[:], 0.0, ALU.mult, ALU.add))
            link(nc.vector.tensor_tensor(tile_cmp[:], tile_end[:].unsqueeze(1).broadcast_to([P, TILES, E]),
                                         consts[:, C_JOTA:C_JOTA + TILES * E].rearrange("p (j e) -> p j e", e=E), ALU.is_le))
            link(nc.vector.tensor_reduce(tile_e[:], tile_cmp[:], X, ALU.add))
            nc.vector.tensor_scalar(tile_tab[:], tile_e[:], E - 1.0, None, ALU.min).then_inc(tab_ready, 1)
            link(nc.vector.scalar_tensor_tensor(base[:], n_tile[:], -1.0, tile_end[:], ALU.mult, ALU.add))
            link(nc.vector.tensor_scalar(base[:], base[:], float(P), None, ALU.mult))
            link(nc.vector.tensor_tensor(cum[:], cum[:], tot[:].rearrange("p e b -> p (e b)"), ALU.subtract))
            link(nc.vector.tensor_tensor(cum_v, cum_v, base[:].unsqueeze(2).broadcast_to([P, E, B]), ALU.add))
            dve.wait_ge(rank_done, L.one0 + 1)
            link(nc.vector.tensor_tensor(pos_be[:], bank[0][:, 0:B * E].rearrange("p (b e) -> p b e", e=E), cum[:].rearrange("p (e b) -> p b e", b=B), ALU.add))
            link(nc.vector.tensor_tensor(pos_be[:], pos_be[:], onehot[:], ALU.mult))
            link(nc.vector.tensor_reduce(pos_f[:], pos_be[:], X, ALU.add))
            nc.vector.tensor_copy(pos[:], pos_f[:]).then_inc(pos_ready, 1)
            dve.wait_ge(share_exp, L.one0 + 1)
            if l == 0:
                link(nc.vector.tensor_scalar(share[:], share[:], 1.0, None, ALU.add))
            else:
                link(nc.vector.tensor_reduce(share[:], eg[:], X, ALU.add))
            nc.vector.reciprocal(share[:], share[:]).then_inc(share_ready, 1)
            assert count[0] == ROUTE_LINKS

        def route_tensor(pe, l):
            L = layers[l]
            pe.wait_ge(onehot_ready, L.one0 + 1)
            flat = onehot[:].rearrange("p b e -> p (b e)")
            nc.tensor.matmul(bank[1][:, 0:B * E], ones_b[:], flat, start=True, stop=True).then_inc(total_done, 1)
            nc.tensor.matmul(bank[0][:, 0:B * E], upper[:], flat, start=True, stop=True).then_inc(rank_done, 1)

        def route_scalar(act, l):
            L = layers[l]
            act.wait_ge(share_in, L.one0 + 1)
            t = share if l == 0 else eg
            nc.scalar.activation(t[:], t[:], ACT.Exp).then_inc(share_exp, 1)

        def scatter(pool, l):
            L = layers[l]
            pool.wait_ge(pos_ready, L.one0 + 1)
            pool.wait_ge(zeroed, 32)
            for b in range(B):
                nc.gpsimd.indirect_dma_start(xs_dram[l], bass.IndirectOffsetOnAxis(pos[:, b:b + 1], 0), xh_all[:, b, :], None).then_inc(scattered, 16)

        def gather(pool, l):
            L = layers[l]
            pool.wait_ge(y_stored, 16 * len(STORES) * (l + 1))
            for b in range(B):
                nc.gpsimd.indirect_dma_start(f_all[:, b, :], None, ys_dram[l], bass.IndirectOffsetOnAxis(pos[:, b:b + 1], 0)).then_inc(gathered[b // GROUP], 16)

        EARLY = 8
        STORES = ((0, 8), (8, 16), (16, 20), (20, TILES))

        def span(dram, lo, hi):
            return dram[lo * P:hi * P, :].rearrange("(j p) d -> p j d", p=P)

        def load_experts(sp, l):
            if l:
                sp.wait_ge(down_done, TILES)
            for half in range(2):
                lo, hi = half * E // 2, (half + 1) * E // 2
                sp.dma_start(weights[:, lo:hi, :], a[f"wf{l}"][:, lo:hi, :]).then_inc(weights_loaded, 16)
            sp.wait_ge(bias_split, 3)
            for k in range(3):
                sp.dma_start(bias3[k:k + 1, :], bias_part[:, l, k, :]).then_inc(bias_loaded, 16)

        def experts_sync(sp, l):
            L = layers[l]
            sp.wait_ge(scattered, L.scatter0 + 16 * B)
            sp.dma_start(tile_rows[:, 0:EARLY, :], span(xs_dram[l], 0, EARLY)).then_inc(tiles_early, 16)
            sp.dma_start(tile_rows[:, EARLY:, :], span(xs_dram[l], EARLY, TILES)).then_inc(tiles_late, 16)
            for lo, hi in STORES:
                sp.wait_ge(y_ready, L.tile0 + hi)
                sp.dma_start(span(ys_dram[l], lo, hi), tile_rows[:, lo:hi, :]).then_inc(y_stored, 16)

        def expert_of(eng, j):
            return eng.value_load(tile_tab[0:1, bass.ds(j, 1)], min_val=0, max_val=E - 1)

        def experts_tensor(pe, l):
            L = layers[l]

            def rows_turn(j, p):
                pe.wait_ge(xt_ready, L.tile0 + (j + 1))
                nc.tensor.transpose(bank[p][:, 0:P], xt[p][:], ident).then_inc(xtT_done, 1)

            def step(j, p):
                fixed = isinstance(j, int)
                if not fixed or j < TILES:
                    e = expert_of(pe, j)
                    pe.wait_ge(xtT_ready, L.tile0 + (j + 1))
                    nc.tensor.matmul(bank[2 + p][:], ones3[:], bias3[:, bass.ds(e * EB, F)], start=True, stop=False)
                    nc.tensor.matmul(bank[2 + p][:], xtT[p][:], weights[:, bass.ds(e, 1), 0:F].rearrange("p o f -> p (o f)"),
                                     start=False, stop=True).then_inc(up_done, 1)
                if not fixed or j + 1 < TILES:
                    rows_turn(j + 1, 1 - p)
                if not fixed or j >= 1:
                    e = expert_of(pe, j - 1)
                    y = bank[6 + 1 - p][:, 0:D]
                    pe.wait_ge(hidT_ready, L.tile0 + j)
                    need(pe, y_ready, L.tile0 + (j - 2))
                    nc.tensor.matmul(y, ones3[:], bias3[:, bass.ds(e * EB + F, D)], start=True, stop=False)
                    for c in range(FC):
                        last = nc.tensor.matmul(y, hidT[1 - p][:, c, :],
                                                weights[:, bass.ds(e, 1), F + c * D:F + (c + 1) * D].rearrange("p o f -> p (o f)"),
                                                start=False, stop=c == FC - 1)
                    last.then_inc(down_done, 1)
                if not fixed or j < TILES:
                    pe.wait_ge(hid_ready, L.tile0 + (j + 1))
                    for c in range(FC):
                        last = nc.tensor.transpose(bank[4 + p][:, c * P:(c + 1) * P], hid[p][:, c * P:(c + 1) * P], ident)
                    last.then_inc(hidT_done, 1)
            pe.wait_ge(weights_loaded, 32 * (l + 1))
            pe.wait_ge(bias_loaded, 48 * (l + 1))
            rows_turn(0, 0)
            skewed(pe, 0, (2, 22), TILES, step)

        def experts_gpsimd(pool, l):
            L = layers[l]

            def step(j, p):
                need(pool, xtT_done, L.tile0 + (j - 1))
                src = tile_rows[:, bass.ds(j, 1), :].rearrange("p o d -> p (o d)")
                if l == 0:
                    e = expert_of(pool, j)
                    nc.gpsimd.tensor_tensor(xt[p][:], src, ln_gb[:, 0, bass.ds(e, 1), :].rearrange("p o d -> p (o d)"), ALU.mult).then_inc(xg_ready, 1)
                    pool.wait_ge(xg_ready, j + 1)
                    nc.gpsimd.tensor_tensor(xt[p][:], xt[p][:], ln_gb[:, 1, bass.ds(e, 1), :].rearrange("p o d -> p (o d)"), ALU.add).then_inc(xt_ready, 1)
                else:
                    nc.gpsimd.tensor_copy(xt[p][:], src).then_inc(xt_ready, 1)
            if l == 0:
                pool.wait_ge(ld_bias, 32)
            pool.wait_ge(tiles_early, 16 * (l + 1))
            skewed(pool, 0, (2, EARLY), EARLY - 1, step)
            pool.wait_ge(tiles_late, 16 * (l + 1))
            skewed(pool, EARLY, (EARLY, 22), TILES - 1, step)

        def experts_scalar(act, l):
            L = layers[l]

            def step(j, p):
                act.wait_ge(up_done, L.tile0 + (j + 1))
                nc.scalar.activation(hid[p][:], bank[2 + p][:], ACT.Silu if l else ACT.Relu).then_inc(hid_ready, 1)
            skewed(act, 0, (2, 22), TILES - 1, step)

        def experts_vector(dve, l):
            L = layers[l]

            def rows_turned(j, p):
                dve.wait_ge(xtT_done, L.tile0 + (j + 1))
                nc.vector.tensor_copy(xtT[p][:], bank[p][:, 0:P]).then_inc(xtT_ready, 1)

            def step(j, p):
                fixed = isinstance(j, int)
                if not fixed or j + 1 < TILES:
                    rows_turned(j + 1, 1 - p)
                if not fixed or j >= 1:
                    dve.wait_ge(down_done, L.tile0 + j)
                    nc.vector.tensor_copy(tile_rows[:, bass.ds(j - 1, 1), :].rearrange("p o d -> p (o d)"), bank[6 + 1 - p][:, 0:D]).then_inc(y_ready, 1)
                if not fixed or j < TILES:
                    dve.wait_ge(hidT_done, L.tile0 + (j + 1))
                    nc.vector.tensor_copy(hidT[p][:].rearrange("p c t -> p (c t)"), bank[4 + p][:]).then_inc(hidT_ready, 1)
            rows_turned(0, 0)
            skewed(dve, 0, (2, 22), TILES, step)

        SLOT_MAIN = (2, 10)

        MAIN = (4, 12)
        block = ctx.enter_context(nc.Block())

        @block.sync
        def _(sp):
            sp.dma_start(ctxT_all[:], a["ctxT_all"]).then_inc(ld_const, 16)
            sp.dma_start(w0[:], a["w0"]).then_inc(ld_const, 16)
            sp.dma_start(vecs[:], a["vecs"]).then_inc(ld_const, 16)
            sp.dma_start(consts[:], a["consts"]).then_inc(ld_const, 16)
            sp.dma_start(x_all[:, 0:4, :], a["x"][0:4].rearrange("b s d -> s b d")).then_inc(ld_x, 16)
            sp.dma_start(x_all[:, 4:B, :], a["x"][4:B].rearrange("b s d -> s b d")).then_inc(ld_x, 16)
            sp.dma_start(gates[:], a["gates"]).then_inc(ld_w1, 16)
            sp.dma_start(w1[:], a["w1"]).then_inc(ld_w1, 16)
            sp.dma_start(gru[:], a["gru"]).then_inc(ld_w1, 16)
            sp.wait_ge(v_ready, B)
            sp.wait_ge(rows_cleared, 1)
            for i, (c, h, key, row, n) in enumerate(PIECES):
                sp.dma_start(v_rows[row:row + n, i, :, :], v_all[key:key + n, h, :, :]).then_inc(v_placed, 16)
            sp.wait_ge(memset_ready, 9)
            for l in range(2):
                sp.dma_start(xs_dram[l].rearrange("(j p) d -> p j d", p=P), zero[:].unsqueeze(1).broadcast_to([P, TILES, D])).then_inc(zeroed, 16)
            load_experts(sp, 0)
            experts_sync(sp, 0)
            load_experts(sp, 1)
            experts_sync(sp, 1)
            for g in range(NG):
                sp.wait_ge(fin_ready, g + 1)
                sp.dma_start(out[g * GROUP:(g + 1) * GROUP].rearrange("b s d -> s b d"), f_all[:, g * GROUP:(g + 1) * GROUP, :]).then_inc(stored, 16)
            sp.wait_ge(stored, 16 * NG)

        @block.gpsimd
        def _(pool):
            nc.gpsimd.memset(v_all[:], 1.0).then_inc(memset_ready, 1)
            nc.gpsimd.memset(zero3[:], 0.0)
            nc.gpsimd.memset(ones3[:], 1.0).then_inc(memset_ready, 1)
            nc.gpsimd.memset(eps_ln[:], LN_EPS).then_inc(memset_ready, 1)
            nc.gpsimd.memset(eps_rms[:], RMS_EPS).then_inc(memset_ready, 1)
            nc.gpsimd.memset(ones_b[:], 1.0).then_inc(memset_ready, 1)
            nc.gpsimd.memset(ones_f[:], 1.0).then_inc(memset_ready, 1)
            nc.gpsimd.memset(ones_e[:], 1.0).then_inc(memset_ready, 1)
            nc.gpsimd.memset(zero[:], 0.0).then_inc(memset_ready, 1)
            nc.gpsimd.memset(att[0][:], ATT_EPS)
            nc.gpsimd.memset(att[1][:], ATT_EPS).then_inc(memset_ready, 1)
            nc.gpsimd.memset(v_rows[:], 0.0).then_inc(rows_cleared, 1)
            pool.wait_ge(ld_const, 64)

            def context(b, p):
                need(pool, v_done, b - 1)
                nc.gpsimd.tensor_copy(ctxT[p][:], ctxT_all[:, bass.ds(b * M, M)]).then_inc(ctx_copied, 1)
            skewed(pool, 0, (2, B), B - 1, context)
            pool.wait_ge(kT_ready, 3)
            pool.wait_ge(ld_rows, 32)
            pool.wait_ge(ld_x, 32)

            def step(b, p):
                need(pool, s_done, 3 * (b - 1))
                nc.gpsimd.tensor_tensor(
                    kblk[p][:], kT_all[:, bass.ds(b * M, M)].unsqueeze(1).broadcast_to([P, H, M]),
                    headmask.unsqueeze(2).broadcast_to([P, H, M]), ALU.mult).then_inc(kblk_ready, 1)

            def with_bias(b, p):
                need(pool, x1_ready, b - 1)
                nc.gpsimd.tensor_tensor(xbo[p][:], x_all[:, bass.ds(b, 1), :].rearrange("p o d -> p (o d)"), rows[:, R_BO:R_BO + D], ALU.add).then_inc(xbo_ready, 1)

            def residual(b, p):
                pool.wait_ge(xin_ready, b + 1)
                nc.gpsimd.tensor_tensor(res_all[:, bass.ds(b, 1), :].rearrange("p o d -> p (o d)"), x1[p][:], xin[p][:], ALU.add).then_inc(res_ready, 1)

            def both(t, p):
                if not isinstance(t, int) or t + 1 < B:
                    step(t + 1, 1 - p)
                if not isinstance(t, int) or 0 <= t - 3 < B:
                    residual(t - 3, 1 - p)
                if not isinstance(t, int) or 0 <= t - 1 < B:
                    with_bias(t - 1, 1 - p)
            skewed(pool, -1, MAIN, B + 2, both)
            nc.gpsimd.tensor_tensor(ctx_n[:], ctxT_all[:], ctxT_all[:], ALU.mult).then_inc(ctxsq_ready, 1)
            scatter(pool, 0)
            experts_gpsimd(pool, 0)
            gather(pool, 0)

            def slot_step(s, g):
                fixed = isinstance(s, int)
                p = g % 2
                if not fixed or s + 1 < SLOT_STEPS:
                    g1 = (g + 1) % NG
                    pool.wait_ge(h_ready, s + 2)
                    need(pool, ss_done, s)
                    nc.gpsimd.tensor_tensor(sq[1 - p][:], hT[:, g1 * G:(g1 + 1) * G], hT[:, g1 * G:(g1 + 1) * G], ALU.mult).then_inc(sq_ready, 1)
                if not fixed or 0 <= s - 1:
                    g0 = (g - 1) % NG
                    pool.wait_ge(nn_ready, s)
                    nc.gpsimd.tensor_tensor(dd[1 - p][:], hT[:, g0 * G:(g0 + 1) * G], nn[1 - p][:], ALU.subtract).then_inc(dd_ready, 1)
            skewed_groups(pool, -1, SLOT_MAIN, SLOT_STEPS, slot_step)
            pool.wait_ge(x3_ready, NG)
            scatter(pool, 1)
            experts_gpsimd(pool, 1)
            gather(pool, 1)

        @block.scalar
        def _(act):
            act.dma_start(mask_i, a["mask"].partition_broadcast(P)).then_inc(ld_ctx, 16)
            act.dma_start(rows[:], a["rows"].partition_broadcast(P)).then_inc(ld_rows, 16)
            act.dma_start(negp[:], a["negp"]).then_inc(ld_rows, 16)
            act.dma_start(bias_in[:], a["biases"]).then_inc(ld_bias, 16)
            act.dma_start(ln_gb[:], a["ln_gb"].partition_broadcast(P)).then_inc(ld_bias, 16)
            act.preload_act_table_set("natural_log_exp_and_others")
            act.wait_ge(memset_ready, 9)
            def rstd_of(b, mv_ready, mvt, ln_t, ln_sem, r_t, r_sem):
                act.wait_ge(mv_ready, b + 1)
                nc.scalar.activation(ln_t[:], mvt[:, 1:2], ACT.Ln, bias=eps_ln[:]).then_inc(ln_sem, 1)
                act.wait_ge(ln_sem, b + 1)
                nc.scalar.activation(r_t[:], ln_t[:], ACT.Exp, scale=-0.5).then_inc(r_sem, 1)

            def step(t, p):
                fixed = isinstance(t, int)
                before = not fixed or 0 <= t - 1 < B

                def turned(q):
                    n = (t - 1) * NT + q
                    slot, (lo, hi) = (1 - p + q) % 2, TURNS[q]
                    act.wait_ge(pT_done, n + 1)
                    need(act, pv_done, n - 1)
                    rows_q = CHUNK_ROWS[hi - 1]
                    if rows_q < P:
                        nc.scalar.copy(pT[slot][0:rows_q, hi - 1 - lo, :], bank[3 + slot][0:rows_q, (hi - 1 - lo) * S:(hi - lo) * S])
                        hi -= 1
                    nc.scalar.copy(pT[slot][:, 0:hi - lo, :], bank[3 + slot][:, 0:(hi - lo) * S].rearrange("p (i s) -> p i s", s=S)).then_inc(pT_ready, 1)

                def exponents(g):
                    h0, n = HEAD_GROUPS[g]
                    act.wait_ge(sub_ready, 3 * t + g + 1)
                    nc.scalar.activation(probs[p][:, h0:h0 + n, :], probs[p][:, h0:h0 + n, :], ACT.Exp).then_inc(exp_ready, 1)

                if not fixed or 0 <= t + 1 < B:
                    act.wait_ge(xnT_done, t + 2)
                    nc.scalar.copy(xnT[1 - p][:], bank[6][:, 0:P]).then_inc(xnT_ready, 1)
                if before:
                    turned(0)
                if not fixed or 0 <= t - 4:
                    act.wait_ge(xinT_done, t - 3)
                    nc.scalar.copy(xinT[p][:], bank[7][:, 2 * P:3 * P]).then_inc(xinT_ready, 1)
                if before:
                    turned(1)
                if not fixed or 0 <= t < B:
                    exponents(0)
                if not fixed or 0 <= t - 4:
                    act.wait_ge(aff_done, t - 3)
                    nc.scalar.copy(aff_all[:, bass.ds(t - 4, 1), :].rearrange("p o e -> p (o e)"), bank[7][:, 3 * P:3 * P + E]).then_inc(aff_ready, 1)
                if not fixed or 0 <= t + 1 < B:
                    act.wait_ge(q_done, t + 2)
                    need(act, s_done, 3 * t)
                    nc.scalar.activation(qT[1 - p][:], bank[6][:, P:2 * P], ACT.Identity, scale=HD ** -0.5, bias=bq[:]).then_inc(q_ready, 1)
                if not fixed or 0 <= t < B:
                    exponents(1)
                if not fixed or 0 <= t - 2 < B:
                    act.wait_ge(oT_done, t - 1)
                    nc.scalar.copy(oT[p][:], bank[7][:, 0:P]).then_inc(oT_ready, 1)
                if before:
                    turned(2)
                if not fixed or 0 <= t < B:
                    exponents(2)
                if not fixed or 0 <= t - 2 < B:
                    rstd_of(t - 2, mv1_ready, mv1[p], lnv1[p], ln1_ready, rstd1[p], r1_ready)
                if not fixed or 0 <= t - 3 < B:
                    rstd_of(t - 3, mv2_ready, mv2[1 - p], lnv2[1 - p], ln2_ready, rstd2[1 - p], r2_ready)
                if not fixed or t + 3 < B:
                    rstd_of(t + 3, lnx_mv, mv[1 - p], lnv[1 - p], lnx_ln, rstd[1 - p], lnx_r)
            skewed(act, -3, MAIN, B + 3, step)
            for c in range(3):
                lo, hi = c * 512, min((c + 1) * 512, B * M)
                act.wait_ge(ctxss_done, c + 1)
                nc.scalar.activation(ctx_n[:, lo:hi], bank[5 + c][:, 0:hi - lo], ACT.Ln, scale=1.0 / D, bias=eps_rms[:]).then_inc(ctxln_ready, 1)
                act.wait_ge(ctxln_ready, c + 1)
                nc.scalar.activation(ctx_n[:, lo:hi], ctx_n[:, lo:hi], ACT.Exp, scale=-0.5).then_inc(ctxr_ready, 1)
            route_scalar(act, 0)

            def gru_inputs(b, p):
                act.wait_ge(vw_done, b + 1)
                nc.scalar.copy(vw_all[:, bass.ds(b, 1), :].rearrange("p o d -> p (o d)"), bank[2 + p][0:M, 0:GATES]).then_inc(vw_ready, 1)
            skewed(act, 0, (2, B), B - 1, gru_inputs)
            experts_scalar(act, 0)

            def group_rstd(g, mv_sem, ln_sem, r_sem):
                act.wait_ge(mv_sem, g + 1)
                nc.scalar.activation(gln[:], gmv[:, :, 1:2].rearrange("p b o -> p (b o)"), ACT.Ln, bias=eps_ln[:]).then_inc(ln_sem, 1)
                act.wait_ge(ln_sem, g + 1)
                nc.scalar.activation(gr[:], gln[:], ACT.Exp, scale=-0.5).then_inc(r_sem, 1)
            act.preload_act_table_set("natural_log_exp_and_others")
            for g in range(NG):
                group_rstd(g, gmv_ready, gln_ready, gr_ready)

            def slot_step(s, g):
                fixed = isinstance(s, int)
                p = g % 2
                now = not fixed or s < SLOT_STEPS
                before = not fixed or 0 <= s - 1
                act.preload_act_table_set("natural_log_exp_and_others")
                if now:
                    act.wait_ge(ss_done, s + 1)
                    nc.scalar.activation(rln[p][:], bank[0][:], ACT.Ln, scale=1.0 / D, bias=eps_rms[:]).then_inc(rln_ready, 1)
                    act.wait_ge(rln_ready, s + 1)
                    nc.scalar.activation(rln[p][:], rln[p][:], ACT.Exp, scale=-0.5).then_inc(rs_ready, 1)
                if before:
                    act.wait_ge(asum_done, s)
                    nc.scalar.activation(aln[1 - p][:], bank[3][0:M, :], ACT.Ln).then_inc(aln_ready, 1)
                    act.wait_ge(aln_ready, s)
                    nc.scalar.activation(aln[1 - p][:], aln[1 - p][:], ACT.Exp, scale=-1.0).then_inc(ar_ready, 1)
                act.preload_act_table_set("exp_and_others")
                if before:
                    act.wait_ge(gx_done, 3 * s - 2)
                    nc.scalar.activation(tr[1 - p][:], bank[4][:], ACT.Tanh, scale=0.5, bias=brz[:, 0:1]).then_inc(tr_ready, 1)
                    act.wait_ge(gx_done, 3 * s - 1)
                    nc.scalar.activation(tz[1 - p][:], bank[5][:], ACT.Tanh, scale=0.5, bias=brz[:, 1:2]).then_inc(tz_ready, 1)
                if now:
                    act.wait_ge(csub_ready, s + 1)
                    nc.scalar.activation(ex[p][:], ex[p][:], ACT.Exp).then_inc(cexp_ready, 1)
                if before:
                    act.wait_ge(un_ready, s)
                    nc.scalar.activation(nn[1 - p][:], u[1 - p][:], ACT.Tanh, bias=vecs[:, V_BIH + 2:V_BIH + 3]).then_inc(nn_ready, 1)
            skewed_groups(act, 0, SLOT_MAIN, SLOT_STEPS, slot_step)
            act.preload_act_table_set("natural_log_exp_and_others")
            for g in range(NG):
                group_rstd(g, gmv3_ready, gln3_ready, gr3_ready)
                act.wait_ge(x3T_done, g + 1)
                nc.scalar.copy(x3T[g % 2][:], bank[4 + g][:]).then_inc(x3T_ready, 1)
            route_scalar(act, 1)
            experts_scalar(act, 1)

        @block.vector
        def _(dve):
            dve.wait_ge(ld_ctx, 16)
            nc.vector.tensor_scalar(mask_f, mask_i, 0.0, None, ALU.not_equal).then_inc(mask_ready, 1)
            dve.wait_ge(ld_const, 64)
            dve.wait_ge(ld_rows, 32)
            dve.wait_ge(mask_ready, 1)
            nc.vector.tensor_scalar(neg3[:], mask_f[0:3, :], 0.0, negp[:], ALU.is_equal, ALU.mult).then_inc(neg_ready, 1)
            nc.vector.tensor_scalar(bq[:], vecs[:, V_BQ:V_BQ + 1], HD ** -0.5, None, ALU.mult).then_inc(small_ready, 1)
            nc.vector.tensor_copy(upper[:], consts[:, C_UPPER:C_UPPER + P]).then_inc(consts2_ready, 1)
            nc.vector.tensor_tensor(brz[:], vecs[:, V_BIH:V_BIH + 2], vecs[:, V_BHH:V_BHH + 2], ALU.add).then_inc(consts2_ready, 1)
            nc.vector.tensor_scalar(bhn[:], vecs[:, V_BHH + 2:V_BHH + 3], 0.5, None, ALU.mult).then_inc(consts2_ready, 1)
            dve.wait_ge(consts2_ready, 3)
            nc.vector.tensor_scalar(brz[:], brz[:], 0.5, None, ALU.mult).then_inc(consts2_ready, 1)
            nc.vector.tensor_scalar(wslot[:], vecs[:, V_WSLOT:V_WSLOT + 1], D ** -0.5, None, ALU.mult).then_inc(small_ready, 1)
            for c in range(3):
                lo, hi = c * 512, min((c + 1) * 512, B * M)
                dve.wait_ge(kproj, c + 1)
                nc.vector.scalar_tensor_tensor(kT_all[:, lo:hi], bank[5 + c][:, 0:hi - lo], vecs[:, V_BK:V_BK + 1], mask_f[:, lo:hi],
                                               ALU.add, ALU.mult).then_inc(kT_ready, 1)

            def values(b, p):
                dve.wait_ge(v_done, b + 1)
                if isinstance(b, int) and b == 0:
                    dve.wait_ge(memset_ready, 9)
                nc.vector.tensor_tensor(
                    v_all[:, :, bass.ds(b, 1), 0:HD].rearrange("m h o c -> m (h o) c"),
                    bank[p][0:M, 0:D].rearrange("m (h c) -> m h c", c=HD),
                    rows[0:M, R_BV:R_BV + D].rearrange("m (h c) -> m h c", c=HD), ALU.add).then_inc(v_ready, 1)
            skewed(dve, 0, (2, B), B - 1, values)
            dve.wait_ge(small_ready, 2)
            dve.wait_ge(ld_x, 32)

            def normalise(dst, src, mv_t, r_t, ready):
                nc.vector.tensor_scalar(dst, src, mv_t[:, 0:1], r_t[:], ALU.subtract, ALU.mult).then_inc(ready, 1)

            def row(t, b):
                return t[:, bass.ds(b, 1), :].rearrange("p o d -> p (o d)")

            def step(t, p):
                fixed = isinstance(t, int)
                if not fixed or t + 3 < B:
                    nc.vector.bn_stats(st[1 - p][:], row(x_all, t + 3)).then_inc(lnx_st, 1)
                if not fixed or 0 <= t - 2 < B:
                    b = t - 2
                    acc = bank[5][:, 0:H * HV].rearrange("p (h c) -> p h c", c=HV)
                    dve.wait_ge(pv_done, NT * b + NT)
                    nc.vector.reciprocal(rden[p][:], acc[:, :, HD:HV].rearrange("p h c -> p (h c)")).then_inc(rden_ready, 1)
                if not fixed or t + 3 < B:
                    dve.wait_ge(lnx_st, t + 4)
                    nc.vector.memset(hold[:, 0:1], 0.0)
                    nc.vector.bn_aggr(mv[1 - p][:], st[1 - p][:]).then_inc(lnx_mv, 1)
                if not fixed or 0 <= t - 2 < B:
                    dve.wait_ge(rden_ready, b + 1)
                    need(dve, oT_done, b - 1)
                    nc.vector.tensor_tensor(o_sb[p][:].rearrange("p (h c) -> p h c", c=HD), acc[:, :, 0:HD],
                                            rden[p][:].unsqueeze(2).broadcast_to([P, H, HD]), ALU.mult).then_inc(o_ready, 1)
                if not fixed or 0 <= t - 4:
                    dve.wait_ge(r2_ready, t - 3)
                    normalise(row(xh_all, t - 4), xin[p][:], mv2[p], rstd2[p], xh_ready)
                if not fixed or 0 <= t + 2 < B:
                    dve.wait_ge(lnx_r, t + 3)
                    need(dve, xnT_done, t + 1)
                    normalise(xn[p][:], row(x_all, t + 2), mv[p], rstd[p], xn_ready)
                if not fixed or 0 <= t < B:
                    def scores(g):
                        h0, n = HEAD_GROUPS[g]
                        return bank[g][:, 0:n * M].rearrange("p (h m) -> p h m", m=M), smax[p][:, h0:h0 + n], probs[p][:, h0:h0 + n, :], n

                    def largest(g):
                        src, top, _, n = scores(g)
                        dve.wait_ge(s_done, 3 * t + g + 1)
                        nc.vector.tensor_reduce(top, src, X, ALU.max).then_inc(max_ready, 1)

                    def less(g):
                        src, top, dst, n = scores(g)
                        dve.wait_ge(max_ready, 3 * t + g + 1)
                        need(dve, pT_done, NT * (t - 1))
                        nc.vector.tensor_tensor(dst, src, top.unsqueeze(2).broadcast_to([P, n, M]), ALU.subtract).then_inc(sub_ready, 1)
                    largest(0)
                    less(0)
                    largest(1)
                    less(1)
                    largest(2)
                    less(2)
                if not fixed or 0 <= t - 2 < B:
                    b = t - 2
                    dve.wait_ge(wo_done, b + 1)
                    dve.wait_ge(xbo_ready, b + 1)
                    need(dve, res_ready, b - 1)
                    nc.vector.tensor_tensor(x1[p][:], bank[7][:, P:2 * P], xbo[p][:], ALU.add).then_inc(x1_ready, 1)
                if not fixed or 0 <= t - 3 < B:
                    dve.wait_ge(r1_ready, t - 2)
                    normalise(xin[1 - p][:], x1[1 - p][:], mv1[1 - p], rstd1[1 - p], xin_ready)
                if not fixed or 0 <= t - 2 < B:
                    dve.wait_ge(x1_ready, t - 1)
                    nc.vector.bn_stats(st1[p][:], x1[p][:]).then_inc(st1_ready, 1)
                if not fixed or 0 <= t - 3 < B:
                    dve.wait_ge(xin_ready, t - 2)
                    nc.vector.bn_stats(st2[1 - p][:], xin[1 - p][:]).then_inc(st2_ready, 1)
                if not fixed or 0 <= t - 2 < B:
                    dve.wait_ge(st1_ready, t - 1)
                    nc.vector.memset(hold[:, 1:2], 0.0)
                    nc.vector.bn_aggr(mv1[p][:], st1[p][:]).then_inc(mv1_ready, 1)
                if not fixed or 0 <= t - 3 < B:
                    dve.wait_ge(st2_ready, t - 2)
                    nc.vector.memset(hold[:, 2:3], 0.0)
                    nc.vector.bn_aggr(mv2[1 - p][:], st2[1 - p][:]).then_inc(mv2_ready, 1)
            skewed(dve, -3, MAIN, B + 3, step)
            dve.wait_ge(aff_ready, B)
            route_vector(dve, 0)
            dve.wait_ge(ld_bias, 32)
            left = bias_in
            for k in range(3):
                nc.vector.tensor_copy(bias_part[:, :, k, :], left[:]).then_inc(bias_split, 1)
                if k < 2:
                    dve.wait_ge(bias_split, k + 1)
                    nc.vector.tensor_tensor(bias_left[:], left[:], bias_part[:, :, k, :], ALU.subtract).then_inc(bias_chain, 1)
                    dve.wait_ge(bias_chain, k + 1)
                    left = bias_left
            dve.wait_ge(abproj, 2)
            nc.vector.tensor_scalar(ab[:, 0:D], bank[3][:, 0:D], vecs[:, V_WIN:V_WIN + 1], None, ALU.mult).then_inc(ab_ready, 1)
            nc.vector.tensor_scalar(ab[:, D:], bank[4][:, 0:GATES], vecs[:, V_WIN:V_WIN + 1], None, ALU.mult).then_inc(ab_ready, 1)
            dve.wait_ge(ctxr_ready, 3)
            nc.vector.tensor_tensor(ctx_n[:], ctx_n[:], ctxT_all[:], ALU.mult).then_inc(ctxn_ready, 1)
            dve.wait_ge(ctxn_ready, 1)

            def context_rows(b, p):
                need(dve, vw_done, b - 1)
                nc.vector.tensor_copy(ctxn[p][:], ctx_n[:, bass.ds(b * M, M)]).then_inc(ctxn_copied, 1)
            skewed(dve, 0, (2, B), B - 1, context_rows)
            kq_flat = kq_all[:].rearrange("p b m -> p (b m)")
            for c in range(3):
                lo, hi = c * 512, min((c + 1) * 512, B * M)
                dve.wait_ge(kq_done, c + 1)
                nc.vector.tensor_scalar(kq_flat[:, lo:hi], bank[5 + c][:, 0:hi - lo], wslot[:], None, ALU.mult).then_inc(kq_ready, 1)
            experts_vector(dve, 0)

            def group_norm(g, src, chain, base_count, mv_sem, r_sem, dst, dst_sem):
                for i in range(GROUP):
                    nc.vector.bn_stats(gst[:, i, :], src[:, i, :]).then_inc(chain, 1)
                dve.wait_ge(chain, base_count + GROUP)
                for i in range(GROUP):
                    last = nc.vector.bn_aggr(gmv[:, i, :], gst[:, i, :])
                last.then_inc(mv_sem, 1)
                dve.wait_ge(mv_sem, g + 1)
                nc.vector.tensor_tensor(dst, src, gmv[:, :, 0:1].broadcast_to([P, GROUP, D]), ALU.subtract).then_inc(chain, 1)
                dve.wait_ge(chain, base_count + GROUP + 1)
                dve.wait_ge(r_sem, g + 1)
                nc.vector.tensor_tensor(dst, dst, gr[:].unsqueeze(2).broadcast_to([P, GROUP, D]), ALU.mult).then_inc(dst_sem, 1)

            for g in range(NG):
                gb = slice(g * GROUP, (g + 1) * GROUP)
                K = 2 + GROUP + 1
                dve.wait_ge(gathered[g], 16 * GROUP)
                dve.wait_ge(share_ready, 1)
                nc.vector.tensor_tensor(f_all[:, gb, :], f_all[:, gb, :], share[:, gb].unsqueeze(2).broadcast_to([P, GROUP, D]), ALU.mult).then_inc(x2_chain, 1)
                dve.wait_ge(x2_chain, K * g + 1)
                dve.wait_ge(res_ready, B)
                nc.vector.tensor_tensor(x2_all[:, gb, :], f_all[:, gb, :], res_all[:, gb, :], ALU.add).then_inc(x2_chain, 1)
                dve.wait_ge(x2_chain, K * g + 2)
                need(dve, gT_done, g - 1)
                group_norm(g, x2_all[:, gb, :], x2_chain, K * g + 2, gmv_ready, gr_ready, gx[g % 2][:], gx_ready)
                if g:
                    dve.wait_ge(gT_done, g)
                    nc.vector.tensor_copy(hT[:, (g - 1) * G:g * G], bank[4 + g - 1][:]).then_inc(h_ready, 1)
            dve.wait_ge(gT_done, NG)
            nc.vector.tensor_copy(hT[:, (NG - 1) * G:], bank[4 + NG - 1][:]).then_inc(h_ready, 1)

            def slot_step(s, g):
                fixed = isinstance(s, int)
                p = g % 2
                now = not fixed or 0 <= s < SLOT_STEPS
                before = not fixed or 0 <= s - 1 < SLOT_STEPS
                g0 = (g - 1) % NG
                h0 = hT[:, g0 * G:(g0 + 1) * G]
                if now:
                    dve.wait_ge(rs_ready, s + 1)
                    nc.vector.tensor_tensor(hs[p][:], hT[:, g * G:(g + 1) * G], rln[p][:], ALU.mult).then_inc(hs_ready, 1)
                if before:
                    dve.wait_ge(gh_done, s)
                    nc.vector.tensor_scalar(hnb[1 - p][:], bank[6][:], 0.5, bhn[:], ALU.mult, ALU.add).then_inc(hnb_ready, 1)
                    dve.wait_ge(ar_ready, s)
                    nc.vector.tensor_tensor(attn[1 - p][:], att[1 - p][0:M, :], aln[1 - p][:], ALU.mult).then_inc(attn_ready, 1)
                if now:
                    dve.wait_ge(c_done, s + 1)
                    sc = bank[2][0:M, :].rearrange("m (b s) -> m b s", s=S)
                    nc.vector.tensor_reduce(cmax[p][:], sc, X, ALU.max).then_inc(cmax_ready, 1)
                    dve.wait_ge(cmax_ready, s + 1)
                    nc.vector.tensor_tensor(ex[p][:], sc, cmax[p][:].unsqueeze(2).broadcast_to([M, GROUP, S]), ALU.subtract).then_inc(csub_ready, 1)
                if before:
                    dve.wait_ge(tr_ready, s)
                    dve.wait_ge(hnb_ready, s)
                    nc.vector.scalar_tensor_tensor(u[1 - p][:], tr[1 - p][:], 1.0, hnb[1 - p][:], ALU.add, ALU.mult).then_inc(u_ready, 1)
                    dve.wait_ge(u_ready, s)
                    dve.wait_ge(gx_done, 3 * s)
                    nc.vector.tensor_tensor(u[1 - p][:], u[1 - p][:], bank[7][:], ALU.add).then_inc(un_ready, 1)
                if now:
                    dve.wait_ge(cexp_ready, s + 1)
                    nc.vector.tensor_reduce(csum[p][:], ex[p][:], X, ALU.add).then_inc(crec_ready, 1)
                    dve.wait_ge(crec_ready, 2 * s + 1)
                    nc.vector.reciprocal(crec[p][:], csum[p][:]).then_inc(crec_ready, 1)
                    dve.wait_ge(crec_ready, 2 * s + 2)
                    nc.vector.tensor_tensor(att[p][0:M, :].rearrange("m (b s) -> m b s", s=S), ex[p][:], crec[p][:].unsqueeze(2).broadcast_to([M, GROUP, S]),
                                            ALU.mult).then_inc(att_ready, 1)
                if before:
                    dve.wait_ge(dd_ready, s)
                    dve.wait_ge(tz_ready, s)
                    nc.vector.scalar_tensor_tensor(dd[1 - p][:], tz[1 - p][:], 1.0, dd[1 - p][:], ALU.add, ALU.mult).then_inc(e_ready, 1)
                    dve.wait_ge(e_ready, s)
                    nc.vector.scalar_tensor_tensor(h0, dd[1 - p][:], 0.5, nn[1 - p][:], ALU.mult, ALU.add).then_inc(h_ready, 1)
            skewed_groups(dve, 0, SLOT_MAIN, SLOT_STEPS, slot_step)

            for g in range(NG):
                gb = slice(g * GROUP, (g + 1) * GROUP)
                K = 1 + GROUP + 1
                dve.wait_ge(hb_done, g + 1)
                nc.vector.tensor_tensor(x2_all[:, gb, :], x2_all[:, gb, :], bank[g][:].rearrange("p (b d) -> p b d", d=D), ALU.add).then_inc(x3_chain, 1)
                dve.wait_ge(x3_chain, K * g + 1)
                group_norm(g, x2_all[:, gb, :], x3_chain, K * g + 1, gmv3_ready, gr3_ready, xh_all[:, gb, :], x3_ready)
                dve.wait_ge(logit_done, g + 1)
                nc.vector.tensor_tensor(aff_all[:, gb, :], bank[g][:, 0:GROUP * E].rearrange("p (b e) -> p b e", e=E),
                                        rows[:, R_BG:R_BG + E].unsqueeze(1).broadcast_to([P, GROUP, E]), ALU.add).then_inc(logit_ready, 1)
            dve.wait_ge(logit_ready, NG)
            route_vector(dve, 1)
            experts_vector(dve, 1)
            for g in range(NG):
                gb = slice(g * GROUP, (g + 1) * GROUP)
                dve.wait_ge(gathered[g], 2 * 16 * GROUP)
                dve.wait_ge(share_ready, 2)
                nc.vector.tensor_tensor(f_all[:, gb, :], f_all[:, gb, :], share[:, gb].unsqueeze(2).broadcast_to([P, GROUP, D]), ALU.mult).then_inc(fin_chain, 1)
                dve.wait_ge(fin_chain, g + 1)
                nc.vector.tensor_tensor(f_all[:, gb, :], f_all[:, gb, :], x2_all[:, gb, :], ALU.add).then_inc(fin_ready, 1)

        @block.tensor
        def _(pe):
            pe.wait_ge(ld_const, 64)
            for c in range(3):
                lo, hi = c * 512, min((c + 1) * 512, B * M)
                nc.tensor.matmul(bank[5 + c][:, 0:hi - lo], w0[:, 1, :], ctxT_all[:, lo:hi], start=True, stop=True).then_inc(kproj, 1)

            def values(b, p):
                pe.wait_ge(ctx_copied, b + 1)
                need(pe, v_ready, b - 1)
                nc.tensor.matmul(bank[p][0:M, 0:D], ctxT[p][:], w0[:, 2, :], start=True, stop=True).then_inc(v_done, 1)
            skewed(pe, 0, (2, B), B - 1, values)
            pe.wait_ge(neg_ready, 1)
            pe.wait_ge(kT_ready, 3)
            pe.wait_ge(v_ready, B)
            pe.wait_ge(ld_w1, 48)
            pe.wait_ge(v_placed, 16 * len(PIECES))

            def p_turn(b, par, q):
                n = b * NT + q
                lo, hi = TURNS[q]
                need(pe, pT_ready, n - 1)
                flat = probs[par][:].rearrange("p h m -> p (h m)")
                for c in range(lo, hi):
                    last = nc.tensor.transpose(bank[3 + (par + q) % 2][0:CHUNK_ROWS[c], (c - lo) * S:(c - lo + 1) * S], flat[:, c * P:c * P + CHUNK_ROWS[c]], ident)
                last.then_inc(pT_done, 1)

            def p_value(b, par, q):
                n = b * NT + q
                lo, hi = TURNS[q]
                if q == 0:
                    need(pe, o_ready, b)
                    nc.tensor.matmul(bank[5][:, 0:H * HV], ones3[:], zero3[:], start=True, stop=False)
                pe.wait_ge(pT_ready, n + 1)
                for c in range(lo, hi):
                    own = CHUNK_PIECES[c]
                    h, count, rows_c = PIECES[own[0]][1], len(own), CHUNK_ROWS[c]
                    last = nc.tensor.matmul(bank[5][:, h * HV:(h + count) * HV].rearrange("p (h c) -> p h c", c=HV), pT[(par + q) % 2][0:rows_c, c - lo, :],
                                            v_rows[0:rows_c, own[0]:own[-1] + 1, bass.ds(b, 1), :].rearrange("p i o c -> p (i o) c"),
                                            start=False, stop=c == CHUNKS - 1)
                last.then_inc(pv_done, 1)

            def step(t, p):
                fixed = isinstance(t, int)
                now = not fixed or 0 <= t < B
                before = not fixed or 0 <= t - 1 < B
                after = not fixed or 0 <= t + 1 < B
                old = not fixed or 0 <= t - 2 < B
                oldest = not fixed or 0 <= t - 4

                def scores(g):
                    h0, n = HEAD_GROUPS[g]
                    need(pe, sub_ready, 3 * (t - 1) + g + 1)
                    dst = bank[g][:, 0:n * M]
                    nc.tensor.matmul(dst, qT[p][:], kblk[p][:, h0:h0 + n, :].rearrange("p h m -> p (h m)"), start=True, stop=False)
                    nc.tensor.matmul(dst.rearrange("p (h m) -> p h m", m=M), ones3[:], neg3[:, bass.ds(t * M, M)].unsqueeze(1).broadcast_to([3, n, M]),
                                     start=False, stop=True).then_inc(s_done, 1)
                if now:
                    pe.wait_ge(q_ready, t + 1)
                    pe.wait_ge(kblk_ready, t + 1)
                    scores(0)
                if after:
                    pe.wait_ge(xn_ready, t + 2)
                    need(pe, q_ready, t + 1)
                    nc.tensor.transpose(bank[6][:, 0:P], xn[1 - p][:], ident).then_inc(xnT_done, 1)
                if before:
                    pe.wait_ge(exp_ready, 3 * t - 1)
                    p_turn(t - 1, 1 - p, 0)
                if oldest:
                    pe.wait_ge(xin_ready, t - 3)
                    pe.wait_ge(x1_ready, min(t - 2, B) if fixed else t - 2)
                    if fixed and not old:
                        need(pe, aff_ready, t - 4)
                    nc.tensor.transpose(bank[7][:, 2 * P:3 * P], xin[p][:], ident).then_inc(xinT_done, 1)
                if now:
                    scores(1)
                if before:
                    pe.wait_ge(exp_ready, 3 * t)
                    p_turn(t - 1, 1 - p, 1)
                    p_value(t - 1, 1 - p, 0)
                if oldest:
                    pe.wait_ge(xinT_ready, t - 3)
                    nc.tensor.matmul(bank[7][:, 3 * P:3 * P + E], xinT[p][:], gates[:, 0, :], start=True, stop=True).then_inc(aff_done, 1)
                if after:
                    pe.wait_ge(xnT_ready, t + 2)
                    nc.tensor.matmul(bank[6][:, P:2 * P], w0[:, 0, :], xnT[1 - p][:], start=True, stop=True).then_inc(q_done, 1)
                if now:
                    scores(2)
                if old:
                    pe.wait_ge(o_ready, t - 1)
                    need(pe, aff_ready, t - 3)
                    if not oldest:
                        need(pe, x1_ready, t - 2)
                    nc.tensor.transpose(bank[7][:, 0:P], o_sb[p][:], ident).then_inc(oT_done, 1)
                if before:
                    p_turn(t - 1, 1 - p, 2)
                    p_value(t - 1, 1 - p, 1)
                if old:
                    pe.wait_ge(oT_ready, t - 1)
                    nc.tensor.matmul(bank[7][:, P:2 * P], oT[p][:], w0[:, 3, :], start=True, stop=True).then_inc(wo_done, 1)
                if before:
                    p_value(t - 1, 1 - p, 2)
            skewed(pe, -1, MAIN, B + 3, step)
            pe.wait_ge(memset_ready, 9)
            pe.wait_ge(consts2_ready, 4)
            pe.wait_ge(aff_ready, B)
            nc.tensor.matmul(bank[3][:, 0:D], w1[:, 1, :], w1[:, 0, :], start=True, stop=True).then_inc(abproj, 1)
            nc.tensor.matmul(bank[4][:, 0:GATES], w1[:, 2, :], gru[:, 0, :], start=True, stop=True).then_inc(abproj, 1)
            route_tensor(pe, 0)
            pe.wait_ge(ctxsq_ready, 1)
            for c in range(3):
                lo, hi = c * 512, min((c + 1) * 512, B * M)
                nc.tensor.matmul(bank[5 + c][:, 0:hi - lo], ones_f[:], ctx_n[:, lo:hi], start=True, stop=True).then_inc(ctxss_done, 1)
            pe.wait_ge(ab_ready, 2)

            def gru_inputs(b, p):
                pe.wait_ge(ctxn_copied, b + 1)
                need(pe, vw_ready, b - 1)
                nc.tensor.matmul(bank[2 + p][0:M, 0:GATES], ctxn[p][:], ab[:, D:], start=True, stop=True).then_inc(vw_done, 1)
            skewed(pe, 0, (2, B), B - 1, gru_inputs)
            for c in range(3):
                lo, hi = c * 512, min((c + 1) * 512, B * M)
                nc.tensor.matmul(bank[5 + c][:, 0:hi - lo], ab[:, 0:D], ctx_n[:, lo:hi], start=True, stop=True).then_inc(kq_done, 1)
            pe.wait_ge(vw_ready, B)
            pe.wait_ge(kq_ready, 3)
            pe.wait_ge(pos_ready, 1)
            experts_tensor(pe, 0)
            pe.wait_ge(y_ready, TILES)
            for g in range(NG):
                pe.wait_ge(gx_ready, g + 1)
                for i in range(GROUP):
                    last = nc.tensor.transpose(bank[4 + g][:, i * P:(i + 1) * P], gx[g % 2][:, i, :], ident)
                last.then_inc(gT_done, 1)

            def slot_step(s, g):
                fixed = isinstance(s, int)
                p = g % 2
                now = not fixed or 0 <= s < SLOT_STEPS
                before = not fixed or 0 <= s - 1 < SLOT_STEPS
                g0 = (g - 1) % NG
                cols = lambda i: slice(i * S, (i + 1) * S)
                if now:
                    pe.wait_ge(sq_ready, s + 1)
                    need(pe, rln_ready, s)
                    nc.tensor.matmul(bank[0][:], ones_f[:], sq[p][:], start=True, stop=True).then_inc(ss_done, 1)
                if before:
                    h0 = hT[:, g0 * G:(g0 + 1) * G]
                    pe.wait_ge(h_ready, s)
                    if fixed and s == 1:
                        pe.wait_ge(h_ready, NG)
                    need(pe, hnb_ready, s - 1)
                    nc.tensor.matmul(bank[6][:], gru[:, 1, 2 * D:], h0, start=True, stop=True).then_inc(gh_done, 1)
                    pe.wait_ge(att_ready, s)
                    nc.tensor.matmul(bank[3][0:M, :], ones_f[0:M + 1, 0:M], att[1 - p][:], start=True, stop=True).then_inc(asum_done, 1)
                    need(pe, tz_ready, s - 1)
                    nc.tensor.matmul(bank[4][:], gru[:, 1, 0:D], h0, start=True, stop=False)
                    nc.tensor.matmul(bank[5][:], gru[:, 1, D:2 * D], h0, start=True, stop=False)
                if now:
                    pe.wait_ge(hs_ready, s + 1)
                    need(pe, csub_ready, s)
                    for i in range(GROUP):
                        last = nc.tensor.matmul(bank[2][0:M, cols(i)], kq_all[:, g * GROUP + i, :], hs[p][:, cols(i)], start=True, stop=True)
                    last.then_inc(c_done, 1)
                if before:
                    pe.wait_ge(attn_ready, s)
                    need(pe, un_ready, s - 1)
                    for k, bk in enumerate((4, 5, 7)):
                        for i in range(GROUP):
                            last = nc.tensor.matmul(bank[bk][:, cols(i)], vw_all[:, g0 * GROUP + i, k * D:(k + 1) * D], attn[1 - p][:, cols(i)],
                                                    start=bk == 7, stop=bk == 7 or i == GROUP - 1)
                        last.then_inc(gx_done, 1)
            skewed_groups(pe, 0, SLOT_MAIN, SLOT_STEPS, slot_step)

            pe.wait_ge(csub_ready, SLOT_STEPS)
            for g in range(NG):
                pe.wait_ge(h_ready, SLOT_STEPS + g + 1)
                for i in range(GROUP):
                    last = nc.tensor.transpose(bank[g][:, i * P:(i + 1) * P], hT[:, (g * GROUP + i) * S:(g * GROUP + i + 1) * S], ident)
                last.then_inc(hb_done, 1)
            for g in range(NG):
                pe.wait_ge(x3_ready, g + 1)
                for i in range(GROUP):
                    last = nc.tensor.transpose(bank[4 + g][:, i * P:(i + 1) * P], xh_all[:, g * GROUP + i, :], ident)
                last.then_inc(x3T_done, 1)
                pe.wait_ge(x3T_ready, g + 1)
                for i in range(GROUP):
                    last = nc.tensor.matmul(bank[g][:, i * E:(i + 1) * E], x3T[g % 2][:, i * P:(i + 1) * P], gates[:, 1, :], start=True, stop=True)
                last.then_inc(logit_done, 1)
            pe.wait_ge(logit_ready, NG)
            route_tensor(pe, 1)
            pe.wait_ge(pos_ready, 2)
            experts_tensor(pe, 1)


def _shape_constants():
    c = np.zeros((P, C_ALL), np.float32)
    c[:, C_IDENT:C_IDENT + P] = np.eye(P)
    c[:, C_HEAD:C_HEAD + H] = np.arange(P)[:, None] // HD == np.arange(H)[None]
    c[:, C_TIE:C_TIE + B * E] = np.tile(E - np.arange(E), B)[None]
    c[:, C_JOTA:C_JOTA + TILES * E] = np.repeat(np.arange(TILES), E)[None]
    c[:, C_RESET:C_UPPER] = np.tile(np.arange(B) > 0, E)[None]
    c[:, C_UPPER:] = np.arange(P)[:, None] < np.arange(P)[None]
    return c


def kernel(**inputs):
    import concourse.bacc as bacc
    from concourse.bass_utils import run_bass_kernel_spmd

    i = {k: np.asarray(v) for k, v in inputs.items()}
    col = lambda v: v.reshape(-1, P).T
    packed = {
        "consts": _shape_constants(),
        "negp": np.array([[-998244352.0], [-1753088.0], [-2560.0]], np.float32),
        "x": i["x"],
        "ctxT_all": i["ctx_1024"].transpose(2, 0, 1).reshape(D, B * M),
        "mask": i["mask_Bx1x1xS2_ik0"].reshape(1, B * M),
        "vecs": np.concatenate([col(i[n]) for n in (
            "L0_xattn_bq", "L0_xattn_bk", "L1_xattn_input_norm_w", "L1_xattn_slot_norm_w", "L1_xattn_gru_bih", "L1_xattn_gru_bhh")], axis=1),
        "rows": np.concatenate([i["L0_xattn_bv"], i["L0_xattn_bo"], i["L1_ffn_bg"]])[None],
        "w0": np.stack([i[f"L0_xattn_W{n}"] for n in "qkvo"], axis=1),
        "w1": np.stack([i[f"L1_xattn_W{n}"] for n in "qkv"], axis=1),
        "gru": np.stack([i["L1_xattn_gru_wih"].T, i["L1_xattn_gru_whh"].T], axis=1),
        "gates": np.stack([i["L0_ffn_centroids"].T, i["L1_ffn_Wg"]], axis=1),
    }
    def experts(up, down):
        return np.concatenate([up.transpose(1, 0, 2), down.reshape(E, FC, P, D).transpose(2, 0, 1, 3).reshape(P, E, FC * D)], axis=2)

    def biases(b1, b2):
        return np.concatenate([b1, b2], axis=1).reshape(BIAS_ROWS, P)
    packed |= {
        "wf0": experts(i["L0_ffn_w1"].transpose(0, 2, 1), i["L0_ffn_w2"].transpose(0, 2, 1)),
        "wf1": experts(i["L1_ffn_W1"], i["L1_ffn_W2"]),
        "biases": np.stack([biases(i["L0_ffn_b1"], i["L0_ffn_b2"]), biases(i["L1_ffn_b1"], i["L1_ffn_b2"])], axis=1),
        "ln_gb": np.stack([i["L0_ffn_ln_g"], i["L0_ffn_ln_b"]]).reshape(1, 2 * E * D),
    }
    nc = bacc.Bacc("TRN2", target_bir_lowering=False, num_devices=1)
    arrays, handles = {}, {}
    for name, v in packed.items():
        v = np.ascontiguousarray(v)
        arrays[f"in_{name}"] = v
        handles[name] = nc.dram_tensor(f"in_{name}", v.shape, mybir.dt.from_np(v.dtype), kind="ExternalInput").ap()
    out = nc.dram_tensor("out", (B, S, D), F32, kind="ExternalOutput").ap()
    build(nc, handles, out)
    got = run_bass_kernel_spmd(nc, [arrays], core_ids=[0])
    return got.results[0]["out"]
```

```python
from contextlib import ExitStack

import numpy as np

import concourse.bass as bass
from concourse import mybir

F32 = mybir.dt.float32
BF16 = mybir.dt.bfloat16
I32 = mybir.dt.int32
ALU = mybir.AluOpType
ACT = mybir.ActivationFunctionType
X = mybir.AxisListType.X

P = 128
B, S, D = 16, 128, 128
M = 77
H, HD = 16, 8
HV = HD + 1
E, F = 8, 512
FC = F // P
TILES = B * S // P + E - 1
HEAD_GROUPS = ((0, 6), (6, 5), (11, 5))
CHUNKS = -(-H * M // P)
PIECES = [(c, h, max(c * P - h * M, 0), max(h * M - c * P, 0), min((h + 1) * M, (c + 1) * P) - max(h * M, c * P))
          for c in range(CHUNKS) for h in range(c * P // M, min(((c + 1) * P - 1) // M + 1, H))]
CHUNK_ROWS = [min(P, H * M - c * P) for c in range(CHUNKS)]
CHUNK_PIECES = [[i for i, piece in enumerate(PIECES) if piece[0] == c] for c in range(CHUNKS)]
TURNS = ((0, 4), (4, 8), (8, CHUNKS))
NT = len(TURNS)
LN_EPS, RMS_EPS, ATT_EPS = 1e-5, 1e-6, 1e-6
NEG = -1e9
GATES = 3 * D

C_IDENT, C_HEAD, C_TIE, C_JOTA = 0, 128, 144, 272
C_RESET = C_JOTA + TILES * E
C_UPPER = C_RESET + E * B
C_ALL = C_UPPER + P
V_BQ, V_BK, V_WIN, V_WSLOT, V_BIH, V_BHH = 0, 1, 2, 3, 4, 7
V_ALL = 10
W_B1 = F
W_G = W_B1 + FC
W_B = W_G + 1
W_UP = W_B + 1
W_2 = W_UP
W_ALL = W_2 + F
GROUP = 4
G = GROUP * S
NG = B // GROUP
ITERS = 3
ROUTE_LINKS = 17
SLOT_STEPS = ITERS * NG
R_BV, R_BO, R_BG = 0, 128, 256
R_ALL = 264


def need(eng, sem, count):
    if not (isinstance(count, int) and count <= 0):
        eng.wait_ge(sem, count)


def skewed(eng, first, main, last, step, unroll=2):
    lo, hi = main
    for t in range(first, lo):
        step(t, t % unroll)
    with eng.Fori(0, (hi - lo) // unroll) as i:
        for k in range(unroll):
            step(i * unroll + (lo + k), (lo + k) % unroll)
    for t in range(hi, last + 1):
        step(t, t % unroll)


def skewed_groups(eng, first, main, last, step):
    lo, hi = main
    for s in range(first, lo):
        step(s, s % NG)
    with eng.Fori(0, (hi - lo) // NG) as i:
        for k in range(NG):
            step(i * NG + (lo + k), (lo + k) % NG)
    for s in range(hi, last + 1):
        step(s, s % NG)


def build(nc, a, out):
    with ExitStack() as ctx:
        def sb(name, shape, dt=F32):
            return ctx.enter_context(nc.sbuf_tensor(name, shape, dt))

        first = ExitStack()
        second = ExitStack()

        def sb1(name, shape, dt=F32):
            return first.enter_context(nc.sbuf_tensor(name, shape, dt))

        def sb2(name, shape, dt=F32):
            return second.enter_context(nc.sbuf_tensor(name, shape, dt))

        def sem(name):
            return ctx.enter_context(nc.semaphore(name))

        bank = [ctx.enter_context(nc.psum_tensor(f"bank{i}", [P, 512], F32)) for i in range(8)]

        consts = sb("consts", [P, C_ALL])
        vecs = sb("vecs", [P, V_ALL])
        rows = sb("rows", [P, R_ALL])
        w1 = sb("w1", [P, 3, D])
        gru = sb("gru", [P, 2, GATES])
        gates = sb("gates", [P, 2, E])
        negp = sb("negp", [3, 1])
        ones3 = sb("ones3", [3, P], BF16)
        ab = sb("ab", [P, D + GATES])
        vw_all = sb("vw_all", [M, B, GATES])
        kq_all = sb("kq_all", [P, B, M])
        ctxT_all = sb("ctxT_all", [P, B * M])
        ctx_n = sb("ctx_n", [P, B * M])
        wslot = sb("wslot", [P, 1])
        bq = sb("bq", [P, 1])
        eps_ln = sb("eps_ln", [P, 1])
        hold = sb("hold", [1, 3])
        eps_rms = sb("eps_rms", [P, 1])
        ident = consts[:, C_IDENT:C_IDENT + P]
        headmask = consts[:, C_HEAD:C_HEAD + H]

        def pair(name, shape, dt=F32):
            return [sb(f"{name}{i}", shape, dt) for i in range(2)]

        xh_all = sb("xh_all", [P, B, D])
        res_all = sb("res_all", [P, B, D])
        aff_all = sb("aff_all", [P, B, E])

        upper = sb("upper", [P, P], BF16)
        ones_b = sb("ones_b", [P, P], BF16)
        ones_e = sb("ones_e", [P, E])
        amax = sb("amax", [P, B])
        apick = sb("apick", [P, B, E])
        onehot = sb("onehot", [P, B, E], BF16)
        tot = sb("tot", [P, E, B])
        cum = sb("cum", [P, E * B])
        n_pad = sb("n_pad", [P, E], I32)
        n_tile_i = sb("n_tile_i", [P, E], I32)
        n_tile = sb("n_tile", [P, E])
        tile_end = sb("tile_end", [P, E])
        base = sb("base", [P, E])
        before_b = sb("before_b", [P, E * B])
        pos_be = sb("pos_be", [P, B, E])
        pos_f = sb("pos_f", [P, B])
        pos = sb("pos", [P, B], I32)
        tile_cmp = sb("tile_cmp", [P, TILES, E])
        tile_e = sb("tile_e", [P, TILES])
        tile_tab = sb("tile_tab", [P, TILES], I32)
        share = sb("share", [P, B])
        eg = sb("eg", [P, B, E])
        zero = sb("zero", [P, D])
        weights = sb("weights", [P, E, W_ALL])
        ctxn = pair("ctxn", [P, M])
        bias_in = sb("bias_in", [E, 2, D])
        bias_left = sb("bias_left", [E, 2, D])
        bias_part = sb("bias_part", [E, 2, 3, D], BF16)
        bias3 = sb("bias3", [3, E * D], BF16)
        att = pair("att", [M + 1, G])
        ones_f = sb("ones_f", [P, P])
        brz = sb("brz", [P, 2])
        bhn = sb("bhn", [P, 1])

        def pair1(name, shape, dt=F32):
            return [sb1(f"{name}{i}", shape, dt) for i in range(2)]
        x_all = sb1("x_all", [P, B, D])
        v_all = sb1("v_all", [M, H, B, HV])
        v_rows = sb1("v_rows", [P, len(PIECES), B, HV])
        zero3 = sb1("zero3", [3, H * HV], BF16)
        w0 = sb1("w0", [P, 4, D])
        mask_i = xh_all[:].rearrange("p b d -> p (b d)")[:, 0:B * M].bitcast(I32)
        mask_f = res_all[:].rearrange("p b d -> p (b d)")[:, 0:B * M]
        neg3 = sb1("neg3", [3, B * M], BF16)
        kT_all = sb1("kT_all", [P, B * M])
        st = pair1("st", [P, 6])
        mv = pair1("mv", [P, 2])
        lnv = pair1("lnv", [P, 1])
        rstd = pair1("rstd", [P, 1])
        xn = pair1("xn", [P, D])
        xnT = pair1("xnT", [P, S])
        qT = pair1("qT", [P, S])
        xbo = pair1("xbo", [P, D])
        kblk = pair1("kblk", [P, H, M])
        smax = pair1("smax", [P, H])
        probs = pair1("probs", [P, H, M])
        pT = pair1("pT", [P, 4, S])
        rden = pair1("rden", [P, H])
        o_sb = pair1("o_sb", [P, D])
        oT = pair1("oT", [P, S])
        x1 = pair1("x1", [P, D])
        st1 = pair1("st1", [P, 6])
        mv1 = pair1("mv1", [P, 2])
        lnv1 = pair1("lnv1", [P, 1])
        rstd1 = pair1("rstd1", [P, 1])
        xin = pair1("xin", [P, D])
        st2 = pair1("st2", [P, 6])
        mv2 = pair1("mv2", [P, 2])
        lnv2 = pair1("lnv2", [P, 1])
        rstd2 = pair1("rstd2", [P, 1])
        xinT = pair1("xinT", [P, S])
        first.close()

        f_all = sb("f_all", [P, B, D])
        x2_all = sb("x2_all", [P, B, D])
        tile_rows = sb2("tile_rows", [P, TILES, D])
        xt, xtT, hidT = ([sb2(f"{n}{i}", shape) for i in range(2)] for n, shape in (("xt", [P, D]), ("xtT", [P, P]), ("hidT", [P, FC, P])))
        w_up = [sb2(f"w_up{i}", [P, W_UP]) for i in range(4)]
        second.close()
        xs_dram = [nc.dram_tensor(f"xs{l}", (TILES * P, D), F32, kind="Internal").ap() for l in range(2)]
        ys_dram = [nc.dram_tensor(f"ys{l}", (TILES * P, D), F32, kind="Internal").ap() for l in range(2)]

        gst = sb("gst", [P, NG, GROUP, 6])
        gmv = sb("gmv", [P, NG, GROUP, 2])
        gln = sb("gln", [P, NG, GROUP])
        gr = sb("gr", [P, NG, GROUP])
        gx = pair("gx", [P, GROUP, D])
        hT = sb("hT", [P, B * S])
        sq = pair("sq", [P, G])
        rln = pair("rln", [P, G])
        hs = pair("hs", [P, G])
        cmax = pair("cmax", [M, GROUP])
        ex = pair("ex", [M, GROUP, S])
        csum = pair("csum", [M, GROUP])
        crec = pair("crec", [M, GROUP])
        aln = pair("aln", [M, G])
        attn = pair("attn", [M, G])
        tr = pair("tr", [P, G])
        tz = pair("tz", [P, G])
        hnb = pair("hnb", [P, G])
        u = pair("u", [P, G])
        nn = pair("nn", [P, G])
        dd = pair("dd", [P, G])
        x3T = tr

        ld_const, ld_rows, ld_x, ld_ctx, ld_w1 = sem("ld_const"), sem("ld_rows"), sem("ld_x"), sem("ld_ctx"), sem("ld_w1")
        memset_ready = sem("memset_ready")
        mask_ready, neg_ready, kproj, kT_ready, kT_mask = (sem(n) for n in ("mask_ready", "neg_ready", "kproj", "kT_ready", "kT_mask"))
        small_ready, abproj, ab_ready = sem("small_ready"), sem("abproj"), sem("ab_ready")
        ctxsq_ready, ctxss_done, ctxln_ready, ctxr_ready, ctxn_ready, kq_done = (sem(n) for n in ("ctxsq_ready", "ctxss_done", "ctxln_ready", "ctxr_ready", "ctxn_ready", "kq_done"))
        v_done, v_ready, rows_cleared, ctxn_copied, vw_done, vw_ready, kq_ready = (
            sem(n) for n in ("v_done", "v_ready", "rows_cleared", "ctxn_copied", "vw_done", "vw_ready", "kq_ready"))
        lnx_st, lnx_mv, lnx_ln, lnx_r, xn_ready = (sem(n) for n in ("lnx_st", "lnx_mv", "lnx_ln", "lnx_r", "xn_ready"))
        xbo_ready, kblk_ready = sem("xbo_ready"), sem("kblk_ready")
        xnT_done, xnT_ready, q_done, q_ready = (sem(n) for n in ("xnT_done", "xnT_ready", "q_done", "q_ready"))
        s_done, max_ready, sub_ready, exp_ready = (sem(n) for n in ("s_done", "max_ready", "sub_ready", "exp_ready"))
        pT_done, pT_ready, pv_done = sem("pT_done"), sem("pT_ready"), sem("pv_done")
        rden_ready, o_ready, oT_done, oT_ready, wo_done = (sem(n) for n in ("rden_ready", "o_ready", "oT_done", "oT_ready", "wo_done"))
        x1_ready, st1_ready, mv1_ready, ln1_ready, r1_ready, xin_ready = (sem(n) for n in ("x1_ready", "st1_ready", "mv1_ready", "ln1_ready", "r1_ready", "xin_ready"))
        st2_ready, mv2_ready, ln2_ready, r2_ready, xh_ready = (sem(n) for n in ("st2_ready", "mv2_ready", "ln2_ready", "r2_ready", "xh_ready"))
        res_ready, xinT_done, xinT_ready, aff_done, aff_ready = (sem(n) for n in ("res_ready", "xinT_done", "xinT_ready", "aff_done", "aff_ready"))
        stored = sem("stored")
        v_placed = [sem(f"v_placed{q}") for q in range(NT)]
        consts2_ready, zeroed = sem("consts2_ready"), sem("zeroed")

        class Layer:
            def __init__(self, l):
                self.chain0, self.one0, self.tile0 = ROUTE_LINKS * l, l, TILES * l
                self.scatter0, self.gather0 = 16 * B * l, 16 * GROUP * l
        layers = [Layer(0), Layer(1)]
        (chain, onehot_ready, rank_done, total_done, pos_ready, tab_ready, share_in, share_exp, share_ready,
         scattered, xtT_done, xtT_ready, up_done, hid_ready, w_up_ready, down_done, y_ready) = (sem(n) for n in (
             "chain", "onehot_ready", "rank_done", "total_done", "pos_ready", "tab_ready", "share_in", "share_exp", "share_ready",
             "scattered", "xtT_done", "xtT_ready", "up_done", "hid_ready", "w_up_ready", "down_done", "y_ready"))
        tiles_early, tiles_late, xt_ready, y_stored, weights_loaded = sem("tiles_early"), sem("tiles_late"), sem("xt_ready"), sem("y_stored"), sem("weights_loaded")
        before_ready = sem("before_ready")
        ld_bias, bias_split, bias_chain, bias_loaded = (sem(n) for n in ("ld_bias", "bias_split", "bias_chain", "bias_loaded"))
        gathered = [sem(f"gathered{g}") for g in range(NG)]
        x2_chain, gmv_ready, gln_ready, gr_ready, gx_ready, gT_done = (sem(n) for n in ("x2_chain", "gmv_ready", "gln_ready", "gr_ready", "gx_ready", "gT_done"))
        h0_ready, h_ready, sq0_ready, sq_ready, ss_done, rln_ready, rs_ready, hs_ready = (
            sem(n) for n in ("h0_ready", "h_ready", "sq0_ready", "sq_ready", "ss_done", "rln_ready", "rs_ready", "hs_ready"))
        c_done, cmax_ready, csub_ready, cexp_ready, crec_ready, att_ready = (
            sem(n) for n in ("c_done", "cmax_ready", "csub_ready", "cexp_ready", "crec_ready", "att_ready"))
        asum_done, aln_ready, ar_ready, attn_ready, gh_done, gx_done = (sem(n) for n in ("asum_done", "aln_ready", "ar_ready", "attn_ready", "gh_done", "gx_done"))
        hnb_ready, tr_ready, tz_ready, u_ready, un_ready, nn_ready, dd_ready, e_ready = (
            sem(n) for n in ("hnb_ready", "tr_ready", "tz_ready", "u_ready", "un_ready", "nn_ready", "dd_ready", "e_ready"))
        hb_done, x3_chain, gmv3_ready, gln3_ready, gr3_ready, x3_ready, x3T_done, x3T_ready, logit_done, logit_ready = (
            sem(n) for n in ("hb_done", "x3_chain", "gmv3_ready", "gln3_ready", "gr3_ready", "x3_ready", "x3T_done", "x3T_ready", "logit_done", "logit_ready"))
        fin_ready = sem("fin_ready")

        def route_vector(dve, l):
            L = layers[l]
            count = [0]

            def link(ins):
                count[0] += 1
                ins.then_inc(chain, 1)
                dve.wait_ge(chain, L.chain0 + count[0])
            link(nc.vector.tensor_reduce(amax[:], aff_all[:], X, ALU.max))
            peak = amax[:].unsqueeze(2).broadcast_to([P, B, E])
            if l == 0:
                nc.vector.tensor_scalar(share[:], amax[:], -1.0, None, ALU.mult).then_inc(share_in, 1)
            else:
                nc.vector.tensor_tensor(eg[:], aff_all[:], peak, ALU.subtract).then_inc(share_in, 1)
            link(nc.vector.tensor_tensor(apick[:], aff_all[:], peak, ALU.is_ge))
            link(nc.vector.tensor_tensor(apick[:], apick[:], consts[:, C_TIE:C_TIE + B * E].rearrange("p (b e) -> p b e", e=E), ALU.mult))
            link(nc.vector.tensor_reduce(amax[:], apick[:], X, ALU.max))
            nc.vector.tensor_tensor(onehot[:], apick[:], peak, ALU.is_equal).then_inc(onehot_ready, 1)
            dve.wait_ge(total_done, L.one0 + 1)
            link(nc.vector.tensor_copy(tot[:], bank[1][:, 0:B * E].rearrange("p (b e) -> p e b", e=E)))
            link(nc.vector.tensor_tensor_scan(cum[:], consts[:, C_RESET:C_RESET + E * B], tot[:].rearrange("p e b -> p (e b)"), 0.0, ALU.mult, ALU.add))
            link(nc.vector.tensor_scalar(n_pad[:], cum[:].rearrange("p (e b) -> p e b", b=B)[:, :, B - 1:B].rearrange("p e b -> p (e b)"), P - 1.0, None, ALU.add))
            nc.vector.tensor_tensor(before_b[:], cum[:], tot[:].rearrange("p e b -> p (e b)"), ALU.subtract).then_inc(before_ready, 1)
            link(nc.vector.tensor_scalar(n_tile_i[:], n_pad[:], 7, None, ALU.arith_shift_right))
            dve.wait_ge(before_ready, L.one0 + 1)
            dve.wait_ge(rank_done, L.one0 + 1)
            nc.vector.tensor_tensor(pos_be[:], bank[0][:, 0:B * E].rearrange("p (b e) -> p b e", e=E), before_b[:].rearrange("p (e b) -> p b e", b=B),
                                    ALU.add)
            link(nc.vector.tensor_copy(n_tile[:], n_tile_i[:]))
            link(nc.vector.tensor_tensor_scan(tile_end[:], ones_e[:], n_tile[:], 0.0, ALU.mult, ALU.add))
            link(nc.vector.scalar_tensor_tensor(base[:], n_tile[:], -1.0, tile_end[:], ALU.mult, ALU.add))
            link(nc.vector.scalar_tensor_tensor(pos_be[:], base[:].unsqueeze(1).broadcast_to([P, B, E]), float(P), pos_be[:], ALU.mult, ALU.add))
            link(nc.vector.tensor_tensor(pos_be[:], pos_be[:], onehot[:], ALU.mult))
            link(nc.vector.tensor_reduce(pos_f[:], pos_be[:], X, ALU.add))
            nc.vector.tensor_copy(pos[:], pos_f[:]).then_inc(pos_ready, 1)
            link(nc.vector.tensor_tensor(tile_cmp[:], tile_end[:].unsqueeze(1).broadcast_to([P, TILES, E]),
                                         consts[:, C_JOTA:C_JOTA + TILES * E].rearrange("p (j e) -> p j e", e=E), ALU.is_le))
            link(nc.vector.tensor_reduce(tile_e[:], tile_cmp[:], X, ALU.add))
            nc.vector.tensor_scalar(tile_tab[:], tile_e[:], E - 1.0, None, ALU.min).then_inc(tab_ready, 1)
            dve.wait_ge(share_exp, L.one0 + 1)
            if l == 0:
                link(nc.vector.tensor_scalar(share[:], share[:], 1.0, None, ALU.add))
            else:
                link(nc.vector.tensor_reduce(share[:], eg[:], X, ALU.add))
            nc.vector.reciprocal(share[:], share[:]).then_inc(share_ready, 1)
            assert count[0] == ROUTE_LINKS

        def route_tensor(pe, l):
            L = layers[l]
            pe.wait_ge(onehot_ready, L.one0 + 1)
            flat = onehot[:].rearrange("p b e -> p (b e)")
            nc.tensor.matmul(bank[1][:, 0:B * E], ones_b[:], flat, start=True, stop=True).then_inc(total_done, 1)
            nc.tensor.matmul(bank[0][:, 0:B * E], upper[:], flat, start=True, stop=True).then_inc(rank_done, 1)

        def route_scalar(act, l):
            L = layers[l]
            act.wait_ge(share_in, L.one0 + 1)
            t = share if l == 0 else eg
            nc.scalar.activation(t[:], t[:], ACT.Exp).then_inc(share_exp, 1)

        def scatter(pool, l):
            L = layers[l]
            pool.wait_ge(pos_ready, L.one0 + 1)
            pool.wait_ge(zeroed, 32)
            for b in range(B):
                nc.gpsimd.indirect_dma_start(xs_dram[l], bass.IndirectOffsetOnAxis(pos[:, b:b + 1], 0), xh_all[:, b, :], None).then_inc(scattered, 16)

        def gather(pool, l):
            L = layers[l]
            pool.wait_ge(y_stored, 16 * len(STORES) * (l + 1))
            for b in range(B):
                nc.gpsimd.indirect_dma_start(f_all[:, b, :], None, ys_dram[l], bass.IndirectOffsetOnAxis(pos[:, b:b + 1], 0)).then_inc(gathered[b // GROUP], 16)

        EARLY = 8
        STORES = ((0, 8), (8, 16), (16, 20), (20, TILES))

        def span(dram, lo, hi):
            return dram[lo * P:hi * P, :].rearrange("(j p) d -> p j d", p=P)

        def load_experts(sp, l):
            if l:
                sp.wait_ge(down_done, TILES)
                for g in range(NG):
                    sp.wait_ge(gathered[g], 16 * GROUP)
            for half in range(2):
                lo, hi = half * E // 2, (half + 1) * E // 2
                sp.dma_start(weights[:, lo:hi, :], a[f"wf{l}"][:, lo:hi, :]).then_inc(weights_loaded, 16)
            sp.wait_ge(bias_split, 3)
            for k in range(3):
                sp.dma_start(bias3[k:k + 1, :], bias_part[:, l, k, :]).then_inc(bias_loaded, 16)

        def experts_sync(sp, l):
            L = layers[l]
            sp.wait_ge(scattered, L.scatter0 + 16 * B)
            sp.dma_start(tile_rows[:, 0:EARLY, :], span(xs_dram[l], 0, EARLY)).then_inc(tiles_early, 16)
            sp.dma_start(tile_rows[:, EARLY:, :], span(xs_dram[l], EARLY, TILES)).then_inc(tiles_late, 16)
            for lo, hi in STORES:
                sp.wait_ge(y_ready, L.tile0 + hi)
                sp.dma_start(span(ys_dram[l], lo, hi), tile_rows[:, lo:hi, :]).then_inc(y_stored, 16)

        def hidden(p, c):
            return bank[2 + 2 * p + c // 2][:, c % 2 * P:(c % 2 + 1) * P]

        def expert_of(eng, j):
            return eng.value_load(tile_tab[0:1, bass.ds(j, 1)], min_val=0, max_val=E - 1)

        def experts_tensor(pe, l):
            L = layers[l]

            def rows_turn(j, p):
                pe.wait_ge(xt_ready, L.tile0 + (j + 1))
                nc.tensor.transpose(bank[p][:, 0:P], xt[p][:], ident).then_inc(xtT_done, 1)

            def step(j, q):
                fixed = isinstance(j, int)
                p = q % 2
                if not fixed or j + 1 < TILES:
                    rows_turn(j + 1, 1 - p)
                if not fixed or j < TILES:
                    pe.wait_ge(xtT_ready, L.tile0 + (j + 1))
                    for c in range(FC):
                        last = nc.tensor.matmul(hidden(p, c), w_up[q][:, c * P:(c + 1) * P], xtT[p][:], start=True, stop=True)
                        if c % 2:
                            last.then_inc(up_done, 1)
                if not fixed or j >= 1:
                    e = expert_of(pe, j - 1)
                    y = bank[6 + 1 - p][:, 0:D]
                    need(pe, y_ready, L.tile0 + (j - 2))
                    nc.tensor.matmul(y, ones3[:], bias3[:, bass.ds(e * D, D)], start=True, stop=False)
                    pe.wait_ge(hid_ready, L.tile0 + j)
                    for c in range(FC):
                        last = nc.tensor.matmul(y, hidT[1 - p][:, c, :],
                                                weights[:, bass.ds(e, 1), W_2 + c * D:W_2 + (c + 1) * D].rearrange("p o f -> p (o f)"),
                                                start=False, stop=c == FC - 1)
                    last.then_inc(down_done, 1)
            pe.wait_ge(tab_ready, L.one0 + 1)
            pe.wait_ge(weights_loaded, 32 * (l + 1))
            pe.wait_ge(bias_loaded, 48 * (l + 1))
            rows_turn(0, 0)
            skewed(pe, 0, (3, 19), TILES, step, unroll=4)

        def experts_gpsimd(pool, l):
            L = layers[l]

            def step(j, p):
                need(pool, xtT_done, L.tile0 + (j - 1))
                src = tile_rows[:, bass.ds(j, 1), :].rearrange("p o d -> p (o d)")
                nc.gpsimd.tensor_copy(xt[p][:], src).then_inc(xt_ready, 1)
            pool.wait_ge(tiles_early, 16 * (l + 1))
            skewed(pool, 0, (2, EARLY), EARLY - 1, step)
            pool.wait_ge(tiles_late, 16 * (l + 1))
            skewed(pool, EARLY, (EARLY, 22), TILES - 1, step)

        def experts_scalar(act, l):
            L = layers[l]

            def step(j, q):
                p = q % 2
                for c in range(FC):
                    act.wait_ge(up_done, j * 2 + (2 * L.tile0 + c // 2 + 1))
                    last = nc.scalar.activation(hidT[p][:, c, :], hidden(p, c), ACT.Silu if l else ACT.Relu, bias=w_up[q][:, W_B1 + c:W_B1 + c + 1])
                last.then_inc(hid_ready, 1)
            skewed(act, 0, (2, 22), TILES - 1, step, unroll=4)

        def experts_vector(dve, l):
            L = layers[l]

            def weights_up(j, q):
                e = expert_of(dve, j)
                need(dve, hid_ready, L.tile0 + (j - 3))
                nc.vector.tensor_copy(w_up[q][:], weights[:, bass.ds(e, 1), 0:W_UP].rearrange("p o f -> p (o f)")).then_inc(w_up_ready, 1)

            def rows_turned(j, q):
                p = q % 2
                dve.wait_ge(xtT_done, L.tile0 + (j + 1))
                if l == 0:
                    dve.wait_ge(w_up_ready, L.tile0 + (j + 1))
                    nc.vector.tensor_scalar(xtT[p][:], bank[p][:, 0:P], w_up[q][:, W_G:W_G + 1], w_up[q][:, W_B:W_B + 1], ALU.mult, ALU.add).then_inc(xtT_ready, 1)
                else:
                    nc.vector.tensor_copy(xtT[p][:], bank[p][:, 0:P]).then_inc(xtT_ready, 1)

            def step(j, q):
                fixed = isinstance(j, int)
                if not fixed or j + 1 < TILES:
                    rows_turned(j + 1, (q + 1) % 4)
                if not fixed or j >= 1:
                    dve.wait_ge(down_done, L.tile0 + j)
                    nc.vector.tensor_copy(tile_rows[:, bass.ds(j - 1, 1), :].rearrange("p o d -> p (o d)"), bank[6 + (q + 1) % 2][:, 0:D]).then_inc(y_ready, 1)
                if not fixed or j + 2 < TILES:
                    weights_up(j + 2, (q + 2) % 4)
            dve.wait_ge(weights_loaded, 32 * (l + 1))
            weights_up(0, 0)
            weights_up(1, 1)
            rows_turned(0, 0)
            skewed(dve, 0, (2, 18), TILES, step, unroll=4)

        SLOT_MAIN = (4, 12)

        MAIN = (4, 12)
        CTX_BANKS = (4, 5, 7)
        block = ctx.enter_context(nc.Block())

        @block.sync
        def _(sp):
            sp.dma_start(ctxT_all[:], a["ctxT_all"]).then_inc(ld_const, 16)
            sp.dma_start(w0[:], a["w0"]).then_inc(ld_const, 16)
            sp.dma_start(vecs[:], a["vecs"]).then_inc(ld_const, 16)
            sp.dma_start(consts[:], a["consts"]).then_inc(ld_const, 16)
            sp.dma_start(x_all[:, 0:4, :], a["x"][0:4].rearrange("b s d -> s b d")).then_inc(ld_x, 16)
            sp.dma_start(x_all[:, 4:B, :], a["x"][4:B].rearrange("b s d -> s b d")).then_inc(ld_x, 16)
            sp.dma_start(gates[:], a["gates"]).then_inc(ld_w1, 16)
            sp.dma_start(w1[:], a["w1"]).then_inc(ld_w1, 16)
            sp.dma_start(gru[:], a["gru"]).then_inc(ld_w1, 16)
            sp.wait_ge(v_ready, NG)
            sp.wait_ge(rows_cleared, 1)
            for i, (c, h, key, row, n) in enumerate(PIECES):
                sp.dma_start(v_rows[row:row + n, i, :, :], v_all[key:key + n, h, :, :]).then_inc(v_placed[min(c // 4, NT - 1)], 16)
            sp.wait_ge(memset_ready, 9)
            for l in range(2):
                sp.dma_start(xs_dram[l].rearrange("(j p) d -> p j d", p=P), zero[:].unsqueeze(1).broadcast_to([P, TILES, D])).then_inc(zeroed, 16)
            load_experts(sp, 0)
            experts_sync(sp, 0)
            load_experts(sp, 1)
            experts_sync(sp, 1)
            for g in range(NG):
                sp.wait_ge(fin_ready, g + 1)
                sp.dma_start(out[g * GROUP:(g + 1) * GROUP].rearrange("b s d -> s b d"), f_all[:, g * GROUP:(g + 1) * GROUP, :]).then_inc(stored, 16)
            sp.wait_ge(stored, 16 * NG)

        @block.gpsimd
        def _(pool):
            nc.gpsimd.memset(v_all[:], 1.0).then_inc(memset_ready, 1)
            nc.gpsimd.memset(zero3[:], 0.0)
            nc.gpsimd.memset(ones3[:], 1.0).then_inc(memset_ready, 1)
            nc.gpsimd.memset(eps_ln[:], LN_EPS).then_inc(memset_ready, 1)
            nc.gpsimd.memset(eps_rms[:], RMS_EPS).then_inc(memset_ready, 1)
            nc.gpsimd.memset(ones_b[:], 1.0).then_inc(memset_ready, 1)
            nc.gpsimd.memset(ones_f[:], 1.0).then_inc(memset_ready, 1)
            nc.gpsimd.memset(ones_e[:], 1.0).then_inc(memset_ready, 1)
            nc.gpsimd.memset(zero[:], 0.0).then_inc(memset_ready, 1)
            nc.gpsimd.memset(att[0][:], ATT_EPS)
            nc.gpsimd.memset(att[1][:], ATT_EPS).then_inc(memset_ready, 1)
            nc.gpsimd.memset(v_rows[:], 0.0).then_inc(rows_cleared, 1)
            pool.wait_ge(ld_const, 64)
            pool.wait_ge(kT_ready, 3)
            pool.wait_ge(ld_rows, 32)
            pool.wait_ge(ld_x, 32)

            def step(b, p):
                need(pool, s_done, 3 * (b - 1))
                nc.gpsimd.tensor_tensor(
                    kblk[p][:], kT_all[:, bass.ds(b * M, M)].unsqueeze(1).broadcast_to([P, H, M]),
                    headmask.unsqueeze(2).broadcast_to([P, H, M]), ALU.mult).then_inc(kblk_ready, 1)

            def with_bias(b, p):
                need(pool, x1_ready, b - 1)
                nc.gpsimd.tensor_tensor(xbo[p][:], x_all[:, bass.ds(b, 1), :].rearrange("p o d -> p (o d)"), rows[:, R_BO:R_BO + D], ALU.add).then_inc(xbo_ready, 1)

            def residual(b, p):
                pool.wait_ge(xin_ready, b + 1)
                nc.gpsimd.tensor_tensor(res_all[:, bass.ds(b, 1), :].rearrange("p o d -> p (o d)"), x1[p][:], xin[p][:], ALU.add).then_inc(res_ready, 1)

            def both(t, p):
                if not isinstance(t, int) or t + 1 < B:
                    step(t + 1, 1 - p)
                if isinstance(t, int) and t == 0:
                    pool.wait_ge(ctxr_ready, 3)
                    nc.gpsimd.tensor_tensor(ctx_n[:], ctx_n[:], ctxT_all[:], ALU.mult).then_inc(ctxn_ready, 1)
                if not isinstance(t, int) or 0 <= t - 3 < B:
                    residual(t - 3, 1 - p)
                if not isinstance(t, int) or 0 <= t - 1 < B:
                    with_bias(t - 1, 1 - p)
            skewed(pool, -1, MAIN, B + 2, both)
            scatter(pool, 0)
            experts_gpsimd(pool, 0)
            gather(pool, 0)

            def slot_step(s, g):
                fixed = isinstance(s, int)
                p = g % 2
                if not fixed or 2 <= s + 1 < SLOT_STEPS:
                    g1 = (g + 1) % NG
                    if fixed and s + 1 < NG:
                        pool.wait_ge(h0_ready, s + 2)
                    else:
                        pool.wait_ge(h_ready, s - 2)
                    need(pool, ss_done, s)
                    nc.gpsimd.tensor_tensor(sq[1 - p][:], hT[:, g1 * G:(g1 + 1) * G], hT[:, g1 * G:(g1 + 1) * G], ALU.mult).then_inc(sq_ready, 1)
                if not fixed or 0 <= s - 1:
                    g0 = (g - 1) % NG
                    pool.wait_ge(nn_ready, s)
                    nc.gpsimd.tensor_tensor(dd[1 - p][:], hT[:, g0 * G:(g0 + 1) * G], nn[1 - p][:], ALU.subtract).then_inc(dd_ready, 1)
            skewed_groups(pool, 1, SLOT_MAIN, SLOT_STEPS, slot_step)
            pool.wait_ge(x3_ready, NG)
            scatter(pool, 1)
            experts_gpsimd(pool, 1)
            gather(pool, 1)

        @block.scalar
        def _(act):
            act.dma_start(mask_i, a["mask"].partition_broadcast(P)).then_inc(ld_ctx, 16)
            act.dma_start(rows[:], a["rows"].partition_broadcast(P)).then_inc(ld_rows, 16)
            act.dma_start(negp[:], a["negp"]).then_inc(ld_rows, 16)
            act.dma_start(bias_in[:], a["biases"]).then_inc(ld_bias, 16)
            act.preload_act_table_set("natural_log_exp_and_others")
            act.wait_ge(memset_ready, 9)
            act.wait_ge(ld_const, 64)
            nc.scalar.activation(ctx_n[:], ctxT_all[:], ACT.Square).then_inc(ctxsq_ready, 1)
            def rstd_of(b, mv_ready, mvt, ln_t, ln_sem, r_t, r_sem):
                act.wait_ge(mv_ready, b + 1)
                nc.scalar.activation(ln_t[:], mvt[:, 1:2], ACT.Ln, bias=eps_ln[:]).then_inc(ln_sem, 1)
                act.wait_ge(ln_sem, b + 1)
                nc.scalar.activation(r_t[:], ln_t[:], ACT.Exp, scale=-0.5).then_inc(r_sem, 1)

            def step(t, p):
                fixed = isinstance(t, int)
                before = not fixed or 0 <= t - 1 < B

                def turned(q):
                    n = (t - 1) * NT + q
                    slot, (lo, hi) = (1 - p + q) % 2, TURNS[q]
                    act.wait_ge(pT_done, n + 1)
                    need(act, pv_done, n - 1)
                    rows_q = CHUNK_ROWS[hi - 1]
                    if rows_q < P:
                        nc.scalar.copy(pT[slot][0:rows_q, hi - 1 - lo, :], bank[3 + slot][0:rows_q, (hi - 1 - lo) * S:(hi - lo) * S])
                        hi -= 1
                    nc.scalar.copy(pT[slot][:, 0:hi - lo, :], bank[3 + slot][:, 0:(hi - lo) * S].rearrange("p (i s) -> p i s", s=S)).then_inc(pT_ready, 1)

                def exponents(g):
                    h0, n = HEAD_GROUPS[g]
                    act.wait_ge(sub_ready, 3 * t + g + 1)
                    nc.scalar.activation(probs[p][:, h0:h0 + n, :], probs[p][:, h0:h0 + n, :], ACT.Exp).then_inc(exp_ready, 1)

                if fixed and t == B + 1:
                    act.wait_ge(oT_done, B)
                    nc.scalar.copy(oT[p][:], bank[0][:, 0:P]).then_inc(oT_ready, 1)
                if not fixed or 0 <= t + 1 < B:
                    act.wait_ge(xnT_done, t + 2)
                    nc.scalar.copy(xnT[1 - p][:], bank[6][:, 0:P]).then_inc(xnT_ready, 1)
                if before:
                    turned(0)
                if not fixed or 0 <= t - 4:
                    act.wait_ge(xinT_done, t - 3)
                    nc.scalar.copy(xinT[p][:], bank[7][:, 2 * P:3 * P]).then_inc(xinT_ready, 1)
                if before:
                    turned(1)
                if not fixed or 0 <= t < B:
                    exponents(0)
                if not fixed or 0 <= t - 4:
                    act.wait_ge(aff_done, t - 3)
                    nc.scalar.copy(aff_all[:, bass.ds(t - 4, 1), :].rearrange("p o e -> p (o e)"), bank[7][:, 3 * P:3 * P + E]).then_inc(aff_ready, 1)
                if not fixed or 0 <= t + 1 < B:
                    act.wait_ge(q_done, t + 2)
                    need(act, s_done, 3 * t)
                    nc.scalar.activation(qT[1 - p][:], bank[6][:, P:2 * P], ACT.Identity, scale=HD ** -0.5, bias=bq[:]).then_inc(q_ready, 1)
                if not fixed or 0 <= t < B:
                    exponents(1)
                if not fixed or 0 <= t - 2 < B - 1:
                    act.wait_ge(oT_done, t - 1)
                    nc.scalar.copy(oT[p][:], bank[7][:, 0:P]).then_inc(oT_ready, 1)
                if before:
                    turned(2)
                if not fixed or 0 <= t < B:
                    exponents(2)
                if not fixed or 0 <= t - 2 < B:
                    rstd_of(t - 2, mv1_ready, mv1[p], lnv1[p], ln1_ready, rstd1[p], r1_ready)
                if not fixed or 0 <= t - 3 < B:
                    rstd_of(t - 3, mv2_ready, mv2[1 - p], lnv2[1 - p], ln2_ready, rstd2[1 - p], r2_ready)
                if not fixed or t + 3 < B:
                    rstd_of(t + 3, lnx_mv, mv[1 - p], lnv[1 - p], lnx_ln, rstd[1 - p], lnx_r)
                if fixed and t == -1:
                    for c in range(3):
                        lo, hi = c * 512, min((c + 1) * 512, B * M)
                        act.wait_ge(ctxss_done, c + 1)
                        nc.scalar.activation(ctx_n[:, lo:hi], bank[CTX_BANKS[c]][:, 0:hi - lo], ACT.Ln, scale=1.0 / D, bias=eps_rms[:]).then_inc(ctxln_ready, 1)
                        act.wait_ge(ctxln_ready, c + 1)
                        nc.scalar.activation(ctx_n[:, lo:hi], ctx_n[:, lo:hi], ACT.Exp, scale=-0.5).then_inc(ctxr_ready, 1)
            skewed(act, -3, MAIN, B + 3, step)
            route_scalar(act, 0)

            def gru_inputs(b, p):
                act.wait_ge(vw_done, b + 1)
                nc.scalar.copy(vw_all[:, bass.ds(b, 1), :].rearrange("p o d -> p (o d)"), bank[2 + p][0:M, 0:GATES]).then_inc(vw_ready, 1)
            skewed(act, 0, (2, B), B - 1, gru_inputs)
            experts_scalar(act, 0)

            def group_rstd(g, mv_sem, ln_sem, r_sem):
                act.wait_ge(mv_sem, g + 1)
                nc.scalar.activation(gln[:, g, :], gmv[:, g, :, 1:2].rearrange("p b o -> p (b o)"), ACT.Ln, bias=eps_ln[:]).then_inc(ln_sem, 1)
                act.wait_ge(ln_sem, g + 1)
                nc.scalar.activation(gr[:, g, :], gln[:, g, :], ACT.Exp, scale=-0.5).then_inc(r_sem, 1)
            act.preload_act_table_set("natural_log_exp_and_others")
            def first_squares(g):
                act.wait_ge(h0_ready, g + 1)
                nc.scalar.activation(sq[g][:], hT[:, g * G:(g + 1) * G], ACT.Square).then_inc(sq0_ready, 1)
            group_rstd(0, gmv_ready, gln_ready, gr_ready)
            first_squares(0)
            group_rstd(1, gmv_ready, gln_ready, gr_ready)

            def slot_step(s, g):
                fixed = isinstance(s, int)
                p = g % 2
                now = not fixed or s < SLOT_STEPS
                before = not fixed or 0 <= s - 1
                act.preload_act_table_set("natural_log_exp_and_others")
                if now:
                    act.wait_ge(ss_done, s + 1)
                    nc.scalar.activation(rln[p][:], bank[0][:], ACT.Ln, scale=1.0 / D, bias=eps_rms[:]).then_inc(rln_ready, 1)
                    act.wait_ge(rln_ready, s + 1)
                    nc.scalar.activation(rln[p][:], rln[p][:], ACT.Exp, scale=-0.5).then_inc(rs_ready, 1)
                if fixed and s == 0:
                    first_squares(1)
                if before:
                    act.wait_ge(asum_done, s)
                    nc.scalar.activation(aln[1 - p][:], bank[3][0:M, :], ACT.Ln).then_inc(aln_ready, 1)
                    act.wait_ge(aln_ready, s)
                    nc.scalar.activation(aln[1 - p][:], aln[1 - p][:], ACT.Exp, scale=-1.0).then_inc(ar_ready, 1)
                if fixed and 2 <= s + 2 < NG:
                    group_rstd(s + 2, gmv_ready, gln_ready, gr_ready)
                act.preload_act_table_set("exp_and_others")
                if before:
                    act.wait_ge(gx_done, 3 * s - 2)
                    nc.scalar.activation(tr[1 - p][:], bank[4][:], ACT.Tanh, scale=0.5, bias=brz[:, 0:1]).then_inc(tr_ready, 1)
                if now:
                    act.wait_ge(csub_ready, s + 1)
                    nc.scalar.activation(ex[p][:], ex[p][:], ACT.Exp).then_inc(cexp_ready, 1)
                if before:
                    act.wait_ge(gx_done, 3 * s - 1)
                    nc.scalar.activation(tz[1 - p][:], bank[5][:], ACT.Tanh, scale=0.5, bias=brz[:, 1:2]).then_inc(tz_ready, 1)
                    act.wait_ge(un_ready, s)
                    nc.scalar.activation(nn[1 - p][:], u[1 - p][:], ACT.Tanh, bias=vecs[:, V_BIH + 2:V_BIH + 3]).then_inc(nn_ready, 1)
            skewed_groups(act, 0, SLOT_MAIN, SLOT_STEPS, slot_step)
            act.preload_act_table_set("natural_log_exp_and_others")
            for g in range(2):
                group_rstd(g, gmv3_ready, gln3_ready, gr3_ready)
            for g in range(NG):
                act.wait_ge(x3T_done, g + 1)
                need(act, logit_done, g - 1)
                nc.scalar.copy(x3T[g % 2][:], bank[g][:]).then_inc(x3T_ready, 1)
                if g + 2 < NG:
                    group_rstd(g + 2, gmv3_ready, gln3_ready, gr3_ready)
            route_scalar(act, 1)
            experts_scalar(act, 1)

        @block.vector
        def _(dve):
            dve.wait_ge(ld_ctx, 16)
            nc.vector.tensor_scalar(mask_f, mask_i, 0.0, None, ALU.not_equal).then_inc(mask_ready, 1)
            dve.wait_ge(ld_const, 64)
            dve.wait_ge(ld_rows, 32)
            dve.wait_ge(mask_ready, 1)
            nc.vector.tensor_scalar(neg3[:], mask_f[0:3, :], 0.0, negp[:], ALU.is_equal, ALU.mult).then_inc(neg_ready, 1)
            nc.vector.tensor_scalar(bq[:], vecs[:, V_BQ:V_BQ + 1], HD ** -0.5, None, ALU.mult).then_inc(small_ready, 1)
            nc.vector.tensor_copy(upper[:], consts[:, C_UPPER:C_UPPER + P]).then_inc(consts2_ready, 1)
            nc.vector.tensor_tensor(brz[:], vecs[:, V_BIH:V_BIH + 2], vecs[:, V_BHH:V_BHH + 2], ALU.add).then_inc(consts2_ready, 1)
            nc.vector.tensor_scalar(bhn[:], vecs[:, V_BHH + 2:V_BHH + 3], 0.5, None, ALU.mult).then_inc(consts2_ready, 1)
            dve.wait_ge(consts2_ready, 3)
            nc.vector.tensor_scalar(brz[:], brz[:], 0.5, None, ALU.mult).then_inc(consts2_ready, 1)
            nc.vector.tensor_scalar(wslot[:], vecs[:, V_WSLOT:V_WSLOT + 1], D ** -0.5, None, ALU.mult).then_inc(small_ready, 1)
            for c in range(3):
                lo, hi = c * 512, min((c + 1) * 512, B * M)
                dve.wait_ge(kproj, c + 1)
                nc.vector.scalar_tensor_tensor(kT_all[:, lo:hi], bank[5 + c][:, 0:hi - lo], vecs[:, V_BK:V_BK + 1], mask_f[:, lo:hi],
                                               ALU.add, ALU.mult).then_inc(kT_ready, 1)
            dve.wait_ge(memset_ready, 9)
            for g in range(NG):
                dve.wait_ge(v_done, g + 1)
                nc.vector.tensor_tensor(
                    v_all[:, :, g * GROUP:(g + 1) * GROUP, 0:HD].rearrange("m h b c -> m b h c"),
                    bank[g][0:M, :].rearrange("m (b h c) -> m b h c", h=H, c=HD),
                    rows[0:M, R_BV:R_BV + D].rearrange("m (h c) -> m h c", c=HD).unsqueeze(1).broadcast_to([M, GROUP, H, HD]), ALU.add).then_inc(v_ready, 1)
            dve.wait_ge(small_ready, 2)
            dve.wait_ge(ld_x, 32)

            def normalise(dst, src, mv_t, r_t, ready):
                nc.vector.tensor_scalar(dst, src, mv_t[:, 0:1], r_t[:], ALU.subtract, ALU.mult).then_inc(ready, 1)

            def row(t, b):
                return t[:, bass.ds(b, 1), :].rearrange("p o d -> p (o d)")

            def step(t, p):
                fixed = isinstance(t, int)
                if not fixed or t + 3 < B:
                    nc.vector.bn_stats(st[1 - p][:], row(x_all, t + 3)).then_inc(lnx_st, 1)
                if not fixed or 0 <= t - 2 < B:
                    b = t - 2
                    acc = bank[5][:, 0:H * HV].rearrange("p (h c) -> p h c", c=HV)
                    dve.wait_ge(pv_done, NT * b + NT)
                    nc.vector.reciprocal(rden[p][:], acc[:, :, HD:HV].rearrange("p h c -> p (h c)")).then_inc(rden_ready, 1)
                if not fixed or t + 3 < B:
                    dve.wait_ge(lnx_st, t + 4)
                    nc.vector.memset(hold[:, 0:1], 0.0)
                    nc.vector.bn_aggr(mv[1 - p][:], st[1 - p][:]).then_inc(lnx_mv, 1)
                if not fixed or 0 <= t - 2 < B:
                    dve.wait_ge(rden_ready, b + 1)
                    need(dve, oT_done, b - 1)
                    nc.vector.tensor_tensor(o_sb[p][:].rearrange("p (h c) -> p h c", c=HD), acc[:, :, 0:HD],
                                            rden[p][:].unsqueeze(2).broadcast_to([P, H, HD]), ALU.mult).then_inc(o_ready, 1)
                def twice_normed():
                    dve.wait_ge(r2_ready, t - 3)
                    normalise(row(xh_all, t - 4), xin[p][:], mv2[p], rstd2[p], xh_ready)
                if not fixed or 0 <= t - 4 < B - 2:
                    twice_normed()
                if not fixed or 0 <= t + 2 < B:
                    dve.wait_ge(lnx_r, t + 3)
                    need(dve, xnT_done, t + 1)
                    normalise(xn[p][:], row(x_all, t + 2), mv[p], rstd[p], xn_ready)
                if not fixed or 0 <= t < B:
                    def scores(g):
                        h0, n = HEAD_GROUPS[g]
                        return bank[g][:, 0:n * M].rearrange("p (h m) -> p h m", m=M), smax[p][:, h0:h0 + n], probs[p][:, h0:h0 + n, :], n

                    def largest(g):
                        src, top, _, n = scores(g)
                        dve.wait_ge(s_done, 3 * t + g + 1)
                        nc.vector.tensor_reduce(top, src, X, ALU.max).then_inc(max_ready, 1)

                    def less(g):
                        src, top, dst, n = scores(g)
                        dve.wait_ge(max_ready, 3 * t + g + 1)
                        need(dve, pT_done, NT * (t - 1))
                        nc.vector.tensor_tensor(dst, src, top.unsqueeze(2).broadcast_to([P, n, M]), ALU.subtract).then_inc(sub_ready, 1)
                    largest(0)
                    less(0)
                    largest(1)
                    less(1)
                    largest(2)
                    less(2)
                if not fixed or 0 <= t - 2 < B:
                    b = t - 2
                    dve.wait_ge(wo_done, b + 1)
                    dve.wait_ge(xbo_ready, b + 1)
                    need(dve, res_ready, b - 1)
                    product = bank[0 if fixed and t == B + 1 else 7]
                    nc.vector.tensor_tensor(x1[p][:], product[:, P:2 * P], xbo[p][:], ALU.add).then_inc(x1_ready, 1)
                if not fixed or 0 <= t - 3 < B:
                    dve.wait_ge(r1_ready, t - 2)
                    normalise(xin[1 - p][:], x1[1 - p][:], mv1[1 - p], rstd1[1 - p], xin_ready)
                if not fixed or 0 <= t - 2 < B:
                    dve.wait_ge(x1_ready, t - 1)
                    nc.vector.bn_stats(st1[p][:], x1[p][:]).then_inc(st1_ready, 1)
                if not fixed or 0 <= t - 3 < B:
                    dve.wait_ge(xin_ready, t - 2)
                    nc.vector.bn_stats(st2[1 - p][:], xin[1 - p][:]).then_inc(st2_ready, 1)
                if not fixed or 0 <= t - 2 < B:
                    dve.wait_ge(st1_ready, t - 1)
                    nc.vector.memset(hold[:, 1:2], 0.0)
                    nc.vector.bn_aggr(mv1[p][:], st1[p][:]).then_inc(mv1_ready, 1)
                if not fixed or 0 <= t - 3 < B:
                    dve.wait_ge(st2_ready, t - 2)
                    nc.vector.memset(hold[:, 2:3], 0.0)
                    nc.vector.bn_aggr(mv2[1 - p][:], st2[1 - p][:]).then_inc(mv2_ready, 1)
                if fixed and B - 2 <= t - 4:
                    twice_normed()
            skewed(dve, -3, MAIN, B + 3, step)
            dve.wait_ge(aff_ready, B)
            route_vector(dve, 0)
            dve.wait_ge(ld_bias, 16)
            left = bias_in
            for k in range(3):
                nc.vector.tensor_copy(bias_part[:, :, k, :], left[:]).then_inc(bias_split, 1)
                if k < 2:
                    dve.wait_ge(bias_split, k + 1)
                    nc.vector.tensor_tensor(bias_left[:], left[:], bias_part[:, :, k, :], ALU.subtract).then_inc(bias_chain, 1)
                    dve.wait_ge(bias_chain, k + 1)
                    left = bias_left
            dve.wait_ge(abproj, 2)
            nc.vector.tensor_scalar(ab[:, 0:D], bank[3][:, 0:D], vecs[:, V_WIN:V_WIN + 1], None, ALU.mult).then_inc(ab_ready, 1)
            nc.vector.tensor_scalar(ab[:, D:], bank[4][:, 0:GATES], vecs[:, V_WIN:V_WIN + 1], None, ALU.mult).then_inc(ab_ready, 1)
            dve.wait_ge(ctxn_ready, 1)

            kq_flat = kq_all[:].rearrange("p b m -> p (b m)")
            for c in range(3):
                lo, hi = c * 512, min((c + 1) * 512, B * M)
                dve.wait_ge(kq_done, c + 1)
                nc.vector.tensor_scalar(kq_flat[:, lo:hi], bank[5 + c][:, 0:hi - lo], wslot[:], None, ALU.mult).then_inc(kq_ready, 1)

            def context_rows(b, p):
                need(dve, vw_done, b - 1)
                nc.vector.tensor_copy(ctxn[p][:], ctx_n[:, bass.ds(b * M, M)]).then_inc(ctxn_copied, 1)
            skewed(dve, 0, (2, B), B - 1, context_rows)
            experts_vector(dve, 0)

            def group_centre(g, src, chain, base_count, mv_sem, dst):
                for i in range(GROUP):
                    nc.vector.bn_stats(gst[:, g, i, :], src[:, i, :]).then_inc(chain, 1)
                dve.wait_ge(chain, base_count + GROUP)
                for i in range(GROUP):
                    last = nc.vector.bn_aggr(gmv[:, g, i, :], gst[:, g, i, :])
                last.then_inc(mv_sem, 1)
                dve.wait_ge(mv_sem, g + 1)
                nc.vector.tensor_tensor(dst, src, gmv[:, g, :, 0:1].broadcast_to([P, GROUP, D]), ALU.subtract).then_inc(chain, 1)

            def group_scale(g, chain, base_count, r_sem, dst, dst_sem):
                dve.wait_ge(chain, base_count + GROUP + 1)
                dve.wait_ge(r_sem, g + 1)
                nc.vector.tensor_tensor(dst, dst, gr[:, g, :].unsqueeze(2).broadcast_to([P, GROUP, D]), ALU.mult).then_inc(dst_sem, 1)

            XK = 1 + GROUP + 1

            def rows_in(g):
                gb = slice(g * GROUP, (g + 1) * GROUP)
                dve.wait_ge(gathered[g], 16 * GROUP)
                dve.wait_ge(share_ready, 1)
                dve.wait_ge(res_ready, B)
                for b in range(g * GROUP, (g + 1) * GROUP):
                    last = nc.vector.scalar_tensor_tensor(x2_all[:, b, :], f_all[:, b, :], share[:, b:b + 1], res_all[:, b, :], ALU.mult, ALU.add)
                last.then_inc(x2_chain, 1)
                dve.wait_ge(x2_chain, XK * g + 1)
                group_centre(g, x2_all[:, gb, :], x2_chain, XK * g + 1, gmv_ready, gx[g % 2][:])

            def rows_scaled(g):
                group_scale(g, x2_chain, XK * g + 1, gr_ready, gx[g % 2][:], gx_ready)

            def rows_out(g):
                gb = slice(g * GROUP, (g + 1) * GROUP)
                dve.wait_ge(hb_done, g + 1)
                nc.vector.tensor_tensor(x2_all[:, gb, :], x2_all[:, gb, :], bank[g][:].rearrange("p (b d) -> p b d", d=D), ALU.add).then_inc(x3_chain, 1)
                dve.wait_ge(x3_chain, XK * g + 1)
                group_centre(g, x2_all[:, gb, :], x3_chain, XK * g + 1, gmv3_ready, xh_all[:, gb, :])

            def rows_scaled_out(g):
                gb = slice(g * GROUP, (g + 1) * GROUP)
                group_scale(g, x3_chain, XK * g + 1, gr3_ready, xh_all[:, gb, :], x3_ready)

            def first_slots(g):
                dve.wait_ge(gT_done, g + 1)
                nc.vector.tensor_copy(hT[:, g * G:(g + 1) * G], bank[1][:]).then_inc(h0_ready, 1)

            def slot_step(s, g):
                fixed = isinstance(s, int)
                p = g % 2
                now = not fixed or 0 <= s < SLOT_STEPS
                before = not fixed or 0 <= s - 1 < SLOT_STEPS
                g0 = (g - 1) % NG
                h0 = hT[:, g0 * G:(g0 + 1) * G]
                bring = s + 2 if fixed and 2 <= s + 2 < NG else None
                if now:
                    dve.wait_ge(rs_ready, s + 1)
                    nc.vector.tensor_tensor(hs[p][:], hT[:, g * G:(g + 1) * G], rln[p][:], ALU.mult).then_inc(hs_ready, 1)
                if before:
                    dve.wait_ge(ar_ready, s)
                    nc.vector.tensor_tensor(attn[1 - p][:], att[1 - p][0:M, :], aln[1 - p][:], ALU.mult).then_inc(attn_ready, 1)
                if bring:
                    rows_in(bring)
                if now:
                    dve.wait_ge(c_done, s + 1)
                    sc = bank[2][0:M, :].rearrange("m (b s) -> m b s", s=S)
                    nc.vector.tensor_reduce(cmax[p][:], sc, X, ALU.max).then_inc(cmax_ready, 1)
                    dve.wait_ge(cmax_ready, s + 1)
                    nc.vector.tensor_tensor(ex[p][:], sc, cmax[p][:].unsqueeze(2).broadcast_to([M, GROUP, S]), ALU.subtract).then_inc(csub_ready, 1)
                if bring:
                    rows_scaled(bring)
                if fixed and s == SLOT_STEPS:
                    rows_out(0)
                if before:
                    dve.wait_ge(tr_ready, s)
                    dve.wait_ge(hnb_ready, s)
                    nc.vector.scalar_tensor_tensor(u[1 - p][:], tr[1 - p][:], 1.0, hnb[1 - p][:], ALU.add, ALU.mult).then_inc(u_ready, 1)
                    dve.wait_ge(u_ready, s)
                    dve.wait_ge(gx_done, 3 * s)
                    nc.vector.tensor_tensor(u[1 - p][:], u[1 - p][:], bank[7][:], ALU.add).then_inc(un_ready, 1)
                if fixed and s == SLOT_STEPS:
                    rows_out(1)
                if now:
                    dve.wait_ge(cexp_ready, s + 1)
                    nc.vector.tensor_reduce(csum[p][:], ex[p][:], X, ALU.add).then_inc(crec_ready, 1)
                    dve.wait_ge(crec_ready, 2 * s + 1)
                    nc.vector.reciprocal(crec[p][:], csum[p][:]).then_inc(crec_ready, 1)
                    dve.wait_ge(crec_ready, 2 * s + 2)
                    nc.vector.tensor_tensor(att[p][0:M, :].rearrange("m (b s) -> m b s", s=S), ex[p][:], crec[p][:].unsqueeze(2).broadcast_to([M, GROUP, S]),
                                            ALU.mult).then_inc(att_ready, 1)
                if now:
                    dve.wait_ge(gh_done, s + 1)
                    nc.vector.tensor_scalar(hnb[p][:], bank[6][:], 0.5, bhn[:], ALU.mult, ALU.add).then_inc(hnb_ready, 1)
                if before:
                    dve.wait_ge(dd_ready, s)
                    dve.wait_ge(tz_ready, s)
                    nc.vector.scalar_tensor_tensor(dd[1 - p][:], tz[1 - p][:], 1.0, dd[1 - p][:], ALU.add, ALU.mult).then_inc(e_ready, 1)
                    dve.wait_ge(e_ready, s)
                    nc.vector.scalar_tensor_tensor(h0, dd[1 - p][:], 0.5, nn[1 - p][:], ALU.mult, ALU.add).then_inc(h_ready, 1)
                if bring:
                    first_slots(bring)
            rows_in(0)
            rows_scaled(0)
            first_slots(0)
            rows_in(1)
            rows_scaled(1)
            first_slots(1)
            skewed_groups(dve, 0, SLOT_MAIN, SLOT_STEPS, slot_step)

            rows_scaled_out(0)
            rows_out(2)
            rows_scaled_out(1)
            rows_out(3)
            rows_scaled_out(2)
            rows_scaled_out(3)
            for g in range(NG):
                dve.wait_ge(logit_done, g + 1)
                nc.vector.tensor_tensor(aff_all[:, g * GROUP:(g + 1) * GROUP, :], bank[g][:, 0:GROUP * E].rearrange("p (b e) -> p b e", e=E),
                                        rows[:, R_BG:R_BG + E].unsqueeze(1).broadcast_to([P, GROUP, E]), ALU.add).then_inc(logit_ready, 1)
            dve.wait_ge(logit_ready, NG)
            route_vector(dve, 1)
            experts_vector(dve, 1)
            for g in range(NG):
                gb = slice(g * GROUP, (g + 1) * GROUP)
                dve.wait_ge(gathered[g], 2 * 16 * GROUP)
                dve.wait_ge(share_ready, 2)
                for b in range(g * GROUP, (g + 1) * GROUP):
                    last = nc.vector.scalar_tensor_tensor(f_all[:, b, :], f_all[:, b, :], share[:, b:b + 1], x2_all[:, b, :], ALU.mult, ALU.add)
                last.then_inc(fin_ready, 1)

        @block.tensor
        def _(pe):
            pe.wait_ge(ld_const, 64)
            for c in range(3):
                lo, hi = c * 512, min((c + 1) * 512, B * M)
                nc.tensor.matmul(bank[5 + c][:, 0:hi - lo], w0[:, 1, :], ctxT_all[:, lo:hi], start=True, stop=True).then_inc(kproj, 1)
            for b in range(B):
                ins = nc.tensor.matmul(bank[b // GROUP][0:M, b % GROUP * D:(b % GROUP + 1) * D], ctxT_all[:, b * M:(b + 1) * M], w0[:, 2, :], start=True, stop=True)
                if b % GROUP == GROUP - 1:
                    ins.then_inc(v_done, 1)
            pe.wait_ge(ctxsq_ready, 1)
            pe.wait_ge(kT_ready, 3)
            for c in range(3):
                lo, hi = c * 512, min((c + 1) * 512, B * M)
                nc.tensor.matmul(bank[CTX_BANKS[c]][:, 0:hi - lo], ones_f[:], ctx_n[:, lo:hi], start=True, stop=True).then_inc(ctxss_done, 1)
            pe.wait_ge(neg_ready, 1)
            pe.wait_ge(kT_ready, 3)
            pe.wait_ge(v_ready, NG)
            pe.wait_ge(ld_w1, 48)

            def p_turn(b, par, q):
                n = b * NT + q
                lo, hi = TURNS[q]
                need(pe, pT_ready, n - 1)
                if isinstance(b, int) and n == 1:
                    pe.wait_ge(ctxln_ready, 3)
                flat = probs[par][:].rearrange("p h m -> p (h m)")
                for c in range(lo, hi):
                    last = nc.tensor.transpose(bank[3 + (par + q) % 2][0:CHUNK_ROWS[c], (c - lo) * S:(c - lo + 1) * S], flat[:, c * P:c * P + CHUNK_ROWS[c]], ident)
                last.then_inc(pT_done, 1)

            def p_value(b, par, q):
                n = b * NT + q
                lo, hi = TURNS[q]
                if q == 0:
                    need(pe, o_ready, b)
                    nc.tensor.matmul(bank[5][:, 0:H * HV], ones3[:], zero3[:], start=True, stop=False)
                pe.wait_ge(pT_ready, n + 1)
                if isinstance(b, int) and b == 0:
                    pe.wait_ge(v_placed[q], 16 * sum(len(CHUNK_PIECES[c]) for c in range(lo, hi)))
                for c in range(lo, hi):
                    own = CHUNK_PIECES[c]
                    h, count, rows_c = PIECES[own[0]][1], len(own), CHUNK_ROWS[c]
                    last = nc.tensor.matmul(bank[5][:, h * HV:(h + count) * HV].rearrange("p (h c) -> p h c", c=HV), pT[(par + q) % 2][0:rows_c, c - lo, :],
                                            v_rows[0:rows_c, own[0]:own[-1] + 1, bass.ds(b, 1), :].rearrange("p i o c -> p (i o) c"),
                                            start=False, stop=c == CHUNKS - 1)
                last.then_inc(pv_done, 1)

            def step(t, p):
                fixed = isinstance(t, int)
                now = not fixed or 0 <= t < B
                before = not fixed or 0 <= t - 1 < B
                after = not fixed or 0 <= t + 1 < B
                old = not fixed or 0 <= t - 2 < B
                oldest = not fixed or 0 <= t - 4
                last_output = fixed and t == B + 1

                def scores(g):
                    h0, n = HEAD_GROUPS[g]
                    need(pe, sub_ready, 3 * (t - 1) + g + 1)
                    dst = bank[g][:, 0:n * M]
                    nc.tensor.matmul(dst, qT[p][:], kblk[p][:, h0:h0 + n, :].rearrange("p h m -> p (h m)"), start=True, stop=False)
                    nc.tensor.matmul(dst.rearrange("p (h m) -> p h m", m=M), ones3[:], neg3[:, bass.ds(t * M, M)].unsqueeze(1).broadcast_to([3, n, M]),
                                     start=False, stop=True).then_inc(s_done, 1)
                if last_output:
                    pe.wait_ge(o_ready, B)
                    pe.wait_ge(sub_ready, 3 * B)
                    nc.tensor.transpose(bank[0][:, 0:P], o_sb[p][:], ident).then_inc(oT_done, 1)
                if now:
                    pe.wait_ge(q_ready, t + 1)
                    pe.wait_ge(kblk_ready, t + 1)
                    scores(0)
                if after:
                    pe.wait_ge(xn_ready, t + 2)
                    need(pe, q_ready, t + 1)
                    nc.tensor.transpose(bank[6][:, 0:P], xn[1 - p][:], ident).then_inc(xnT_done, 1)
                if before:
                    pe.wait_ge(exp_ready, 3 * t - 1)
                    p_turn(t - 1, 1 - p, 0)
                if oldest:
                    pe.wait_ge(xin_ready, t - 3)
                    pe.wait_ge(x1_ready, min(t - 2, B) if fixed else t - 2)
                    if fixed and not old:
                        need(pe, aff_ready, t - 4)
                    nc.tensor.transpose(bank[7][:, 2 * P:3 * P], xin[p][:], ident).then_inc(xinT_done, 1)
                if now:
                    scores(1)
                if last_output:
                    pe.wait_ge(oT_ready, B)
                    nc.tensor.matmul(bank[0][:, P:2 * P], oT[p][:], w0[:, 3, :], start=True, stop=True).then_inc(wo_done, 1)
                if before:
                    pe.wait_ge(exp_ready, 3 * t)
                    p_turn(t - 1, 1 - p, 1)
                    p_value(t - 1, 1 - p, 0)
                if oldest:
                    pe.wait_ge(xinT_ready, t - 3)
                    nc.tensor.matmul(bank[7][:, 3 * P:3 * P + E], xinT[p][:], gates[:, 0, :], start=True, stop=True).then_inc(aff_done, 1)
                if after:
                    pe.wait_ge(xnT_ready, t + 2)
                    nc.tensor.matmul(bank[6][:, P:2 * P], w0[:, 0, :], xnT[1 - p][:], start=True, stop=True).then_inc(q_done, 1)
                if now:
                    scores(2)
                if old and not last_output:
                    pe.wait_ge(o_ready, t - 1)
                    need(pe, aff_ready, t - 3)
                    if not oldest:
                        need(pe, x1_ready, t - 2)
                    nc.tensor.transpose(bank[7][:, 0:P], o_sb[p][:], ident).then_inc(oT_done, 1)
                if before:
                    p_turn(t - 1, 1 - p, 2)
                    p_value(t - 1, 1 - p, 1)
                if old and not last_output:
                    pe.wait_ge(oT_ready, t - 1)
                    nc.tensor.matmul(bank[7][:, P:2 * P], oT[p][:], w0[:, 3, :], start=True, stop=True).then_inc(wo_done, 1)
                if before:
                    p_value(t - 1, 1 - p, 2)
            skewed(pe, -1, MAIN, B + 3, step)
            pe.wait_ge(memset_ready, 9)
            pe.wait_ge(consts2_ready, 4)
            route_tensor(pe, 0)
            nc.tensor.matmul(bank[3][:, 0:D], w1[:, 1, :], w1[:, 0, :], start=True, stop=True).then_inc(abproj, 1)
            nc.tensor.matmul(bank[4][:, 0:GATES], w1[:, 2, :], gru[:, 0, :], start=True, stop=True).then_inc(abproj, 1)
            pe.wait_ge(ab_ready, 2)

            pe.wait_ge(ctxn_ready, 1)
            for c in range(3):
                lo, hi = c * 512, min((c + 1) * 512, B * M)
                nc.tensor.matmul(bank[5 + c][:, 0:hi - lo], ab[:, 0:D], ctx_n[:, lo:hi], start=True, stop=True).then_inc(kq_done, 1)

            def gru_inputs(b, p):
                pe.wait_ge(ctxn_copied, b + 1)
                need(pe, vw_ready, b - 1)
                nc.tensor.matmul(bank[2 + p][0:M, 0:GATES], ctxn[p][:], ab[:, D:], start=True, stop=True).then_inc(vw_done, 1)
            skewed(pe, 0, (2, B), B - 1, gru_inputs)
            pe.wait_ge(vw_ready, B)
            pe.wait_ge(kq_ready, 3)
            pe.wait_ge(pos_ready, 1)
            experts_tensor(pe, 0)
            pe.wait_ge(y_ready, TILES)

            def turn_in(g):
                pe.wait_ge(gx_ready, g + 1)
                need(pe, h0_ready, g)
                for i in range(GROUP):
                    last = nc.tensor.transpose(bank[1][:, i * P:(i + 1) * P], gx[g % 2][:, i, :], ident)
                last.then_inc(gT_done, 1)

            def slot_step(s, g):
                fixed = isinstance(s, int)
                p = g % 2
                now = not fixed or 0 <= s < SLOT_STEPS
                before = not fixed or 0 <= s - 1 < SLOT_STEPS
                g0 = (g - 1) % NG
                cols = lambda i: slice(i * S, (i + 1) * S)
                if not fixed or 0 < s < SLOT_STEPS:
                    square_sums(s, p)
                if before:
                    h0 = hT[:, g0 * G:(g0 + 1) * G]
                    need(pe, hnb_ready, s - 1)
                    nc.tensor.matmul(bank[6][:], gru[:, 1, 2 * D:], h0, start=True, stop=True).then_inc(gh_done, 1)
                    pe.wait_ge(att_ready, s)
                    nc.tensor.matmul(bank[3][0:M, :], ones_f[0:M + 1, 0:M], att[1 - p][:], start=True, stop=True).then_inc(asum_done, 1)
                    need(pe, tz_ready, s - 1)
                    nc.tensor.matmul(bank[4][:], gru[:, 1, 0:D], h0, start=True, stop=False)
                    nc.tensor.matmul(bank[5][:], gru[:, 1, D:2 * D], h0, start=True, stop=False)
                if fixed and s == SLOT_STEPS:
                    for done in range(3):
                        turn_back(done)
                if now:
                    pe.wait_ge(hs_ready, s + 1)
                    need(pe, csub_ready, s)
                    for i in range(GROUP):
                        last = nc.tensor.matmul(bank[2][0:M, cols(i)], kq_all[:, g * GROUP + i, :], hs[p][:, cols(i)], start=True, stop=True)
                    last.then_inc(c_done, 1)
                if before:
                    pe.wait_ge(attn_ready, s)
                    need(pe, un_ready, s - 1)
                    for k, bk in enumerate((4, 5, 7)):
                        for i in range(GROUP):
                            last = nc.tensor.matmul(bank[bk][:, cols(i)], vw_all[:, g0 * GROUP + i, k * D:(k + 1) * D], attn[1 - p][:, cols(i)],
                                                    start=bk == 7, stop=bk == 7 or i == GROUP - 1)
                        last.then_inc(gx_done, 1)
                if fixed and 2 <= s + 2 < NG:
                    turn_in(s + 2)

            def turn_back(g):
                pe.wait_ge(h_ready, SLOT_STEPS - NG + g + 1)
                if g == 0:
                    pe.wait_ge(csub_ready, SLOT_STEPS)
                    pe.wait_ge(rln_ready, SLOT_STEPS)
                if g == 3:
                    pe.wait_ge(aln_ready, SLOT_STEPS)
                for i in range(GROUP):
                    last = nc.tensor.transpose(bank[g][:, i * P:(i + 1) * P], hT[:, (g * GROUP + i) * S:(g * GROUP + i + 1) * S], ident)
                last.then_inc(hb_done, 1)
            def square_sums(s, p):
                if isinstance(s, int) and s < 2:
                    pe.wait_ge(sq0_ready, s + 1)
                else:
                    pe.wait_ge(sq_ready, s - 1)
                need(pe, rln_ready, s)
                nc.tensor.matmul(bank[0][:], ones_f[:], sq[p][:], start=True, stop=True).then_inc(ss_done, 1)
            turn_in(0)
            square_sums(0, 0)
            turn_in(1)
            skewed_groups(pe, 0, SLOT_MAIN, SLOT_STEPS, slot_step)

            turn_back(3)

            def rows_turn_out(g):
                pe.wait_ge(x3_ready, g + 1)
                for i in range(GROUP):
                    last = nc.tensor.transpose(bank[g][:, i * P:(i + 1) * P], xh_all[:, g * GROUP + i, :], ident)
                last.then_inc(x3T_done, 1)

            def logits(g):
                pe.wait_ge(x3T_ready, g + 1)
                for i in range(GROUP):
                    last = nc.tensor.matmul(bank[g][:, i * E:(i + 1) * E], x3T[g % 2][:, i * P:(i + 1) * P], gates[:, 1, :], start=True, stop=True)
                last.then_inc(logit_done, 1)
            for g in range(2):
                rows_turn_out(g)
                logits(g)
            rows_turn_out(2)
            rows_turn_out(3)
            logits(2)
            logits(3)
            pe.wait_ge(logit_ready, NG)
            route_tensor(pe, 1)
            pe.wait_ge(pos_ready, 2)
            experts_tensor(pe, 1)


def _shape_constants():
    c = np.zeros((P, C_ALL), np.float32)
    c[:, C_IDENT:C_IDENT + P] = np.eye(P)
    c[:, C_HEAD:C_HEAD + H] = np.arange(P)[:, None] // HD == np.arange(H)[None]
    c[:, C_TIE:C_TIE + B * E] = np.tile(E - np.arange(E), B)[None]
    c[:, C_JOTA:C_JOTA + TILES * E] = np.repeat(np.arange(TILES), E)[None]
    c[:, C_RESET:C_UPPER] = np.tile(np.arange(B) > 0, E)[None]
    c[:, C_UPPER:] = np.arange(P)[:, None] < np.arange(P)[None]
    return c


def kernel(**inputs):
    import concourse.bacc as bacc
    from concourse.bass_utils import run_bass_kernel_spmd

    i = {k: np.asarray(v) for k, v in inputs.items()}
    col = lambda v: v.reshape(-1, P).T
    packed = {
        "consts": _shape_constants(),
        "negp": np.array([[-998244352.0], [-1753088.0], [-2560.0]], np.float32),
        "x": i["x"],
        "ctxT_all": i["ctx_1024"].transpose(2, 0, 1).reshape(D, B * M),
        "mask": i["mask_Bx1x1xS2_ik0"].reshape(1, B * M),
        "vecs": np.concatenate([col(i[n]) for n in (
            "L0_xattn_bq", "L0_xattn_bk", "L1_xattn_input_norm_w", "L1_xattn_slot_norm_w", "L1_xattn_gru_bih", "L1_xattn_gru_bhh")], axis=1),
        "rows": np.concatenate([i["L0_xattn_bv"], i["L0_xattn_bo"], i["L1_ffn_bg"]])[None],
        "w0": np.stack([i[f"L0_xattn_W{n}"] for n in "qkvo"], axis=1),
        "w1": np.stack([i[f"L1_xattn_W{n}"] for n in "qkv"], axis=1),
        "gru": np.stack([i["L1_xattn_gru_wih"].T, i["L1_xattn_gru_whh"].T], axis=1),
        "gates": np.stack([i["L0_ffn_centroids"].T, i["L1_ffn_Wg"]], axis=1),
    }
    def experts(up, down, b1, g, b):
        return np.concatenate([up.transpose(1, 0, 2), b1.reshape(E, FC, P).transpose(2, 0, 1), g.T[:, :, None], b.T[:, :, None],
                               down.reshape(E, FC, P, D).transpose(2, 0, 1, 3).reshape(P, E, FC * D)], axis=2)
    none = np.zeros((E, D), np.float32)
    packed |= {
        "wf0": experts(i["L0_ffn_w1"].transpose(0, 2, 1), i["L0_ffn_w2"].transpose(0, 2, 1), i["L0_ffn_b1"], i["L0_ffn_ln_g"], i["L0_ffn_ln_b"]),
        "wf1": experts(i["L1_ffn_W1"], i["L1_ffn_W2"], i["L1_ffn_b1"], none, none),
        "biases": np.stack([i["L0_ffn_b2"], i["L1_ffn_b2"]], axis=1),
    }
    nc = bacc.Bacc("TRN2", target_bir_lowering=False, num_devices=1)
    arrays, handles = {}, {}
    for name, v in packed.items():
        v = np.ascontiguousarray(v)
        arrays[f"in_{name}"] = v
        handles[name] = nc.dram_tensor(f"in_{name}", v.shape, mybir.dt.from_np(v.dtype), kind="ExternalInput").ap()
    out = nc.dram_tensor("out", (B, S, D), F32, kind="ExternalOutput").ap()
    build(nc, handles, out)
    got = run_bass_kernel_spmd(nc, [arrays], core_ids=[0])
    return got.results[0]["out"]
```
